# Optimizing a Trainium2 kernel written in Bass

```python
import numpy as np
import jax
import jax.numpy as jnp

def _softmax(x, axis=-1):
    return jax.nn.softmax(x, axis=axis)

def _gelu(x):
    return jax.nn.gelu(x, approximate=True)

def _silu(x):
    return jax.nn.silu(x)

def _sigmoid(x):
    return jax.nn.sigmoid(x)

def _layernorm(x, axis=-1, eps=1e-05):
    m = jnp.mean(x, axis=axis, keepdims=True)
    v = jnp.var(x, axis=axis, keepdims=True)
    return (x - m) / jnp.sqrt(v + eps)

def _scatter_add(tgt, idx, src, axis=0):
    return tgt.at[idx].add(src)

def _segment_sum(src, seg, n):
    return jax.ops.segment_sum(src, seg, n)
kernel_name = 'mk_vit_tower_d2_tok_img768_r4_5a770a'

def setup_inputs(seed: int=0):
    np.random.seed(seed)
    _w = jnp.asarray

    def _rec_inputs():
        import jax
        import jax.numpy as jnp
        _rk = jax.random.key(seed)
        x = -0.000356955 + 1 * jax.random.normal(jax.random.fold_in(_rk, 1), (16, 3, 96, 96), jnp.float32)
        return x
    x = _rec_inputs()

    def _L0_tok_setup():
        import jax, jax.numpy as jnp
        import numpy as np
        PATCH = 16
        EMB = 192
        key = jax.random.key(seed)
        k1, k2 = jax.random.split(key)
        x = jax.random.normal(k1, (128, 3, 224, 224), dtype=jnp.float32)
        W = jax.random.normal(k2, (EMB, PATCH * PATCH * 3), dtype=jnp.float32) * 0.02
        return {'x': x, 'W': W}
    _L0_tok_all = _L0_tok_setup()
    _L0_tok_in = {k: v for k, v in _L0_tok_all.items() if k in ('W',)}
    del _L0_tok_all

    def _L0_attn_setup():
        import jax, jax.numpy as jnp
        import numpy as np
        B, N, C = (16, 1024, 192)
        H = 12
        D = C // H
        SCALE = D ** (-0.5)
        key = jax.random.key(seed)
        k1, k2, k3, k4 = jax.random.split(key, 4)
        x = jax.random.normal(k1, (B, N, C), dtype=jnp.float32)
        w_qkv = jax.random.normal(k2, (C, 3 * C), dtype=jnp.float32) * 0.02
        w_proj = jax.random.normal(k3, (C, C), dtype=jnp.float32) * 0.02
        b_proj = jax.random.normal(k4, (C,), dtype=jnp.float32) * 0.02
        return {'x': x, 'w_qkv': w_qkv, 'w_proj': w_proj, 'b_proj': b_proj}
    _L0_attn_all = _L0_attn_setup()
    _L0_attn_in = {k: v for k, v in _L0_attn_all.items() if k in ('w_qkv', 'w_proj', 'b_proj')}
    del _L0_attn_all

    def _L0_ffn_setup():
        import jax, jax.numpy as jnp
        import numpy as np
        DIM = 192
        HID = 128
        E = 16
        G = 8
        TOPK_G = 4
        TOPK_E = 4
        SCALE = 2.5
        B, S = (2, 512)
        key = jax.random.key(seed)
        ks = jax.random.split(key, 9)
        init = lambda k, shape: jax.random.normal(k, shape, dtype=jnp.float32) * 0.02
        z = lambda shape: jnp.zeros(shape, jnp.float32)
        return {'x': jax.random.normal(ks[0], (B, S, DIM), dtype=jnp.float32), 'gate_w': init(ks[1], (DIM, E)), 'gate_b': z((E,)), 'bias': z((E,)), 'Wu': init(ks[2], (E, DIM, HID)), 'bu': z((E, HID)), 'Wg': init(ks[3], (E, DIM, HID)), 'bg': z((E, HID)), 'Wd': init(ks[4], (E, HID, DIM)), 'bd': z((E, DIM)), 'sWu': init(ks[5], (DIM, HID)), 'sbu': z((HID,)), 'sWg': init(ks[6], (DIM, HID)), 'sbg': z((HID,)), 'sWd': init(ks[7], (HID, DIM)), 'sbd': z((DIM,))}
    _L0_ffn_all = _L0_ffn_setup()
    _L0_ffn_in = {k: v for k, v in _L0_ffn_all.items() if k in ('gate_w', 'gate_b', 'bias', 'Wu', 'bu', 'Wg', 'bg', 'Wd', 'bd', 'sWu', 'sbu', 'sWg', 'sbg', 'sWd', 'sbd')}
    del _L0_ffn_all

    def _L1_attn_setup():
        import jax, jax.numpy as jnp
        import numpy as np
        import math
        B, L, D = (2, 512, 192)
        H, DK = (8, 64)
        DV = D // H
        N_POS = 32
        DFF = 2 * D
        EPS = 1e-05

        def _rel_basis(l: int, n: int) -> jnp.ndarray:
            pos = jnp.arange(l)
            distance = pos[None, :] - pos[:, None]
            pow_rate = jnp.exp(jnp.log(jnp.float32((l + 1) / 2.0)) / (n // 2))
            center_widths = pow_rate ** jnp.arange(1, n // 2 + 1, dtype=jnp.float32)
            d = distance[:, :, None].astype(jnp.float32)
            unsigned = (jnp.abs(d) <= center_widths).astype(jnp.float32)
            signed = jnp.sign(d) * unsigned
            return jnp.concatenate([unsigned, signed], axis=-1)

        def _rmsnorm(x, w):
            norm = jnp.mean(x * x, axis=-1, keepdims=True)
            return x * jax.lax.rsqrt(norm + EPS) * w
        key = jax.random.key(seed)
        ks = jax.random.split(key, 12)
        s = 0.02
        return {'x': jax.random.normal(ks[0], (B, L, D), jnp.float32), 'norm1_w': jnp.ones((D,), jnp.float32), 'norm2_w': jnp.ones((D,), jnp.float32), 'wq': jax.random.normal(ks[1], (D, H * DK), jnp.float32) * s, 'wk': jax.random.normal(ks[2], (D, H * DK), jnp.float32) * s, 'wv': jax.random.normal(ks[3], (D, H * DV), jnp.float32) * s, 'wo': jax.random.normal(ks[4], (H * DV, D), jnp.float32) * s, 'bo': jnp.zeros((D,), jnp.float32), 'u_param': jax.random.normal(ks[5], (H, DK), jnp.float32) * s, 'v_param': jax.random.normal(ks[6], (H, DK), jnp.float32) * s, 'w_pos': jax.random.normal(ks[7], (H, DK, N_POS), jnp.float32) * s, 'w1': jax.random.normal(ks[8], (D, DFF), jnp.float32) * s, 'b1': jnp.zeros((DFF,), jnp.float32), 'w2': jax.random.normal(ks[9], (DFF, D), jnp.float32) * s, 'b2': jnp.zeros((D,), jnp.float32)}
    _L1_attn_all = _L1_attn_setup()
    _L1_attn_in = {k: v for k, v in _L1_attn_all.items() if k in ('norm1_w', 'norm2_w', 'wq', 'wk', 'wv', 'wo', 'bo', 'u_param', 'v_param', 'w_pos', 'w1', 'b1', 'w2', 'b2')}
    del _L1_attn_all

    def _L1_ffn_setup():
        import jax, jax.numpy as jnp
        import numpy as np
        B, N, D, H, E, HID, TOPK = (8, 197, 192, 12, 8, 768, 2)

        def _layernorm(x, w, b, eps=1e-05):
            mu = jnp.mean(x, axis=-1, keepdims=True)
            var = jnp.mean((x - mu) ** 2, axis=-1, keepdims=True)
            return (x - mu) * jax.lax.rsqrt(var + eps) * w + b
        key = jax.random.key(seed)
        ks = jax.random.split(key, 8)
        s = 0.02
        return {'x': jax.random.normal(ks[0], (B, N, D), jnp.float32), 'norm1_w': jnp.ones((D,), jnp.float32), 'norm1_b': jnp.zeros((D,), jnp.float32), 'qkv_w': jax.random.normal(ks[1], (3 * D, D), jnp.float32) * s, 'qkv_b': jnp.zeros((3 * D,), jnp.float32), 'proj_w': jax.random.normal(ks[2], (D, D), jnp.float32) * s, 'proj_b': jnp.zeros((D,), jnp.float32), 'norm2_w': jnp.ones((D,), jnp.float32), 'norm2_b': jnp.zeros((D,), jnp.float32), 'w_gate': jax.random.normal(ks[3], (D, E), jnp.float32) * s, 'W1': jax.random.normal(ks[4], (E, D, HID), jnp.float32) * s, 'b1': jnp.zeros((E, HID), jnp.float32), 'W2': jax.random.normal(ks[5], (E, HID, D), jnp.float32) * s, 'b2': jnp.zeros((E, D), jnp.float32)}
    _L1_ffn_all = _L1_ffn_setup()
    _L1_ffn_in = {k: v for k, v in _L1_ffn_all.items() if k in ('norm1_w', 'norm1_b', 'qkv_w', 'qkv_b', 'proj_w', 'proj_b', 'norm2_w', 'norm2_b', 'w_gate', 'W1', 'b1', 'W2', 'b2')}
    del _L1_ffn_all
    return {'x': x, 'L0_tok_W': _L0_tok_in['W'], 'L0_attn_w_qkv': _L0_attn_in['w_qkv'], 'L0_attn_w_proj': _L0_attn_in['w_proj'], 'L0_attn_b_proj': _L0_attn_in['b_proj'], 'L0_ffn_gate_w': _L0_ffn_in['gate_w'], 'L0_ffn_gate_b': _L0_ffn_in['gate_b'], 'L0_ffn_bias': _L0_ffn_in['bias'], 'L0_ffn_Wu': _L0_ffn_in['Wu'], 'L0_ffn_bu': _L0_ffn_in['bu'], 'L0_ffn_Wg': _L0_ffn_in['Wg'], 'L0_ffn_bg': _L0_ffn_in['bg'], 'L0_ffn_Wd': _L0_ffn_in['Wd'], 'L0_ffn_bd': _L0_ffn_in['bd'], 'L0_ffn_sWu': _L0_ffn_in['sWu'], 'L0_ffn_sbu': _L0_ffn_in['sbu'], 'L0_ffn_sWg': _L0_ffn_in['sWg'], 'L0_ffn_sbg': _L0_ffn_in['sbg'], 'L0_ffn_sWd': _L0_ffn_in['sWd'], 'L0_ffn_sbd': _L0_ffn_in['sbd'], 'L1_attn_norm1_w': _L1_attn_in['norm1_w'], 'L1_attn_norm2_w': _L1_attn_in['norm2_w'], 'L1_attn_wq': _L1_attn_in['wq'], 'L1_attn_wk': _L1_attn_in['wk'], 'L1_attn_wv': _L1_attn_in['wv'], 'L1_attn_wo': _L1_attn_in['wo'], 'L1_attn_bo': _L1_attn_in['bo'], 'L1_attn_u_param': _L1_attn_in['u_param'], 'L1_attn_v_param': _L1_attn_in['v_param'], 'L1_attn_w_pos': _L1_attn_in['w_pos'], 'L1_attn_w1': _L1_attn_in['w1'], 'L1_attn_b1': _L1_attn_in['b1'], 'L1_attn_w2': _L1_attn_in['w2'], 'L1_attn_b2': _L1_attn_in['b2'], 'L1_ffn_norm1_w': _L1_ffn_in['norm1_w'], 'L1_ffn_norm1_b': _L1_ffn_in['norm1_b'], 'L1_ffn_qkv_w': _L1_ffn_in['qkv_w'], 'L1_ffn_qkv_b': _L1_ffn_in['qkv_b'], 'L1_ffn_proj_w': _L1_ffn_in['proj_w'], 'L1_ffn_proj_b': _L1_ffn_in['proj_b'], 'L1_ffn_norm2_w': _L1_ffn_in['norm2_w'], 'L1_ffn_norm2_b': _L1_ffn_in['norm2_b'], 'L1_ffn_w_gate': _L1_ffn_in['w_gate'], 'L1_ffn_W1': _L1_ffn_in['W1'], 'L1_ffn_b1': _L1_ffn_in['b1'], 'L1_ffn_W2': _L1_ffn_in['W2'], 'L1_ffn_b2': _L1_ffn_in['b2']}

def reference(x, L0_tok_W, L0_attn_w_qkv, L0_attn_w_proj, L0_attn_b_proj, L0_ffn_gate_w, L0_ffn_gate_b, L0_ffn_bias, L0_ffn_Wu, L0_ffn_bu, L0_ffn_Wg, L0_ffn_bg, L0_ffn_Wd, L0_ffn_bd, L0_ffn_sWu, L0_ffn_sbu, L0_ffn_sWg, L0_ffn_sbg, L0_ffn_sWd, L0_ffn_sbd, L1_attn_norm1_w, L1_attn_norm2_w, L1_attn_wq, L1_attn_wk, L1_attn_wv, L1_attn_wo, L1_attn_bo, L1_attn_u_param, L1_attn_v_param, L1_attn_w_pos, L1_attn_w1, L1_attn_b1, L1_attn_w2, L1_attn_b2, L1_ffn_norm1_w, L1_ffn_norm1_b, L1_ffn_qkv_w, L1_ffn_qkv_b, L1_ffn_proj_w, L1_ffn_proj_b, L1_ffn_norm2_w, L1_ffn_norm2_b, L1_ffn_w_gate, L1_ffn_W1, L1_ffn_b1, L1_ffn_W2, L1_ffn_b2):
    import jax
    import jax.numpy as jnp

    def _L0_tok_ref(x, W):
        import jax, jax.numpy as jnp
        import numpy as np
        PATCH = 16
        EMB = 192
        B, C, H, Wd = x.shape
        p = PATCH
        hp, wp = (H // p, Wd // p)
        num_patches = hp * wp
        xp = x.reshape(B, C, hp, p, wp, p).transpose(0, 1, 2, 4, 3, 5)
        xp = xp.reshape(B, C, num_patches, p, p).transpose(0, 2, 1, 3, 4)
        xp = xp.reshape(B, num_patches, C * p * p)
        return jnp.einsum('bnf,ef->bne', xp, W)

    def _L0_attn_ref(x, w_qkv, w_proj, b_proj):
        import jax, jax.numpy as jnp
        import numpy as np
        B, N, C = (16, 1024, 192)
        H = 12
        D = C // H
        SCALE = D ** (-0.5)
        b, n, c = x.shape
        qkv = (x @ w_qkv).reshape(b, n, 3, H, D).transpose(2, 0, 3, 1, 4)
        q, k, v = (qkv[0], qkv[1], qkv[2])
        kv = jnp.einsum('bhnd,bhne->bhde', k, v) * SCALE
        gq = jax.nn.gelu(q, approximate=False)
        gkv = jax.nn.gelu(kv, approximate=False)
        out = jnp.einsum('bhtd,bhde->bhte', gq, gkv)
        out = out.transpose(0, 2, 1, 3).reshape(b, n, c)
        return out @ w_proj + b_proj

    def _L0_ffn_ref(x, gate_w, gate_b, bias, Wu, bu, Wg, bg, Wd, bd, sWu, sbu, sWg, sbg, sWd, sbd):
        import jax, jax.numpy as jnp
        import numpy as np
        DIM = 192
        HID = 128
        E = 16
        G = 8
        TOPK_G = 4
        TOPK_E = 4
        SCALE = 2.5
        B, S = (2, 512)
        orig_shape = x.shape
        xt = x.reshape(-1, DIM)
        T = xt.shape[0]
        scores = jax.nn.softmax(xt @ gate_w + gate_b, axis=-1)
        orig_scores = jax.lax.stop_gradient(scores)
        s = scores + bias[None, :]
        s3 = s.reshape(T, G, E // G)
        group_scores = jax.lax.top_k(s3, 2)[0].sum(-1)
        gidx = jax.lax.top_k(group_scores, TOPK_G)[1]
        gmask = jnp.any(jnp.arange(G)[None, None, :] == gidx[:, :, None], axis=1)
        s_masked = jnp.where(gmask[:, :, None], s3, -jnp.inf).reshape(T, E)
        _, idx = jax.lax.top_k(s_masked, TOPK_E)
        w = jnp.take_along_axis(orig_scores, idx, axis=1) * SCALE
        w_full = jnp.zeros((T, E), xt.dtype).at[jnp.arange(T)[:, None], idx].add(w)
        up = jax.nn.silu(jnp.einsum('td,edh->teh', xt, Wu) + bu)
        gt = jnp.einsum('td,edh->teh', xt, Wg) + bg
        act = up * gt * w_full[:, :, None]
        y = jnp.einsum('teh,ehd->td', act, Wd) + w_full @ bd
        sh = jax.nn.silu(xt @ sWu + sbu) * (xt @ sWg + sbg)
        y = y + sh @ sWd + sbd
        return y.reshape(orig_shape)

    def _L1_attn_ref(x, norm1_w, norm2_w, wq, wk, wv, wo, bo, u_param, v_param, w_pos, w1, b1, w2, b2):
        import jax, jax.numpy as jnp
        import numpy as np
        import math
        B, L, D = (2, 512, 192)
        H, DK = (8, 64)
        DV = D // H
        N_POS = 32
        DFF = 2 * D
        EPS = 1e-05

        def _rel_basis(l: int, n: int) -> jnp.ndarray:
            pos = jnp.arange(l)
            distance = pos[None, :] - pos[:, None]
            pow_rate = jnp.exp(jnp.log(jnp.float32((l + 1) / 2.0)) / (n // 2))
            center_widths = pow_rate ** jnp.arange(1, n // 2 + 1, dtype=jnp.float32)
            d = distance[:, :, None].astype(jnp.float32)
            unsigned = (jnp.abs(d) <= center_widths).astype(jnp.float32)
            signed = jnp.sign(d) * unsigned
            return jnp.concatenate([unsigned, signed], axis=-1)

        def _rmsnorm(x, w):
            norm = jnp.mean(x * x, axis=-1, keepdims=True)
            return x * jax.lax.rsqrt(norm + EPS) * w
        b, l, _ = x.shape
        skip = x
        h1 = _rmsnorm(x, norm1_w)
        q = (h1 @ wq).reshape(b, l, H, DK)
        k = (h1 @ wk).reshape(b, l, H, DK)
        v = (h1 @ wv).reshape(b, l, H, DV)
        basis = _rel_basis(l, N_POS)
        scale = 1.0 / math.sqrt(DK)
        qw = jnp.einsum('bihd,hdn->bihn', q, w_pos)
        qr = jnp.einsum('bihn,ijn->bhij', qw, basis)
        uk = jnp.einsum('hd,bjhd->bhj', u_param, k)[:, :, None, :]
        vw = jnp.einsum('hd,hdn->hn', v_param, w_pos)
        vr = jnp.einsum('hn,ijn->hij', vw, basis)[None]
        bias = (qr + uk + vr) * scale
        scores = jnp.einsum('bihd,bjhd->bhij', q, k) * scale + bias
        attn = jax.nn.softmax(scores, axis=-1)
        out = jnp.einsum('bhij,bjhd->bihd', attn, v)
        out = out.reshape(b, l, H * DV) @ wo + bo
        x = out + skip
        skip = x
        h2 = _rmsnorm(x, norm2_w)
        h2 = jax.nn.gelu(h2 @ w1 + b1, approximate=False) @ w2 + b2
        return h2 + skip

    def _L1_ffn_ref(x, norm1_w, norm1_b, qkv_w, qkv_b, proj_w, proj_b, norm2_w, norm2_b, w_gate, W1, b1, W2, b2):
        import jax, jax.numpy as jnp
        import numpy as np
        B, N, D, H, E, HID, TOPK = (8, 197, 192, 12, 8, 768, 2)

        def _layernorm(x, w, b, eps=1e-05):
            mu = jnp.mean(x, axis=-1, keepdims=True)
            var = jnp.mean((x - mu) ** 2, axis=-1, keepdims=True)
            return (x - mu) * jax.lax.rsqrt(var + eps) * w + b
        Bx, Nx, C = x.shape
        hd = C // H
        scale = hd ** (-0.5)
        xn = _layernorm(x, norm1_w, norm1_b)
        qkv = (xn @ qkv_w.T + qkv_b).reshape(Bx, Nx, 3, H, hd).transpose(2, 0, 3, 1, 4)
        q, k, v = (qkv[0], qkv[1], qkv[2])
        attn = jax.nn.softmax(jnp.einsum('bhqd,bhkd->bhqk', q, k) * scale, axis=-1)
        o = jnp.einsum('bhqk,bhkd->bqhd', attn, v).reshape(Bx, Nx, C)
        x = x + (o @ proj_w.T + proj_b)
        xn2 = _layernorm(x, norm2_w, norm2_b).reshape(-1, C)
        T = xn2.shape[0]
        logits = xn2 @ w_gate
        top_vals, top_idx = jax.lax.top_k(logits, TOPK)
        gates = jax.nn.softmax(top_vals, axis=-1)
        gates_full = jnp.zeros((T, E), xn2.dtype).at[jnp.arange(T)[:, None], top_idx].add(gates)

        def body(acc, p):
            w1, bb1, w2, bb2, g = p
            h = jax.nn.gelu(xn2 @ w1 + bb1, approximate=False)
            return (acc + g[:, None] * (h @ w2 + bb2), None)
        moe_out, _ = jax.lax.scan(body, jnp.zeros_like(xn2), (W1, b1, W2, b2, gates_full.T))
        return x + moe_out.reshape(Bx, Nx, C)
    h = _L0_tok_ref(x, L0_tok_W)
    h = h + _L0_attn_ref(_layernorm(h, axis=-1), L0_attn_w_qkv, L0_attn_w_proj, L0_attn_b_proj)
    h = h + _L0_ffn_ref(_layernorm(h, axis=-1), L0_ffn_gate_w, L0_ffn_gate_b, L0_ffn_bias, L0_ffn_Wu, L0_ffn_bu, L0_ffn_Wg, L0_ffn_bg, L0_ffn_Wd, L0_ffn_bd, L0_ffn_sWu, L0_ffn_sbu, L0_ffn_sWg, L0_ffn_sbg, L0_ffn_sWd, L0_ffn_sbd)
    h = h + _L1_attn_ref(_layernorm(h, axis=-1), L1_attn_norm1_w, L1_attn_norm2_w, L1_attn_wq, L1_attn_wk, L1_attn_wv, L1_attn_wo, L1_attn_bo, L1_attn_u_param, L1_attn_v_param, L1_attn_w_pos, L1_attn_w1, L1_attn_b1, L1_attn_w2, L1_attn_b2)
    h = h + _L1_ffn_ref(_layernorm(h, axis=-1), L1_ffn_norm1_w, L1_ffn_norm1_b, L1_ffn_qkv_w, L1_ffn_qkv_b, L1_ffn_proj_w, L1_ffn_proj_b, L1_ffn_norm2_w, L1_ffn_norm2_b, L1_ffn_w_gate, L1_ffn_W1, L1_ffn_b1, L1_ffn_W2, L1_ffn_b2)
    return h

_drawn_inputs = setup_inputs


def setup_inputs(seed=0):
    import zlib

    import numpy as np

    out = dict(_drawn_inputs(seed))
    spreads = {'L0_ffn_gate_b': (0.0, 0.31),
     'L0_ffn_bias': (0.0, 0.1),
     'L0_ffn_bu': (0.0, 0.8),
     'L0_ffn_bg': (0.0, 0.8),
     'L0_ffn_bd': (0.0, 0.287),
     'L0_ffn_sbu': (0.0, 0.8),
     'L0_ffn_sbg': (0.0, 0.8),
     'L0_ffn_sbd': (0.0, 0.1),
     'L1_attn_norm1_w': (1.0, 0.6),
     'L1_attn_norm2_w': (1.0, 0.6),
     'L1_attn_bo': (0.0, 0.336),
     'L1_attn_b1': (0.0, 0.513),
     'L1_attn_b2': (0.0, 0.3),
     'L1_ffn_norm1_w': (1.0, 0.6),
     'L1_ffn_norm1_b': (0.0, 0.8),
     'L1_ffn_qkv_b': (0.0, 0.63),
     'L1_ffn_proj_b': (0.0, 0.46),
     'L1_ffn_norm2_w': (1.0, 0.6),
     'L1_ffn_norm2_b': (0.0, 0.72),
     'L1_ffn_b1': (0.0, 0.8),
     'L1_ffn_b2': (0.0, 0.289)}
    factors = {'L0_attn_w_qkv': 2.893,
     'L0_attn_w_proj': 2.858,
     'L0_ffn_Wu': 8.0,
     'L0_ffn_Wg': 8.0,
     'L0_ffn_Wd': 8.0,
     'L0_ffn_sWu': 3.314,
     'L0_ffn_sWg': 3.264,
     'L0_ffn_sWd': 3.095,
     'L1_attn_wq': 8.0,
     'L1_attn_wk': 8.0,
     'L1_attn_wv': 4.32,
     'L1_attn_wo': 4.038,
     'L1_attn_u_param': 8.0,
     'L1_attn_v_param': 38.26,
     'L1_attn_w_pos': 8.0,
     'L1_ffn_qkv_w': 5.811,
     'L1_ffn_proj_w': 3.575,
     'L1_ffn_W1': 2.95}
    for name, (base, spread) in spreads.items():
        noise = np.random.default_rng([zlib.crc32(name.encode()), seed]).standard_normal(out[name].shape)
        drawn = base * np.exp(spread * noise) if base else spread * noise
        out[name] = jnp.asarray(drawn.astype(out[name].dtype))
    for name, factor in factors.items():
        out[name] = (out[name] * factor).astype(out[name].dtype)
    return out
```

```python
from contextlib import ExitStack

import numpy as np

import concourse.bass as bass
from concourse import mybir

F32 = mybir.dt.float32
ALU = mybir.AluOpType
ACT = mybir.ActivationFunctionType
AX = mybir.AxisListType

IMAGES = 16
TOK = 36
D = 192
C = 96
SLOT = 64
PAIRS = IMAGES // 2
HP = PAIRS // 2
HI = IMAGES // 2
HT = HI * TOK
T = IMAGES * TOK
PATCH_CHUNKS = 768 // 128
EPS = 1e-5

H0 = 12
HB, HD = 8, 64
HBV = D // HB
HF, HFD = 12, 16
REL = 2 * TOK - 1
NPOS = 32
HID1 = 384

E0, G0, HID0 = 16, 8, 128
E1, HID1M = 8, 768
M1 = HID1M // 128
NB0, NB1 = 4, 2
AHEAD = 4
BIG = 1.0e30

COL96 = {n: (2 * i, 2) for i, n in enumerate(
    ["sbd", "rms1_w", "rms2_w", "ln1_w", "ln1_b", "ln2_w", "ln2_b", "q_b", "k_b"])}
N96 = 2 * len(COL96)
COL128 = {"u": (0, 4), "v": (4, 4), "b1": (8, 3)}
N128 = 11


def psum_uses():
    keys = []
    halves = range(2)
    pairs = lambda hf: range(HP * hf, HP * hf + HP)

    def norm(tag, hf):
        keys.extend((tag, hf, c) for c in range(2))

    keys.extend(("tok", p) for p in range(PAIRS))
    for hf in halves:
        norm("n0", hf)
    for hf in halves:
        keys.extend(("q0", hf, c) for c in range(2))
        keys.extend(("kv0", p) for p in pairs(hf))
    for hf in halves:
        keys.extend(("kTv", hf, pp, par) for pp in range(2) for par in range(2))
        keys.extend(("o0", hf, c) for c in range(2))
    keys.extend(("proj0", p) for p in range(PAIRS))
    for hf in halves:
        norm("n1", hf)
    keys.extend(("gate0", hf) for hf in halves)
    used, uses, at = [0] * 8, {}, 0

    def place(keys, at):
        for k in keys:
            b = at % 8
            assert k not in uses
            uses[k] = (b, used[b])
            used[b] += 1
            at += 1
        return at

    place(keys, at)
    for hf in halves:
        uses["wT0", hf] = (2 * hf, used[2 * hf])
        used[2 * hf] += 1
    for hf in halves:
        uses["u", hf] = (4 + 2 * hf, used[4 + 2 * hf])
        uses["g", hf] = (5 + 2 * hf, used[5 + 2 * hf])
        for c in range(2):
            uses["y0", hf, c] = (2 * hf + c, used[2 * hf + c])
    for b in range(4):
        used[b] += 1
        used[4 + b] += E0 + 1
    keys = [("y0t", p) for p in range(PAIRS)]
    for hf in halves:
        keys += [("n2", hf, c) for c in range(2)]
    keys += [("rel_w", m) for m in range(4)]
    for hf in halves:
        keys += [("q1", hf, m) for m in range(4)]
        keys += [("rel", p, s) for p in pairs(hf) for s in range(2)]
        keys += [("k1", hf, m) for m in range(4)]
        keys += [("v1", hf, q) for q in range(2)]
    keys += [("s1", p) for p in range(AHEAD)]
    for p in range(PAIRS):
        keys += [("p1t", p)] + [("s1", p + AHEAD)] * (p + AHEAD < PAIRS) + [("av1", p)]
    for hf in halves:
        keys += [("o1t", hf, c) for c in range(2)]
    keys += [("wo1", p) for p in range(PAIRS)]
    for hf in halves:
        keys += [("n3", hf, c) for c in range(2)]
    for hf in halves:
        keys += [("f1", hf, m) for m in range(3)]
        keys += [("f2", p) for p in pairs(hf)]
    for hf in halves:
        keys += [("n4", hf, c) for c in range(2)]
    for hf in halves:
        keys += [("q2", hf, c) for c in range(2)]
        keys += [("k2", hf, c) for c in range(2)]
        keys += [("v2", hf, q) for q in range(2)]
    keys += [("s2", p) for p in range(AHEAD)]
    for p in range(PAIRS):
        keys += [("p2t", p, 0), ("p2t", p, 1)]
        keys += [("s2", p + AHEAD)] * (p + AHEAD < PAIRS) + [("av2", p)]
    for hf in halves:
        keys += [("o2t", hf, c) for c in range(2)]
    keys += [("wo2", p) for p in range(PAIRS)]
    for hf in halves:
        keys += [("n5", hf, c) for c in range(2)]
    keys += [("gate1", hf) for hf in halves]
    keys += [("wT1", hf) for hf in halves]
    place(keys, 0)
    for b in range(4):
        uses["hid", b] = (4 + b, used[4 + b])
        uses["y1", b // 2, b % 2] = (b, used[b])
    for b in range(4):
        used[b] += 1
        used[4 + b] += E1 * 2 * M1 // 4
    place([("y1t", p) for p in range(PAIRS)], 0)
    return uses


def build_tower(nc, a, out):
    uses = psum_uses()
    ctx = ExitStack()
    with ctx:
        def sb(name, shape):
            return ctx.enter_context(nc.sbuf_tensor(name, shape, F32))

        semaphores = {}

        def sem(name):
            if name not in semaphores:
                semaphores[name] = ctx.enter_context(nc.semaphore(name))
            return semaphores[name]

        def dram(name, shape):
            return nc.dram_tensor(name, shape, F32, kind="Internal").ap()

        bank = [ctx.enter_context(nc.psum_tensor(f"bank{b}", [128, 512], F32)) for b in range(8)]
        bank_full = [sem(f"bank_full{b}") for b in range(8)]
        bank_free = [sem(f"bank_free{b}") for b in range(8)]

        rel_d = dram("rel_by_distance", [PAIRS, 128, HB * REL])
        w0_d = dram("expert_weights0", [E0, T])
        w1_d = dram("expert_weights1", [E1, T])

        h = sb("h", [128, PAIRS, D])
        xn = sb("xn", [128, PAIRS, D])
        u = sb("u", [128, PAIRS, D])
        stats = sb("stats", [128, PAIRS, 6])
        mv = sb("mv", [128, PAIRS, 2])
        pw_in = sb("pw_in", [128, 2, PAIRS])
        pw_out = sb("pw_out", [128, 2, PAIRS])
        minus_half = sb("minus_half", [128, 2, PAIRS])
        row_max = sb("row_max", [128, PAIRS, HF])
        row_sum = sb("row_sum", [128, PAIRS, HF])
        row_inv = sb("row_inv", [128, PAIRS, HF])

        xT = sb("xT", [97, 2, IMAGES * SLOT])
        oT = sb("oT", [97, 2, IMAGES * SLOT])

        ident = sb("ident", [128, 128])
        mask_pair = sb("mask_pair", [128, 2])
        mask_head = sb("mask_head", [C, 6])
        tri = sb("tri", [128, G0 * G0 + E0 * E0])
        basis = sb("basis", [NPOS, REL])
        c96 = sb("c96", [C, N96])
        c128 = sb("c128", [128, N128])
        b2_row = sb("b2_row", [128, D])
        route_bias = sb("route_bias", [128, E0])
        wproj0 = sb("wproj0", [97, 2, D])
        gate0w = sb("gate0w", [97, 2, E0])
        bd0 = sb("bd0", [E0, D])
        wq1 = sb("wq1", [C, 2, HB * HD])
        wk1 = sb("wk1", [C, 2, HB * HD])
        wv1 = sb("wv1", [C, 2, D])
        wout1 = sb("wout1", [97, 2, D])
        wposT = sb("wposT", [NPOS, HB * HD])
        w1a = sb("w1a", [C, 2, HID1])
        w2a = sb("w2a", [128, 3, D])
        wqk2 = sb("wqk2", [C, 2, 2 * D])
        wv2 = sb("wv2", [97, 2, D])
        wout2 = sb("wout2", [97, 2, D])
        gate1w = sb("gate1w", [C, 2, E1])
        b2m = sb("b2m", [E1, D])
        wT = sb("wT", [E0, T])

        arena = sb("arena", [128, 25624])

        def part(lo, n):
            return arena[:, lo:lo + n]

        QU, QV, KB, RS, VB, PP, PT = 0, 4096, 8192, 15640, 17944, 21016, 24088
        qu = part(QU, 4096).rearrange("p (m t) -> p m t", m=4)
        qv = part(QV, 4096).rearrange("p (m t) -> p m t", m=4)
        kbd1 = part(KB, 4608).rearrange("p (m i e j) -> p m i e j", m=4, i=IMAGES, e=2)
        rbd = part(KB + 4608, 568).rearrange("p (m e r) -> p m e r", m=4, e=2)
        relb = part(KB + 5176, HP * HB * REL).rearrange("p (q n) -> p q n", q=HP)
        rels = part(RS, PAIRS * HB * TOK).rearrange("p (q h j) -> p q h j", q=PAIRS, h=HB)
        vbd1 = part(VB, IMAGES * D).rearrange("p (n e d) -> p n e d", e=2, d=HBV)
        probs1 = part(PP, AHEAD * HB * SLOT).rearrange("p (r h j) -> p r h j", r=AHEAD, h=HB)
        pt1 = part(PT, 2 * 512).rearrange("p (r n) -> p r n", r=2)
        g1 = qu[:, 0:3, :]
        q2 = qv[0:C, 0:2, :]
        kbd2 = part(KB, 6912)[0:C, :].rearrange("p (c i e j) -> p c i e j", c=2, i=IMAGES, e=6)
        k2 = part(RS, 2 * T)[0:C, :].rearrange("p (c t) -> p c t", c=2)
        vbd2 = part(VB, IMAGES * D).rearrange("p (n e d) -> p n e d", e=2, d=HFD)
        probs2 = part(PP, AHEAD * HF * SLOT).rearrange("p (r h j) -> p r h j", r=AHEAD, h=HF)
        pt2 = part(PT, 2 * 768).rearrange("p (r n) -> p r n", r=2)
        xp = part(0, 6144).rearrange("p (q k t) -> p q k t", q=PAIRS, k=PATCH_CHUNKS)
        tokw = part(6144, 1152).rearrange("p (k n) -> p k n", k=PATCH_CHUNKS)
        kv = part(7296, 3072).rearrange("p (q n) -> p q n", q=PAIRS)
        gq = part(10368, 1152)[0:C, :].rearrange("p (c t) -> p c t", c=2)
        gkr = part(11520, 3072)[0:C, :].rearrange("p (i c e) -> p i c e", i=IMAGES, c=2)
        gkv = part(14592, 3072)[0:C, :].rearrange("p (i c e) -> p i c e", i=IMAGES, c=2)
        wqkv0 = part(17664, 1152)[0:C, :].rearrange("p (c n) -> p c n", c=2)
        rt = {}
        at = KB
        for name, n in (("e", 64), ("score", 64), ("s", 64), ("gs", 32), ("gm", 32), ("rank", 64),
                        ("sel", 64), ("w", 128), ("mx", 4), ("sum", 4), ("inv", 4), ("pen", 32)):
            rt[name] = part(at, n)
            at += n
        rt_gt = part(at, 1024)
        rt_eq = part(at + 1024, 1024)

        moe = sb("moe", [128, 8844])

        def moe_part(lo, n):
            return moe[:, lo:lo + n]

        up0 = [moe_part(706 * b, 512)[0:C, :].rearrange("p (c n) -> p c n", c=2) for b in range(NB0)]
        down0 = [moe_part(706 * b + 512, 194) for b in range(NB0)]
        wb0 = [moe_part(706 * NB0 + T * b, T) for b in range(NB0)]
        at = (706 + T) * NB0
        s0, a0, f0 = ([moe_part(at + (3 * hf + i) * HT, HT) for hf in range(2)] for i in range(3))
        up1 = [moe_part(2694 * b, 1536)[0:C, :].rearrange("p (c n) -> p c n", c=2) for b in range(NB1)]
        down1 = [moe_part(2694 * b + 1536, 1158) for b in range(NB1)]
        wb1 = [moe_part(2694 * NB1 + T * b, T) for b in range(NB1)]
        at = (2694 + T) * NB1
        hg, hs = ([moe_part(at + (4 * i + r) * HT, HT) for r in range(4)] for i in range(2))

        turns = 2 * M1 // 4

        def col96(name, c):
            return c96[:, COL96[name][0] + c:COL96[name][0] + c + 1]

        def col128(name, m):
            return c128[:, COL128[name][0] + m:COL128[name][0] + m + 1]

        def real(t, c, hf):
            rows = min(t.shape[0], 128) if t.shape[0] != 97 else C
            return t[0:rows, c, hf * HI * SLOT:(hf + 1) * HI * SLOT]\
                .rearrange("p (i t) -> p i t", t=SLOT)[:, :, 0:TOK]

        def by_image(x):
            return x.rearrange("p (i t) -> p i t", t=TOK)

        def half(hf):
            return slice(hf * HT, (hf + 1) * HT)

        def pad_half(hf):
            return slice(hf * HI * SLOT, (hf + 1) * HI * SLOT)

        def pairs(hf):
            return range(HP * hf, HP * hf + HP)

        def pair_cols(p):
            return slice(2 * SLOT * p, 2 * SLOT * (p + 1))

        def fill(pe, key):
            b, n = uses[key]
            if n:
                pe.wait_ge(bank_free[b], n)
            return bank[b]

        def full(ins, key):
            ins.then_inc(bank_full[uses[key][0]], 1)

        def read(eng, key):
            b, n = uses[key]
            eng.wait_ge(bank_full[b], n + 1)
            return bank[b]

        def free(ins, key):
            ins.then_inc(bank_free[uses[key][0]], 1)

        def await_read_out(eng, key):
            b, n = uses[key]
            eng.wait_ge(bank_free[b], n + 1)

        block = ctx.enter_context(nc.Block())

        @block.sync
        def _(sp):
            for q in range(4):
                sp.dma_start(xp[:, 2 * q:2 * q + 2], a["patches"][2 * q:2 * q + 2].rearrange("q p k t -> p q k t"))\
                  .then_inc(sem(f"patches{q}_loaded"), 16)
                if q == 0:
                    sp.dma_start(tokw, a["tok_w"]).then_inc(sem("tok_w_loaded"), 16)
            for dst, name in ((ident[:, :], "ident"), (c96[:, :], "c96"), (mask_head[:, :], "mask_head"),
                              (wqkv0, "wqkv0"), (wproj0[:, :, :], "wproj0")):
                sp.dma_start(dst, a[name]).then_inc(sem("set0_loaded"), 16)
            for dst, name in ((gate0w[:, :, :], "gate0w"), (tri[:, :], "tri"), (route_bias[:, :], "route_bias"),
                              (bd0[:, :], "bd0")):
                sp.dma_start(dst, a[name]).then_inc(sem("set1_loaded"), 16)
            for x in range(NB0):
                sp.dma_start(up0[x], a["up0"][x]).then_inc(sem(f"expert0_loaded{x}"), 16)
                sp.dma_start(down0[x], a["down0"][x]).then_inc(sem(f"expert0_loaded{x}"), 16)
            for dst, name in ((mask_pair[:, :], "mask_pair"), (basis[:, :], "basis"), (c128[:, :], "c128"),
                              (b2_row[:, :], "b2_row"), (wq1[:, :, :], "wq1"), (wk1[:, :, :], "wk1"),
                              (wv1[:, :, :], "wv1"), (wout1[:, :, :], "wout1"), (wposT[:, :], "wposT"),
                              (w1a[:, :, :], "w1a"), (w2a[:, :, :], "w2a")):
                sp.dma_start(dst, a[name]).then_inc(sem("set2_loaded"), 16)
            for dst, name in ((wqk2[:, :, :], "wqk2"), (wv2[:, :, :], "wv2"), (wout2[:, :, :], "wout2"),
                              (gate1w[:, :, :], "gate1w"), (b2m[:, :], "b2m")):
                sp.dma_start(dst, a[name]).then_inc(sem("set3_loaded"), 16)

            for hf in range(2):
                await_read_out(sp, ("wT0", hf))
            sp.dma_start(w0_d, wT[:, :]).then_inc(sem("w0_stored"), 16)
            sp.wait_ge(sem("w0_stored"), 16)
            for x in range(1, NB0):
                sp.dma_start(wb0[x], w0_d[x - 1].partition_broadcast(128)).then_inc(sem(f"w0_loaded{x}"), 16)

            def reload0(it, b):
                sp.wait_ge(sem("expert0_done"), it * NB0 + (b + 1))
                sp.dma_start(up0[b], a["up0"][it * NB0 + (NB0 + b)]).then_inc(sem(f"expert0_loaded{b}"), 16)
                sp.dma_start(down0[b], a["down0"][it * NB0 + (NB0 + b)]).then_inc(sem(f"expert0_loaded{b}"), 16)
                sp.dma_start(wb0[b], w0_d[it * NB0 + (NB0 + b - 1)].partition_broadcast(128))\
                  .then_inc(sem(f"w0_loaded{b}"), 16)

            with sp.Fori(0, E0 // NB0 - 1) as it:
                for b in range(NB0):
                    reload0(it, b)
            reload0(E0 // NB0 - 1, 0)

            sp.wait_ge(sem("expert0_done"), E0 + 1)
            for b in range(NB1):
                sp.dma_start(up1[b], a["up1"][b]).then_inc(sem(f"expert1_loaded{b}"), 16)
                sp.dma_start(down1[b], a["down1"][b]).then_inc(sem(f"expert1_loaded{b}"), 16)

            for hf in range(2):
                for p in pairs(hf):
                    for s in range(2):
                        await_read_out(sp, ("rel", p, s))
                sp.dma_start(rel_d[HP * hf:HP * hf + HP].rearrange("q p n -> p q n"), relb)\
                  .then_inc(sem("rel_stored"), 16)
                sp.wait_ge(sem("rel_stored"), 16 * (hf + 1))
                for par in range(2):
                    row = HB * REL
                    for p in pairs(hf):
                        at = (p * 128 + par * SLOT) * row + TOK - 1
                        skewed = bass.AP(tensor=rel_d.tensor, offset=at,
                                         ap=[[row - 1, TOK], [REL, HB], [1, TOK]])
                        sp.dma_start(rels[par * SLOT:par * SLOT + TOK, p], skewed)\
                          .then_inc(sem(f"rel_loaded{hf}"), 16)

            for hf in range(2):
                await_read_out(sp, ("wT1", hf))
            sp.dma_start(w1_d, wT[0:E1, :]).then_inc(sem("w1_stored"), 16)
            sp.wait_ge(sem("w1_stored"), 16)
            for b in range(NB1):
                sp.dma_start(wb1[b], w1_d[b].partition_broadcast(128)).then_inc(sem(f"w1_loaded{b}"), 16)
            with sp.Fori(0, E1 // NB1 - 1) as it:
                for b in range(NB1):
                    sp.wait_ge(sem("expert1_done"), it * NB1 + b + 1)
                    sp.dma_start(up1[b], a["up1"][it * NB1 + NB1 + b]).then_inc(sem(f"expert1_loaded{b}"), 16)
                    sp.dma_start(down1[b], a["down1"][it * NB1 + NB1 + b])\
                      .then_inc(sem(f"expert1_loaded{b}"), 16)
                    sp.dma_start(wb1[b], w1_d[it * NB1 + NB1 + b].partition_broadcast(128))\
                      .then_inc(sem(f"w1_loaded{b}"), 16)
            for p in range(PAIRS):
                sp.wait_ge(sem("result_ready"), p + 1)
                for par in range(2):
                    sp.dma_start(out[2 * p + par], h[par * SLOT:par * SLOT + TOK, p, :])\
                      .then_inc(sem("result_stored"), 16)
            sp.wait_ge(sem("result_stored"), 16 * 2 * PAIRS)

        @block.gpsimd
        def _(pool):
            step = [0]

            def link(ins):
                step[0] += 1
                ins.then_inc(sem("pool_step"), 1)
                pool.wait_ge(sem("pool_step"), step[0])

            link(nc.gpsimd.memset(minus_half[:, :, :], -0.5))
            link(nc.gpsimd.memset(xT[C:C + 1, :, :], 1.0))
            link(nc.gpsimd.memset(oT[C:C + 1, :, :], 1.0))
            nc.gpsimd.memset(oT[0:C, :, :], 0.0).then_inc(sem("pool_init"), 1)
            pool.wait_ge(sem("pool_init"), 1)

            def rstd(n, hf, kind):
                sl = slice(HP * hf, HP * hf + HP)
                mean, var = mv[:, sl, 0], mv[:, sl, 1]
                pool.wait_ge(sem("stats_done"), 2 * n + hf + 1)
                if kind == "rms":
                    link(nc.gpsimd.tensor_tensor(pw_in[:, 0, sl], mean, mean, ALU.mult))
                    link(nc.gpsimd.tensor_tensor(pw_in[:, 0, sl], pw_in[:, 0, sl], var, ALU.add))
                    link(nc.gpsimd.tensor_scalar(pw_in[:, 0, sl], pw_in[:, 0, sl], EPS, None, ALU.add))
                else:
                    link(nc.gpsimd.tensor_scalar(pw_in[:, 0, sl], var, EPS, None, ALU.add))
                k = 1
                if kind == "ln+norm":
                    link(nc.gpsimd.tensor_scalar(pw_in[:, 1, sl], var, 1.0 + EPS, EPS * EPS, ALU.mult, ALU.add))
                    k = 2
                nc.gpsimd.tensor_tensor(pw_out[:, 0:k, sl], pw_in[:, 0:k, sl], minus_half[:, 0:k, sl], ALU.pow)\
                    .then_inc(sem("rstd_done"), 1)

            for hf in range(2):
                rstd(0, hf, "ln")
            pool.wait_ge(sem("set0_loaded"), 16 * 5)
            for hf in range(2):
                for pp in range(2):
                    for par in range(2):
                        await_read_out(pool, ("kTv", hf, pp, par))
                blocks = gkr[:, HI * hf:HI * hf + HI].rearrange("p i c (h e) -> p (i c) h e", e=HFD)
                kept = gkv[:, HI * hf:HI * hf + HI].rearrange("p i c (h e) -> p (i c) h e", e=HFD)
                mask = mask_head[:, :].unsqueeze(1).unsqueeze(3).broadcast_to([C, 2 * HI, 6, HFD])
                nc.gpsimd.tensor_tensor(kept, blocks, mask, ALU.mult).then_inc(sem("kv_masked"), 1)
            for hf in range(2):
                rstd(1, hf, "ln")
            for p in range(PAIRS):
                await_read_out(pool, ("proj0", p))
            nc.gpsimd.memset(part(QU, 8192), 0.0)
            nc.gpsimd.memset(part(RS, PAIRS * HB * TOK), 0.0)
            nc.gpsimd.memset(part(PP, AHEAD * HF * SLOT), 0.0).then_inc(sem("pads_zeroed"), 1)
            for hf in range(2):
                rstd(2, hf, "ln+norm")
            for hf in range(2):
                rstd(3, hf, "rms")
            pool.wait_ge(sem("set2_loaded"), 16 * 11)
            link(nc.gpsimd.tensor_tensor(h[:, :, :], h[:, :, :], u[:, :, :], ALU.add))
            nc.gpsimd.tensor_tensor(h[:, :, :], h[:, :, :],
                                    b2_row[:, :].unsqueeze(1).broadcast_to([128, PAIRS, D]), ALU.add)\
                .then_inc(sem("skip1_added"), 1)
            for hf in range(2):
                rstd(4, hf, "ln+norm")
            for hf in range(2):
                await_read_out(pool, ("k2", hf, 0))
                imgs = slice(HI * hf, HI * hf + HI)
                nc.gpsimd.tensor_tensor(
                    kbd2[:, 0, imgs], by_image(k2[:, 0, half(hf)]).unsqueeze(2).broadcast_to([C, HI, 6, TOK]),
                    mask_head[:, :].unsqueeze(1).unsqueeze(3).broadcast_to([C, HI, 6, TOK]), ALU.mult)\
                    .then_inc(sem("keys2_masked_pool"), 1)
            for hf in range(2):
                rstd(5, hf, "ln")
            nc.gpsimd.tensor_tensor(h[:, :, :], h[:, :, :], u[:, :, :], ALU.add).then_inc(sem("skip2_added"), 1)

        @block.tensor
        def _(pe):
            mm = nc.tensor.matmul

            def transposes(n, hf):
                pe.wait_ge(sem("xn_done"), 2 * n + hf + 1)
                for c in range(2):
                    b = fill(pe, (f"n{n}", hf, c))
                    for q, p in enumerate(pairs(hf)):
                        last = nc.tensor.transpose(b[0:C, q * 128:(q + 1) * 128], xn[:, p, c * C:(c + 1) * C],
                                                   ident[:, :])
                    full(last, (f"n{n}", hf, c))

            def await_xT(n, hf):
                for c in range(2):
                    await_read_out(pe, (f"n{n}", hf, c))

            def feature_major(key, w, c0, width, src, hf):
                b = fill(pe, key)
                o = by_image(b[0:width, 0:HT])
                for kc in range(2):
                    last = mm(o, w[0:C, kc, c0:c0 + width], real(src, kc, hf), start=kc == 0, stop=kc == 1)
                full(last, key)

            def token_major(key, src, w, p, biased):
                b = fill(pe, key)
                n = w.shape[2]
                for kc in range(2):
                    rows = C + (1 if kc and biased else 0)
                    last = mm(b[:, 0:n], src[0:rows, kc, pair_cols(p)], w[0:rows, kc, :],
                              start=kc == 0, stop=kc == 1)
                full(last, key)

            pe.wait_ge(sem("tok_w_loaded"), 16)
            for p in range(PAIRS):
                pe.wait_ge(sem(f"patches{p // 2}_loaded"), 16)
                b = fill(pe, ("tok", p))
                for k in range(PATCH_CHUNKS):
                    last = mm(b[:, 0:D], xp[:, p, k, :], tokw[:, k, :], start=k == 0, stop=k == PATCH_CHUNKS - 1)
                full(last, ("tok", p))
            pe.wait_ge(sem("set0_loaded"), 16 * 5)
            pe.wait_ge(sem("pool_init"), 1)

            for hf in range(2):
                transposes(0, hf)
            for hf in range(2):
                await_xT(0, hf)
                for c in range(2):
                    feature_major(("q0", hf, c), wqkv0, c * C, C, xT, hf)
                for p in pairs(hf):
                    token_major(("kv0", p), xT, wqkv0[:, :, D:3 * D], p, False)
            for hf in range(2):
                for p in pairs(hf):
                    await_read_out(pe, ("kv0", p))
                for pp in range(2):
                    for par in range(2):
                        key = ("kTv", hf, pp, par)
                        b = fill(pe, key)
                        rows = slice(par * SLOT, par * SLOT + TOK)
                        for q in range(2):
                            for c in range(2):
                                p = HP * hf + 2 * pp + q
                                at = (2 * q + c) * C
                                last = mm(b[0:C, at:at + C], kv[rows, p, c * C:(c + 1) * C],
                                          kv[rows, p, D + c * C:D + (c + 1) * C], start=True, stop=True)
                        full(last, key)
                pe.wait_ge(sem("kv_masked"), hf + 1)
                for c in range(2):
                    await_read_out(pe, ("q0", hf, c))
                    b = fill(pe, ("o0", hf, c))
                    for i in range(HI):
                        at = hf * HT + i * TOK
                        last = mm(b[0:C, i * TOK:(i + 1) * TOK], gkv[:, HI * hf + i, c, :], gq[:, c, at:at + TOK],
                                  start=True, stop=True)
                    full(last, ("o0", hf, c))
            for p in range(PAIRS):
                for c in range(2):
                    await_read_out(pe, ("o0", p // HP, c))
                token_major(("proj0", p), oT, wproj0, p, True)

            for hf in range(2):
                transposes(1, hf)
            pe.wait_ge(sem("set1_loaded"), 16 * 4)
            for hf in range(2):
                await_xT(1, hf)
                key = ("gate0", hf)
                b = fill(pe, key)
                for q, p in enumerate(pairs(hf)):
                    for kc in range(2):
                        rows = C + kc
                        last = mm(b[:, q * E0:(q + 1) * E0], xT[0:rows, kc, pair_cols(p)], gate0w[0:rows, kc, :],
                                  start=kc == 0, stop=kc == 1)
                full(last, key)
            y = {(hf, c): bank[2 * hf + c][0:C, 0:HT] for hf in range(2) for c in range(2)}

            def hidden0(x, buf, hf):
                for name in "ug":
                    b, n = uses[name, hf]
                    pe.wait_ge(bank_free[b], x + n)
                for name, at in (("u", 0), ("g", HID0)):
                    b, n = uses[name, hf]
                    o = by_image(bank[b][:, 0:HT])
                    for kc in range(2):
                        last = mm(o, up0[buf][:, kc, at:at + HID0], real(xT, kc, hf), start=kc == 0, stop=kc == 1)
                    last.then_inc(bank_full[b], 1)

            def sums0(x, buf, hf):
                pe.wait_ge(sem(f"act0_ready{hf}"), x + 1)
                for c in range(2):
                    last = mm(y[hf, c], down0[buf][:, c * C:(c + 1) * C], a0[hf], start=False, stop=False,
                              skip_group_check=True)
                return last

            pe.wait_ge(sem("expert0_loaded0"), 32)
            hidden0(0, 0, 0)
            hidden0(0, 0, 1)
            for hf in range(2):
                pe.wait_ge(sem("routed"), hf + 1)
                b = fill(pe, ("wT0", hf))
                for q in range(HP):
                    at = (HP * hf + q) * E0
                    last = nc.tensor.transpose(b[0:E0, q * 128:(q + 1) * 128], rt["w"][:, at:at + E0], ident[:, :])
                full(last, ("wT0", hf))
            for hf in range(2):
                await_read_out(pe, ("wT0", hf))
            for hf in range(2):
                for c in range(2):
                    fill(pe, ("y0", hf, c))
                    full(mm(y[hf, c], bd0[:, c * C:(c + 1) * C], wT[0:E0, half(hf)], start=True, stop=False,
                            skip_group_check=True), ("y0", hf, c))
            sums0(0, 0, 0)
            with pe.Fori(0, E0 // NB0) as it:
                for j in range(NB0):
                    x, buf = it * NB0 + (j + 1), (j + 1) % NB0
                    pe.wait_ge(sem(f"expert0_loaded{buf}"), it * 32 + 32 * (2 if buf == 0 else 1))
                    hidden0(x, buf, 0)
                    sums0(it * NB0 + j, j, 1).then_inc(sem("expert0_done"), 1)
                    hidden0(x, buf, 1)
                    sums0(x, buf, 0)
            sums0(E0, E0 % NB0, 1).then_inc(sem("expert0_done"), 1)

            def sums_token_major(tag):
                for p in range(PAIRS):
                    for c in range(2):
                        await_read_out(pe, (tag, p // HP, c))
                    b = fill(pe, (tag + "t", p))
                    for c in range(2):
                        last = nc.tensor.transpose(b[:, c * C:(c + 1) * C], oT[0:C, c, pair_cols(p)],
                                                   ident[0:C, 0:C])
                    full(last, (tag + "t", p))

            sums_token_major("y0")

            for hf in range(2):
                transposes(2, hf)
            pe.wait_ge(sem("set2_loaded"), 16 * 11)
            for m in range(4):
                b = fill(pe, ("rel_w", m))
                full(mm(b[:, 0:REL], wposT[:, m * 128:(m + 1) * 128], basis[:, :], start=True, stop=True),
                     ("rel_w", m))
            for hf in range(2):
                await_xT(2, hf)
                for m in range(4):
                    feature_major(("q1", hf, m), wq1, m * 128, 128, xT, hf)
                for m in range(4):
                    await_read_out(pe, ("rel_w", m))
                    await_read_out(pe, ("q1", hf, m))
                for p in pairs(hf):
                    for s in range(2):
                        b = fill(pe, ("rel", p, s))
                        for m in (2 * s, 2 * s + 1):
                            at = (m % 2) * 2 * REL
                            last = mm(b[:, at:at + 2 * REL], qv[:, m, pair_cols(p)],
                                      rbd[:, m].rearrange("p e r -> p (e r)"), start=True, stop=True)
                        full(last, ("rel", p, s))
                for m in range(4):
                    feature_major(("k1", hf, m), wk1, m * 128, 128, xT, hf)
                for q in range(2):
                    key = ("v1", hf, q)
                    b = fill(pe, key)
                    for i in range(4):
                        img = HI * hf + 4 * q + i
                        for par in range(2):
                            for kc in range(2):
                                last = mm(b[par * SLOT:(par + 1) * SLOT, i * C:(i + 1) * C],
                                          xT[0:C, kc, img * SLOT:(img + 1) * SLOT],
                                          wv1[:, kc, par * C:(par + 1) * C], start=kc == 0, stop=kc == 1,
                                          skip_group_check=True)
                    full(last, key)

            def scores1(p):
                if p % HP == 0:
                    for m in range(4):
                        await_read_out(pe, ("k1", p // HP, m))
                b = fill(pe, ("s1", p))
                for m in range(4):
                    for par in range(2):
                        img = 2 * p + par
                        last = mm(b[par * SLOT:(par + 1) * SLOT, m * 2 * TOK:(m + 1) * 2 * TOK],
                                  qu[:, m, img * SLOT:(img + 1) * SLOT],
                                  kbd1[:, m, img].rearrange("p e j -> p (e j)"), start=True, stop=True,
                                  skip_group_check=True)
                full(last, ("s1", p))

            for p in range(AHEAD):
                scores1(p)
            for p in range(PAIRS):
                pe.wait_ge(sem("exp1_done"), p + 1)
                b = fill(pe, ("p1t", p))
                for m in range(4):
                    last = nc.tensor.transpose(b[:, m * 128:(m + 1) * 128],
                                               probs1[:, p % AHEAD, 2 * m:2 * m + 2].rearrange("p h j -> p (h j)"),
                                               ident[:, :])
                full(last, ("p1t", p))
                if p + AHEAD < PAIRS:
                    scores1(p + AHEAD)
                await_read_out(pe, ("p1t", p))
                if p % 2 == 0:
                    await_read_out(pe, ("v1", p // HP, (p % HP) // 2))
                b = fill(pe, ("av1", p))
                for m in range(4):
                    for par in range(2):
                        img = 2 * p + par
                        last = mm(b[par * SLOT:(par + 1) * SLOT, m * 2 * HBV:(m + 1) * 2 * HBV],
                                  pt1[:, p % 2, m * 128 + par * SLOT:m * 128 + (par + 1) * SLOT],
                                  vbd1[:, img * 4 + m].rearrange("p e d -> p (e d)"), start=True, stop=True,
                                  skip_group_check=True)
                full(last, ("av1", p))

            def attended(tag, av, w, wo):
                for hf in range(2):
                    for p in pairs(hf):
                        await_read_out(pe, (av, p))
                    for c in range(2):
                        b = fill(pe, (tag, hf, c))
                        for q, p in enumerate(pairs(hf)):
                            last = nc.tensor.transpose(b[0:C, q * 128:(q + 1) * 128], xn[:, p, c * C:(c + 1) * C],
                                                       ident[:, :])
                        full(last, (tag, hf, c))
                for p in range(PAIRS):
                    for c in range(2):
                        await_read_out(pe, (tag, p // HP, c))
                    token_major((wo, p), oT, w, p, True)

            attended("o1t", "av1", wout1, "wo1")

            for hf in range(2):
                transposes(3, hf)
            for hf in range(2):
                await_xT(3, hf)
                for m in range(3):
                    feature_major(("f1", hf, m), w1a, m * 128, 128, xT, hf)
                for m in range(3):
                    await_read_out(pe, ("f1", hf, m))
                for p in pairs(hf):
                    b = fill(pe, ("f2", p))
                    for m in range(3):
                        last = mm(b[:, 0:D], g1[:, m, pair_cols(p)], w2a[:, m, :], start=m == 0, stop=m == 2)
                    full(last, ("f2", p))

            for hf in range(2):
                transposes(4, hf)
            pe.wait_ge(sem("set3_loaded"), 16 * 5)
            for hf in range(2):
                await_xT(4, hf)
                for c in range(2):
                    feature_major(("q2", hf, c), wqk2, c * C, C, xT, hf)
                for c in range(2):
                    feature_major(("k2", hf, c), wqk2, D + c * C, C, xT, hf)
                for q in range(2):
                    key = ("v2", hf, q)
                    b = fill(pe, key)
                    for i in range(4):
                        img = HI * hf + 4 * q + i
                        for par in range(2):
                            for kc in range(2):
                                rows = C + kc
                                last = mm(b[par * SLOT:(par + 1) * SLOT, i * C:(i + 1) * C],
                                          xT[0:rows, kc, img * SLOT:(img + 1) * SLOT],
                                          wv2[0:rows, kc, par * C:(par + 1) * C], start=kc == 0, stop=kc == 1,
                                          skip_group_check=True)
                    full(last, key)

            def scores2(p):
                if p % HP == 0:
                    for c in range(2):
                        await_read_out(pe, ("q2", p // HP, c))
                    pe.wait_ge(sem("keys2_masked_pool"), p // HP + 1)
                    pe.wait_ge(sem("keys2_masked_dve"), p // HP + 1)
                b = fill(pe, ("s2", p))
                for c in range(2):
                    for par in range(2):
                        img = 2 * p + par
                        last = mm(b[par * SLOT:(par + 1) * SLOT, c * 6 * TOK:(c + 1) * 6 * TOK],
                                  q2[:, c, img * SLOT:(img + 1) * SLOT],
                                  kbd2[:, c, img].rearrange("p e j -> p (e j)"), start=True, stop=True,
                                  skip_group_check=True)
                full(last, ("s2", p))

            for p in range(AHEAD):
                scores2(p)
            for p in range(PAIRS):
                pe.wait_ge(sem("exp2_done"), p + 1)
                for s in range(2):
                    b = fill(pe, ("p2t", p, s))
                    for m in range(3):
                        h0 = 2 * (3 * s + m)
                        last = nc.tensor.transpose(b[:, m * 128:(m + 1) * 128],
                                                   probs2[:, p % AHEAD, h0:h0 + 2].rearrange("p h j -> p (h j)"),
                                                   ident[:, :])
                    full(last, ("p2t", p, s))
                if p + AHEAD < PAIRS:
                    scores2(p + AHEAD)
                for s in range(2):
                    await_read_out(pe, ("p2t", p, s))
                if p % 2 == 0:
                    await_read_out(pe, ("v2", p // HP, (p % HP) // 2))
                b = fill(pe, ("av2", p))
                for m in range(6):
                    for par in range(2):
                        img = 2 * p + par
                        last = mm(b[par * SLOT:(par + 1) * SLOT, m * 2 * HFD:(m + 1) * 2 * HFD],
                                  pt2[:, p % 2, m * 128 + par * SLOT:m * 128 + (par + 1) * SLOT],
                                  vbd2[:, img * 6 + m].rearrange("p e d -> p (e d)"), start=True, stop=True,
                                  skip_group_check=True)
                full(last, ("av2", p))
            attended("o2t", "av2", wout2, "wo2")

            for hf in range(2):
                transposes(5, hf)
            for hf in range(2):
                await_xT(5, hf)
                key = ("gate1", hf)
                b = fill(pe, key)
                for q, p in enumerate(pairs(hf)):
                    for kc in range(2):
                        last = mm(b[:, q * E1:(q + 1) * E1], xT[0:C, kc, pair_cols(p)], gate1w[:, kc, :],
                                  start=kc == 0, stop=kc == 1)
                full(last, key)
            for hf in range(2):
                pe.wait_ge(sem("routed"), 2 + hf + 1)
                b = fill(pe, ("wT1", hf))
                for q in range(HP):
                    at = (HP * hf + q) * E1
                    last = nc.tensor.transpose(b[0:E1, q * 128:(q + 1) * 128], rt["w"][:, at:at + E1], ident[:, :])
                full(last, ("wT1", hf))

            for hf in range(2):
                await_read_out(pe, ("wT1", hf))
            for hf in range(2):
                for c in range(2):
                    fill(pe, ("y1", hf, c))
                    full(mm(y[hf, c], b2m[:, c * C:(c + 1) * C], wT[0:E1, half(hf)], start=True, stop=False,
                            skip_group_check=True), ("y1", hf, c))
            with pe.Fori(0, E1 // NB1) as it:
                for buf in range(NB1):
                    pe.wait_ge(sem(f"expert1_loaded{buf}"), it * 32 + 32)
                    for hf in range(2):
                        def hidden1(m):
                            n = hf * M1 + m
                            b, base = uses["hid", n % 4]
                            pe.wait_ge(bank_free[b], it * (NB1 * turns) + (base + buf * turns + n // 4))
                            o = by_image(bank[b][:, 0:HT])
                            for kc in range(2):
                                last = mm(o, up1[buf][:, kc, m * 128:(m + 1) * 128], real(xT, kc, hf),
                                          start=kc == 0, stop=kc == 1)
                            last.then_inc(bank_full[b], 1)

                        def sums1(m):
                            n = hf * M1 + m
                            pe.wait_ge(sem("hid1_ready"), it * (NB1 * 2 * M1) + (buf * 2 * M1 + n + 1))
                            for c in range(2):
                                last = mm(y[hf, c], down1[buf][:, m * D + c * C:m * D + (c + 1) * C],
                                          hs[n % 4], start=False, stop=False, skip_group_check=True)
                            return last

                        hidden1(0)
                        hidden1(1)
                        for m in range(2, M1):
                            hidden1(m)
                            sums1(m - 2)
                        sums1(M1 - 2)
                        last = sums1(M1 - 1)
                    last.then_inc(sem("expert1_done"), 1)
            sums_token_major("y1")

        @block.scalar
        def _(act):
            activation = nc.scalar.activation

            def columns(n, hf, scale=None, bias=None):
                key = (f"n{n}", hf, 0)
                b = read(act, key)
                free(activation(xT[0:C, 0, pad_half(hf)], b[0:C, :], ACT.Identity,
                                scale=col96(scale, 0) if scale else 1.0,
                                bias=col96(bias, 0) if bias else 0.0), key)

            for p in range(PAIRS):
                b = read(act, ("tok", p))
                free(activation(h[:, p, :], b[:, 0:D], ACT.Copy), ("tok", p))
            act.wait_ge(sem("set0_loaded"), 16 * 5)
            act.wait_ge(sem("pool_init"), 1)
            for hf in range(2):
                columns(0, hf)
            for hf in range(2):
                for c in range(2):
                    b = read(act, ("q0", hf, c))
                    free(activation(gq[:, c, half(hf)], b[0:C, 0:HT], ACT.Gelu), ("q0", hf, c))
                for p in pairs(hf):
                    if p % 2:
                        b = read(act, ("kv0", p))
                        free(activation(kv[:, p, :], b[:, 0:2 * D], ACT.Copy), ("kv0", p))
            for hf in range(2):
                for pp in range(2):
                    for par in range(2):
                        key = ("kTv", hf, pp, par)
                        b = read(act, key)
                        img = HI * hf + 4 * pp + par
                        free(activation(gkr[:, img:img + 3:2], b[0:C, 0:4 * C].rearrange(
                            "p (q c e) -> p q c e", q=2, c=2), ACT.Gelu, scale=float(HFD) ** -0.5), key)
            for hf in range(2):
                columns(1, hf)

            for hf in range(2):
                await_read_out(act, ("gate0", hf))
                activation(rt["e"][:, 0:HP * E0], rt["s"][:, 0:HP * E0], ACT.Exp).then_inc(sem("route_exp"), 1)

            def silu(x, buf, hf):
                b, n = uses["u", hf]
                act.wait_ge(bank_full[b], x + (n + 1))
                activation(s0[hf], bank[b][:, 0:HT], ACT.Silu, bias=down0[buf][:, D:D + 1])\
                    .then_inc(bank_free[b], 1)

            act.wait_ge(sem("expert0_loaded0"), 32)
            for hf in range(2):
                silu(0, 0, hf)
            for hf in range(2):
                b = read(act, ("wT0", hf))
                free(activation(by_image(wT[0:E0, half(hf)]), b[0:E0, :].rearrange(
                    "p (i t) -> p i t", t=SLOT)[:, :, 0:TOK], ACT.Copy), ("wT0", hf))
            with act.Fori(0, E0 // NB0) as it:
                for j in range(NB0):
                    x, buf = it * NB0 + (j + 1), (j + 1) % NB0
                    act.wait_ge(sem(f"expert0_loaded{buf}"), it * 32 + 32 * (2 if buf == 0 else 1))
                    for hf in range(2):
                        silu(x, buf, hf)
            act.wait_ge(sem("expert0_done"), E0 + 1)
            for hf in range(2):
                for c in range(2):
                    b = read(act, ("y0", hf, c))
                    free(activation(real(oT, c, hf), by_image(b[0:C, 0:HT]), ACT.Identity,
                                    bias=col96("sbd", c)), ("y0", hf, c))

            act.wait_ge(sem("set2_loaded"), 16 * 11)
            for hf in range(2):
                columns(2, hf, "rms1_w")
            act.wait_ge(sem("pads_zeroed"), 1)
            for hf in range(2):
                for m in range(4):
                    b = read(act, ("q1", hf, m))
                    activation(real(qu, m, hf), by_image(b[:, 0:HT]), ACT.Identity, bias=col128("u", m))
                    free(activation(real(qv, m, hf), by_image(b[:, 0:HT]), ACT.Identity, bias=col128("v", m)),
                         ("q1", hf, m))
                if hf:
                    act.wait_ge(sem("rel_stored"), 16)
                for q, p in enumerate(pairs(hf)):
                    for s in range(2):
                        b = read(act, ("rel", p, s))
                        free(activation(relb[:, q, s * 4 * REL:(s + 1) * 4 * REL], b[:, 0:4 * REL], ACT.Copy),
                             ("rel", p, s))

            def softmax_exp1(p):
                act.wait_ge(sem("shifted1"), p + 1)
                x = probs1[:, p % AHEAD, :, 0:TOK]
                activation(x, x, ACT.Exp, scale=float(HD) ** -0.5).then_inc(sem("exp1_done"), 1)

            for p in range(AHEAD):
                softmax_exp1(p)
            for p in range(PAIRS):
                b = read(act, ("p1t", p))
                free(activation(pt1[:, p % 2, :], b[:, :], ACT.Copy), ("p1t", p))
                if p + AHEAD < PAIRS:
                    softmax_exp1(p + AHEAD)

            def attended(tag):
                for hf in range(2):
                    b = read(act, (tag, hf, 0))
                    free(activation(oT[0:C, 0, pad_half(hf)], b[0:C, :], ACT.Copy), (tag, hf, 0))

            attended("o1t")
            for hf in range(2):
                columns(3, hf, "rms2_w")
            for hf in range(2):
                for m in range(3):
                    b = read(act, ("f1", hf, m))
                    free(activation(real(g1, m, hf), by_image(b[:, 0:HT]), ACT.Gelu, bias=col128("b1", m)),
                         ("f1", hf, m))

            for hf in range(2):
                columns(4, hf, "ln1_w", "ln1_b")
            for hf in range(2):
                for c in range(2):
                    b = read(act, ("q2", hf, c))
                    free(activation(real(q2, c, hf), by_image(b[0:C, 0:HT]), ACT.Identity, bias=col96("q_b", c)),
                         ("q2", hf, c))
                for c in range(2):
                    b = read(act, ("k2", hf, c))
                    free(activation(k2[:, c, half(hf)], b[0:C, 0:HT], ACT.Identity, bias=col96("k_b", c)),
                         ("k2", hf, c))

            def softmax_exp2(p):
                await_read_out(act, ("s2", p))
                x = probs2[:, p % AHEAD, :, 0:TOK]
                activation(x, x, ACT.Exp, scale=float(HFD) ** -0.5).then_inc(sem("exp2_done"), 1)

            for p in range(AHEAD):
                softmax_exp2(p)
            for p in range(PAIRS):
                for s in range(2):
                    b = read(act, ("p2t", p, s))
                    free(activation(pt2[:, p % 2, s * 384:(s + 1) * 384], b[:, 0:384], ACT.Copy), ("p2t", p, s))
                if p + AHEAD < PAIRS:
                    softmax_exp2(p + AHEAD)
            attended("o2t")
            for hf in range(2):
                columns(5, hf, "ln2_w", "ln2_b")

            for hf in range(2):
                await_read_out(act, ("gate1", hf))
                activation(rt["e"][:, 0:HP * E1], rt["s"][:, 0:HP * E1], ACT.Exp).then_inc(sem("route_exp"), 1)
            act.wait_ge(sem("w0_stored"), 16)
            for hf in range(2):
                b = read(act, ("wT1", hf))
                free(activation(by_image(wT[0:E1, half(hf)]), b[0:E1, :].rearrange(
                    "p (i t) -> p i t", t=SLOT)[:, :, 0:TOK], ACT.Copy), ("wT1", hf))

            with act.Fori(0, E1 // NB1) as it:
                for buf in range(NB1):
                    act.wait_ge(sem(f"expert1_loaded{buf}"), it * 32 + 32)
                    for n in range(2 * M1):
                        b, base = uses["hid", n % 4]
                        m = n % M1
                        act.wait_ge(bank_full[b], it * (NB1 * turns) + (base + buf * turns + n // 4 + 1))
                        activation(hg[n % 4], bank[b][:, 0:HT], ACT.Gelu,
                                   bias=down1[buf][:, M1 * D + m:M1 * D + m + 1]).then_inc(bank_free[b], 1)
            act.wait_ge(sem("expert1_done"), E1)
            for hf in range(2):
                for c in range(2):
                    b = read(act, ("y1", hf, c))
                    free(activation(real(oT, c, hf), by_image(b[0:C, 0:HT]), ACT.Copy), ("y1", hf, c))

        @block.vector
        def _(dve):
            tt, ts, stt, reduce = (nc.vector.tensor_tensor, nc.vector.tensor_scalar,
                                   nc.vector.scalar_tensor_tensor, nc.vector.tensor_reduce)
            step = [0]

            def link(ins):
                step[0] += 1
                ins.then_inc(sem("dve_step"), 1)
                dve.wait_ge(sem("dve_step"), step[0])

            def statistics(x, hf):
                for p in pairs(hf):
                    last = nc.vector.bn_stats(stats[:, p, :], x[:, p, :])
                link(last)
                for p in pairs(hf):
                    last = nc.vector.bn_aggr(mv[:, p, :], stats[:, p, :])
                last.then_inc(sem("stats_done"), 1)

            def normalize(n, hf, kind):
                dve.wait_ge(sem("rstd_done"), 2 * n + hf + 1)
                for p in pairs(hf):
                    mean = mv[:, p, 0:1]
                    first, second = pw_out[:, 0, p:p + 1], pw_out[:, 1, p:p + 1]
                    if kind == "ln":
                        last = ts(xn[:, p, :], rows[n][:, p, :], mean, first, ALU.subtract, ALU.mult)
                    elif kind == "ln+norm":
                        ts(u[:, p, :], rows[n][:, p, :], mean, first, ALU.subtract, ALU.mult)
                        last = ts(xn[:, p, :], rows[n][:, p, :], mean, second, ALU.subtract, ALU.mult)
                    else:
                        last = ts(xn[:, p, :], rows[n][:, p, :], first, None, ALU.mult)
                last.then_inc(sem("xn_done"), 1)

            def columns(n, hf, scale=None, bias=None):
                key = (f"n{n}", hf, 1)
                b = read(dve, key)
                if scale and bias:
                    last = ts(xT[0:C, 1, pad_half(hf)], b[0:C, :], col96(scale, 1), col96(bias, 1), ALU.mult, ALU.add)
                elif scale:
                    last = ts(xT[0:C, 1, pad_half(hf)], b[0:C, :], col96(scale, 1), None, ALU.mult)
                else:
                    last = nc.vector.tensor_copy(xT[0:C, 1, pad_half(hf)], b[0:C, :])
                free(last, key)

            rows = {0: h, 1: h, 2: h, 3: u, 4: h, 5: u}

            def add_to(x, key, y):
                b = read(dve, key)
                last = tt(x[:, key[1], :], b[:, 0:D], y[:, key[1], :], ALU.add)
                free(last, key)
                await_read_out(dve, key)

            for hf in range(2):
                for p in pairs(hf):
                    await_read_out(dve, ("tok", p))
                statistics(h, hf)
            for hf in range(2):
                normalize(0, hf, "ln")
            dve.wait_ge(sem("pool_init"), 1)
            for hf in range(2):
                columns(0, hf)
            for hf in range(2):
                for p in pairs(hf):
                    if p % 2 == 0:
                        b = read(dve, ("kv0", p))
                        free(nc.vector.tensor_copy(kv[:, p, :], b[:, 0:2 * D]), ("kv0", p))
            for hf in range(2):
                for c in range(2):
                    b = read(dve, ("o0", hf, c))
                    free(nc.vector.tensor_copy(real(oT, c, hf), by_image(b[0:C, 0:HT])), ("o0", hf, c))
            for hf in range(2):
                for p in pairs(hf):
                    add_to(h, ("proj0", p), h)
                statistics(h, hf)
            for hf in range(2):
                normalize(1, hf, "ln")
            for hf in range(2):
                columns(1, hf)

            def by_token(name, n):
                return rt[name][:, 0:HP * n].rearrange("p (q e) -> p q e", q=HP)

            def ranks(x, n, tri_at):
                shape = [128, HP, n, n]
                mine, other = x.unsqueeze(3).broadcast_to(shape), x.unsqueeze(2).broadcast_to(shape)
                gt = rt_gt[:, 0:HP * n * n].rearrange("p (q e f) -> p q e f", q=HP, e=n)
                eq = rt_eq[:, 0:HP * n * n].rearrange("p (q e f) -> p q e f", q=HP, e=n)
                lower = tri[:, tri_at:tri_at + n * n].rearrange("p (e f) -> p e f", e=n)\
                    .unsqueeze(1).broadcast_to(shape)
                tt(gt, other, mine, ALU.is_gt)
                link(tt(eq, other, mine, ALU.is_equal))
                link(tt(eq, eq, lower, ALU.mult))
                link(tt(gt, gt, eq, ALU.add))
                link(reduce(by_token("rank", n), gt, AX.X, ALU.add))

            def spread(x, n):
                return x.unsqueeze(2).broadcast_to([128, HP, n])

            dve.wait_ge(sem("set1_loaded"), 16 * 4)
            for hf in range(2):
                b = read(dve, ("gate0", hf))
                logits = b[:, 0:HP * E0].rearrange("p (q e) -> p q e", q=HP)
                e, score, sb_, gm = by_token("e", E0), by_token("score", E0), by_token("s", E0), by_token("gm", G0)
                link(reduce(rt["mx"][:, :], logits, AX.X, ALU.max))
                free(tt(sb_, logits, spread(rt["mx"], E0), ALU.subtract), ("gate0", hf))
                await_read_out(dve, ("gate0", hf))
                dve.wait_ge(sem("route_exp"), hf + 1)
                link(reduce(rt["sum"][:, :], e, AX.X, ALU.add))
                link(nc.vector.reciprocal(rt["inv"][:, :], rt["sum"][:, :]))
                link(tt(score, e, spread(rt["inv"], E0), ALU.mult))
                link(tt(sb_, score, route_bias[:, :].unsqueeze(1).broadcast_to([128, HP, E0]), ALU.add))
                two = rt["s"][:, 0:HP * E0].rearrange("p (n two) -> p n two", two=2)
                link(reduce(rt["gs"][:, :], two, AX.X, ALU.add))
                ranks(by_token("gs", G0), G0, 0)
                link(ts(gm, by_token("rank", G0), 4.0, None, ALU.is_lt))
                ts(rt["pen"][:, :], rt["gm"][:, :], BIG, BIG, ALU.mult, ALU.subtract)
                link(tt(two, two, rt["gm"][:, :].unsqueeze(2).broadcast_to([128, HP * G0, 2]), ALU.mult))
                link(tt(two, two, rt["pen"][:, :].unsqueeze(2).broadcast_to([128, HP * G0, 2]), ALU.add))
                ranks(sb_, E0, G0 * G0)
                link(ts(by_token("sel", E0), by_token("rank", E0), 4.0, 2.5, ALU.is_lt, ALU.mult))
                w = rt["w"][:, hf * HP * E0:(hf + 1) * HP * E0].rearrange("p (q e) -> p q e", q=HP)
                tt(w, score, by_token("sel", E0), ALU.mult).then_inc(sem("routed"), 1)

            def gate(x, buf, hf, dst):
                b, n = uses["g", hf]
                dve.wait_ge(bank_full[b], x + (n + 1))
                bu, nu = uses["u", hf]
                dve.wait_ge(bank_free[bu], x + (nu + 1))
                return stt(dst, bank[b][:, 0:HT], down0[buf][:, D + 1:D + 2], s0[hf], ALU.add, ALU.mult), bank_free[b]

            dve.wait_ge(sem("expert0_loaded0"), 32)
            for hf in range(2):
                ins, freed = gate(0, 0, hf, f0[hf])
                ins.then_inc(freed, 1)
                dve.wait_ge(freed, uses["g", hf][1] + 1)
                nc.vector.tensor_copy(a0[hf], f0[hf]).then_inc(sem(f"act0_ready{hf}"), 1)
            with dve.Fori(0, E0 // NB0) as it:
                for j in range(NB0):
                    x, buf = it * NB0 + (j + 1), (j + 1) % NB0
                    dve.wait_ge(sem(f"w0_loaded{buf}"), it * 16 + 16)
                    for hf in range(2):
                        ins, freed = gate(x, buf, hf, f0[hf])
                        ins.then_inc(freed, 1)
                        dve.wait_ge(freed, x + (uses["g", hf][1] + 1))
                        tt(a0[hf], f0[hf], wb0[buf][:, half(hf)], ALU.mult).then_inc(sem(f"act0_ready{hf}"), 1)
            for hf in range(2):
                for p in pairs(hf):
                    add_to(h, ("y0t", p), h)
                statistics(h, hf)

            for hf in range(2):
                normalize(2, hf, "ln+norm")
            dve.wait_ge(sem("set2_loaded"), 16 * 11)
            for hf in range(2):
                columns(2, hf, "rms1_w")
            for m in range(4):
                b = read(dve, ("rel_w", m))
                free(tt(rbd[:, m], b[:, 0:REL].unsqueeze(1).broadcast_to([128, 2, REL]),
                        mask_pair[:, :].unsqueeze(2).broadcast_to([128, 2, REL]), ALU.mult), ("rel_w", m))
            for hf in range(2):
                imgs = slice(HI * hf, HI * hf + HI)
                for m in range(4):
                    b = read(dve, ("k1", hf, m))
                    shape = [128, HI, 2, TOK]
                    free(tt(kbd1[:, m, imgs], by_image(b[:, 0:HT]).unsqueeze(2).broadcast_to(shape),
                            mask_pair[:, :].unsqueeze(1).unsqueeze(3).broadcast_to(shape), ALU.mult), ("k1", hf, m))
                for q in range(2):
                    b = read(dve, ("v1", hf, q))
                    shape = [128, 16, 2, HBV]
                    at = (HI * hf + 4 * q) * 4
                    free(tt(vbd1[:, at:at + 16], b[:, 0:4 * C].rearrange("p (n d) -> p n d", d=HBV)
                            .unsqueeze(2).broadcast_to(shape),
                            mask_pair[:, :].unsqueeze(1).unsqueeze(3).broadcast_to(shape), ALU.mult), ("v1", hf, q))

            def shifted1(p):
                if p % HP == 0:
                    dve.wait_ge(sem(f"rel_loaded{p // HP}"), 16 * 2 * HP)
                x = probs1[:, p % AHEAD, :, 0:TOK]
                b = read(dve, ("s1", p))
                free(tt(x, b[:, 0:HB * TOK].rearrange("p (h j) -> p h j", h=HB), rels[:, p], ALU.add), ("s1", p))
                await_read_out(dve, ("s1", p))
                mx = row_max[:, p, 0:HB]
                link(reduce(mx, x, AX.X, ALU.max))
                tt(x, x, mx.unsqueeze(2).broadcast_to([128, HB, TOK]), ALU.subtract).then_inc(sem("shifted1"), 1)

            def sums(p, probs, done, n):
                dve.wait_ge(sem(done), p + 1)
                link(reduce(row_sum[:, p, 0:n], probs[:, p % AHEAD, :, 0:TOK], AX.X, ALU.add))
                link(nc.vector.reciprocal(row_inv[:, p, 0:n], row_sum[:, p, 0:n]))

            def scaled(p, key, n):
                b = read(dve, key)
                shape = [128, n, D // n]
                ins = tt(xn[:, p, :].rearrange("p (h d) -> p h d", h=n),
                         b[:, 0:D].rearrange("p (h d) -> p h d", h=n),
                         row_inv[:, p, 0:n].unsqueeze(2).broadcast_to(shape), ALU.mult)
                free(ins, key)

            for p in range(AHEAD):
                shifted1(p)
            for p in range(PAIRS):
                sums(p, probs1, "exp1_done", HB)
                if p + AHEAD < PAIRS:
                    shifted1(p + AHEAD)
                scaled(p, ("av1", p), HB)

            def attended(tag):
                for hf in range(2):
                    b = read(dve, (tag, hf, 1))
                    free(nc.vector.tensor_copy(oT[0:C, 1, pad_half(hf)], b[0:C, :]), (tag, hf, 1))

            attended("o1t")
            for hf in range(2):
                for p in pairs(hf):
                    add_to(u, ("wo1", p), u)
                statistics(u, hf)
            for hf in range(2):
                normalize(3, hf, "rms")
            for hf in range(2):
                columns(3, hf, "rms2_w")
            dve.wait_ge(sem("skip1_added"), 1)
            for hf in range(2):
                for p in pairs(hf):
                    add_to(h, ("f2", p), h)
                statistics(h, hf)

            for hf in range(2):
                normalize(4, hf, "ln+norm")
            dve.wait_ge(sem("set3_loaded"), 16 * 5)
            for hf in range(2):
                columns(4, hf, "ln1_w", "ln1_b")
            for hf in range(2):
                imgs = slice(HI * hf, HI * hf + HI)
                await_read_out(dve, ("k2", hf, 1))
                shape = [C, HI, 6, TOK]
                tt(kbd2[:, 1, imgs], by_image(k2[:, 1, half(hf)]).unsqueeze(2).broadcast_to(shape),
                   mask_head[:, :].unsqueeze(1).unsqueeze(3).broadcast_to(shape), ALU.mult)\
                    .then_inc(sem("keys2_masked_dve"), 1)
                for q in range(2):
                    b = read(dve, ("v2", hf, q))
                    shape = [128, 24, 2, HFD]
                    at = (HI * hf + 4 * q) * 6
                    free(tt(vbd2[:, at:at + 24], b[:, 0:4 * C].rearrange("p (n d) -> p n d", d=HFD)
                            .unsqueeze(2).broadcast_to(shape),
                            mask_pair[:, :].unsqueeze(1).unsqueeze(3).broadcast_to(shape), ALU.mult), ("v2", hf, q))

            def shifted2(p):
                x = probs2[:, p % AHEAD, :, 0:TOK]
                b = read(dve, ("s2", p))
                scores = b[:, 0:HF * TOK].rearrange("p (h j) -> p h j", h=HF)
                mx = row_max[:, p, :]
                link(reduce(mx, scores, AX.X, ALU.max))
                free(tt(x, scores, mx.unsqueeze(2).broadcast_to([128, HF, TOK]), ALU.subtract), ("s2", p))

            for p in range(AHEAD):
                shifted2(p)
            for p in range(PAIRS):
                sums(p, probs2, "exp2_done", HF)
                if p + AHEAD < PAIRS:
                    shifted2(p + AHEAD)
                scaled(p, ("av2", p), HF)
            attended("o2t")
            for hf in range(2):
                for p in pairs(hf):
                    add_to(u, ("wo2", p), u)
                statistics(u, hf)
            for hf in range(2):
                normalize(5, hf, "ln")
            for hf in range(2):
                columns(5, hf, "ln2_w", "ln2_b")

            for hf in range(2):
                b = read(dve, ("gate1", hf))
                logits = b[:, 0:HP * E1].rearrange("p (q e) -> p q e", q=HP)
                e, sh = by_token("e", E1), by_token("s", E1)
                link(reduce(rt["mx"][:, :], logits, AX.X, ALU.max))
                free(tt(sh, logits, spread(rt["mx"], E1), ALU.subtract), ("gate1", hf))
                await_read_out(dve, ("gate1", hf))
                ranks(sh, E1, 0)
                link(ts(by_token("sel", E1), by_token("rank", E1), 2.0, None, ALU.is_lt))
                dve.wait_ge(sem("route_exp"), 2 + hf + 1)
                link(tt(e, e, by_token("sel", E1), ALU.mult))
                link(reduce(rt["sum"][:, :], e, AX.X, ALU.add))
                link(nc.vector.reciprocal(rt["inv"][:, :], rt["sum"][:, :]))
                w = rt["w"][:, hf * HP * E1:(hf + 1) * HP * E1].rearrange("p (q e) -> p q e", q=HP)
                tt(w, e, spread(rt["inv"], E1), ALU.mult).then_inc(sem("routed"), 1)

            with dve.Fori(0, E1 // NB1) as it:
                for buf in range(NB1):
                    dve.wait_ge(sem(f"w1_loaded{buf}"), it * 16 + 16)
                    for n in range(2 * M1):
                        b, base = uses["hid", n % 4]
                        dve.wait_ge(bank_free[b], it * (NB1 * turns) + (base + buf * turns + n // 4 + 1))
                        tt(hs[n % 4], hg[n % 4], wb1[buf][:, half(n // M1)], ALU.mult)\
                            .then_inc(sem("hid1_ready"), 1)
            dve.wait_ge(sem("skip2_added"), 1)
            for p in range(PAIRS):
                b = read(dve, ("y1t", p))
                tt(h[:, p, :], b[:, 0:D], h[:, p, :], ALU.add).then_inc(sem("result_ready"), 1)


def laid_out(i):
    f = {k: np.asarray(v) for k, v in i.items()}
    z = np.zeros
    t = np.float32

    def chunks(w, p=C):
        return np.ascontiguousarray(w.reshape(-1, p, w.shape[1]).transpose(1, 0, 2))

    def biased(w, b):
        r = z((C + 1, 2, w.shape[1]), t)
        r[:C] = chunks(w)
        r[C, 1] = b
        return r

    def columns(v, p=C):
        return v.reshape(-1, p).T

    def by_parity(w, heads):
        return w.reshape(*w.shape[:-1], heads // 2, 2, D // heads).swapaxes(-3, -2).reshape(*w.shape[:-1], D)

    p = f["x"].reshape(IMAGES, 3, 6, 16, 6, 16).transpose(0, 2, 4, 1, 3, 5).reshape(IMAGES, TOK, 768)
    padded = z((IMAGES, SLOT, 768), t)
    padded[:, :TOK] = p
    o = {}
    o["patches"] = padded.reshape(PAIRS, 128, PATCH_CHUNKS, 128).transpose(0, 3, 2, 1)
    o["tok_w"] = chunks(f["L0_tok_W"].T, 128)
    o["wqkv0"] = chunks(f["L0_attn_w_qkv"])
    o["wproj0"] = biased(f["L0_attn_w_proj"], f["L0_attn_b_proj"])
    o["gate0w"] = biased(f["L0_ffn_gate_w"], f["L0_ffn_gate_b"])
    o["route_bias"] = np.tile(f["L0_ffn_bias"], (128, 1))
    o["bd0"] = f["L0_ffn_bd"]
    wu = np.concatenate([f["L0_ffn_sWu"][None], f["L0_ffn_Wu"]]).reshape(E0 + 1, 2, C, HID0)
    wg = np.concatenate([f["L0_ffn_sWg"][None], f["L0_ffn_Wg"]]).reshape(E0 + 1, 2, C, HID0)
    o["up0"] = np.concatenate([wu, wg], 3).transpose(0, 2, 1, 3)
    wd = np.concatenate([f["L0_ffn_sWd"][None], f["L0_ffn_Wd"]])
    bu = np.concatenate([f["L0_ffn_sbu"][None], f["L0_ffn_bu"]])[:, :, None]
    bg = np.concatenate([f["L0_ffn_sbg"][None], f["L0_ffn_bg"]])[:, :, None]
    o["down0"] = np.concatenate([wd, bu, bg], 2)
    o["wq1"], o["wk1"] = chunks(f["L1_attn_wq"]), chunks(f["L1_attn_wk"])
    o["wv1"] = chunks(by_parity(f["L1_attn_wv"], HB))
    o["wout1"] = biased(f["L1_attn_wo"], f["L1_attn_bo"])
    o["wposT"] = f["L1_attn_w_pos"].reshape(HB * HD, NPOS).T
    o["w1a"], o["w2a"] = chunks(f["L1_attn_w1"]), chunks(f["L1_attn_w2"], 128)
    o["b2_row"] = np.tile(f["L1_attn_b2"], (128, 1))
    qkv = f["L1_ffn_qkv_w"].T
    o["wqk2"] = chunks(qkv[:, :2 * D])
    qkv_b = f["L1_ffn_qkv_b"]
    o["wv2"] = biased(by_parity(qkv[:, 2 * D:], HF), by_parity(qkv_b[2 * D:], HF))
    o["wout2"] = biased(f["L1_ffn_proj_w"].T, f["L1_ffn_proj_b"])
    o["gate1w"] = chunks(f["L1_ffn_w_gate"])
    o["b2m"] = f["L1_ffn_b2"]
    o["up1"] = f["L1_ffn_W1"].reshape(E1, 2, C, HID1M).transpose(0, 2, 1, 3)
    w2 = f["L1_ffn_W2"].reshape(E1, M1, 128, D).transpose(0, 2, 1, 3).reshape(E1, 128, M1 * D)
    o["down1"] = np.concatenate([w2, f["L1_ffn_b1"].reshape(E1, M1, 128).transpose(0, 2, 1)], 2)
    o["c96"] = np.concatenate([columns(v) for v in (
        f["L0_ffn_sbd"], f["L1_attn_norm1_w"], f["L1_attn_norm2_w"], f["L1_ffn_norm1_w"], f["L1_ffn_norm1_b"],
        f["L1_ffn_norm2_w"], f["L1_ffn_norm2_b"], qkv_b[:D], qkv_b[D:2 * D])], 1)
    o["c128"] = np.concatenate([columns(f["L1_attn_u_param"].reshape(-1), 128),
                                columns(f["L1_attn_v_param"].reshape(-1), 128),
                                columns(f["L1_attn_b1"], 128)], 1)
    o["ident"] = np.eye(128, dtype=t)
    o["mask_pair"] = (np.arange(128)[:, None] // 64 == np.arange(2)).astype(t)
    o["mask_head"] = (np.arange(C)[:, None] // HFD == np.arange(6)).astype(t)
    lower = lambda n: (np.arange(n)[None, :] < np.arange(n)[:, None]).astype(t).reshape(-1)
    o["tri"] = np.tile(np.concatenate([lower(G0), lower(E0)]), (128, 1))
    d = np.arange(-(TOK - 1), TOK).astype(t)
    rate = np.exp(np.log(t((TOK + 1) / 2.0)) / t(NPOS // 2)).astype(t)
    widths = (rate ** np.arange(1, NPOS // 2 + 1, dtype=t)).astype(t)
    near = (np.abs(d)[None, :] <= widths[:, None]).astype(t)
    o["basis"] = np.concatenate([near, np.sign(d)[None, :] * near]).astype(t)
    return {k: np.ascontiguousarray(v) for k, v in o.items()}


def kernel(**inputs):
    import concourse.bacc as bacc
    from concourse.bass_utils import run_bass_kernel_spmd

    arrays = laid_out(inputs)
    nc = bacc.Bacc("TRN2", target_bir_lowering=False, num_devices=1)
    args = {k: nc.dram_tensor(f"in_{k}", v.shape, mybir.dt.from_np(v.dtype), kind="ExternalInput").ap()
            for k, v in arrays.items()}
    out = nc.dram_tensor("out", (IMAGES, TOK, D), F32, kind="ExternalOutput").ap()
    build_tower(nc, args, out)
    r = run_bass_kernel_spmd(nc, [{f"in_{k}": v for k, v in arrays.items()}], core_ids=[0])
    return r.results[0]["out"]
```

```python
from contextlib import ExitStack

import numpy as np

import concourse.bass as bass
from concourse import mybir

F32 = mybir.dt.float32
F32R = mybir.dt.float32r
ALU = mybir.AluOpType
ACT = mybir.ActivationFunctionType
AX = mybir.AxisListType

IMAGES = 16
TOK = 36
D = 192
C = 96
SLOT = 64
PAIRS = IMAGES // 2
HP = PAIRS // 2
HI = IMAGES // 2
HT = HI * TOK
T = IMAGES * TOK
PATCH_CHUNKS = 768 // 128
PATCH_LOADS = [(0, 1), (1, 1), (2, 2), (4, 2), (6, 2)]
EPS = 1e-5

H0 = 12
HB, HD = 8, 64
HBV = D // HB
HF, HFD = 12, 16
REL = 2 * TOK - 1
NPOS = 32
HID1 = 384

E0, G0, HID0 = 16, 8, 128
E1, HID1M = 8, 768
M1 = HID1M // 128
NB0, NB1 = 4, 2
AHEAD = 4
BIG = 1.0e30

COL96 = {n: (2 * i, 2) for i, n in enumerate(
    ["sbd", "rms1_w", "rms2_w", "ln1_w", "ln1_b", "ln2_w", "ln2_b", "q_b", "k_b"])}
N96 = 2 * len(COL96)
COL128 = {"u": (0, 4), "v": (4, 4), "b1": (8, 3)}
N128 = 11


def psum_uses():
    keys = []
    halves = range(2)
    pairs = lambda hf: range(HP * hf, HP * hf + HP)

    def norm(tag, hf):
        keys.extend((tag, hf, c) for c in range(2))

    keys.extend(("tok", p) for p in range(HP + 2))
    norm("n0", 0)
    keys.extend(("tok", p) for p in range(HP + 2, PAIRS))
    for hf in halves:
        if hf:
            norm("n0", 1)
            keys.extend(("kTv", 0, pp, par) for pp in range(2) for par in range(2))
        keys.extend(("q0", hf, c) for c in range(2))
        keys.extend(("kv0", p) for p in pairs(hf))
    keys.extend(("o0", 0, c) for c in range(2))
    keys.extend(("kTv", 1, pp, par) for pp in range(2) for par in range(2))
    keys.extend(("proj0", p) for p in pairs(0))
    keys.extend(("o0", 1, c) for c in range(2))
    keys.extend(("proj0", p) for p in pairs(1))
    for hf in halves:
        norm("n1", hf)
        keys.append(("gate0", hf))
    used, uses, at = [0] * 8, {}, 0

    def place(keys, at):
        for k in keys:
            b = at % 8
            assert k not in uses
            uses[k] = (b, used[b])
            used[b] += 1
            at += 1
        return at

    place(keys, at)
    for hf in halves:
        uses["wT0", hf] = (2 * hf, used[2 * hf])
        used[2 * hf] += 1
    for hf in halves:
        uses["u", hf] = (4 + 2 * hf, used[4 + 2 * hf])
        uses["g", hf] = (5 + 2 * hf, used[5 + 2 * hf])
        for c in range(2):
            uses["y0", hf, c] = (2 * hf + c, used[2 * hf + c])
    for b in range(4):
        used[b] += 1
        used[4 + b] += E0 + 1
    place([("y0t", p) for p in range(PAIRS)], 4)
    keys = [("rel_w", m) for m in range(4)]
    for hf in halves:
        keys += [("n2", hf, c) for c in range(2)]
    for hf in halves:
        keys += [("q1", hf, m) for m in range(4)]
        keys += [("k1", hf, m) for m in range(4)]
        keys += [("rel", p, s) for p in pairs(hf) for s in range(2)]
        keys += [("v1", hf, q) for q in range(2)]
    keys += [("s1", p) for p in range(AHEAD)]
    for p in range(PAIRS + 1):
        keys += [("p1t", p)] * (p < PAIRS) + [("s1", p + AHEAD)] * (p + AHEAD < PAIRS)
        keys += [("av1", p - 1)] * (p > 0)
        if p == HP + 1:
            norm("o1t", 0)
        if p == HP + 2:
            keys += [("wo1", q) for q in pairs(0)]
    norm("o1t", 1)
    keys += [("wo1", p) for p in pairs(1)]
    norm("n3", 0)
    keys += [("f1", 0, m) for m in range(3)]
    norm("n3", 1)
    keys += [("f2", p) for p in pairs(0)]
    keys += [("f1", 1, m) for m in range(3)]
    norm("n4", 0)
    keys += [("f2", p) for p in pairs(1)]
    for hf in halves:
        keys += [("q2", hf, c) for c in range(2)]
        keys += [("k2", hf, c) for c in range(2)]
        if hf == 0:
            norm("n4", 1)
        keys += [("v2", hf, q) for q in range(2)]
    keys += [("s2", p) for p in range(AHEAD)]
    for p in range(PAIRS + 1):
        keys += [("p2t", p, 0), ("p2t", p, 1)] * (p < PAIRS) + [("s2", p + AHEAD)] * (p + AHEAD < PAIRS)
        keys += [("av2", p - 1)] * (p > 0)
        if p == HP + 1:
            norm("o2t", 0)
        if p == HP + 2:
            keys += [("wo2", q) for q in pairs(0)]
    norm("o2t", 1)
    keys += [("wo2", p) for p in pairs(1)]
    for hf in halves:
        norm("n5", hf)
        keys.append(("gate1", hf))
    place(keys, 0)
    for hf in halves:
        uses["wT1", hf] = (2 * hf, used[2 * hf])
        used[2 * hf] += 1
    uses["first_row1"] = (7, used[7])
    used[7] += 1
    for b in range(4):
        uses["hid", b] = (4 + b, used[4 + b])
        uses["y1", b // 2, b % 2] = (b, used[b])
    for b in range(4):
        used[b] += 1
        used[4 + b] += E1 * 2 * M1 // 4
    place([("y1t", p) for p in range(PAIRS)], 4)
    return uses


def build_tower(nc, a, out):
    uses = psum_uses()
    ctx = ExitStack()
    with ctx:
        def sb(name, shape):
            return ctx.enter_context(nc.sbuf_tensor(name, shape, F32))

        semaphores = {}

        def sem(name):
            if name not in semaphores:
                semaphores[name] = ctx.enter_context(nc.semaphore(name))
            return semaphores[name]

        def dram(name, shape):
            return nc.dram_tensor(name, shape, F32, kind="Internal").ap()

        bank = [ctx.enter_context(nc.psum_tensor(f"bank{b}", [128, 512], F32)) for b in range(8)]
        bank_full = [sem(f"bank_full{b}") for b in range(8)]
        bank_free = [sem(f"bank_free{b}") for b in range(8)]

        rel_d = dram("rel_by_distance", [PAIRS, 128, HB * REL])
        w0_d = dram("expert_weights0", [E0, T])
        w1_d = dram("expert_weights1", [E1, T])

        h = sb("h", [128, PAIRS, D])
        xn = sb("xn", [128, PAIRS, D])
        u = sb("u", [128, PAIRS, D])
        stats = sb("stats", [128, PAIRS, 6])
        mv = sb("mv", [128, PAIRS, 2])
        pw_in = sb("pw_in", [128, 2, PAIRS])
        pw_out = sb("pw_out", [128, 2, PAIRS])
        minus_half = sb("minus_half", [128, 2, PAIRS])
        warm = sb("warm", [128, 1])
        warm_dve = sb("warm_dve", [128, 1])
        first_row = sb("first_row", [E1, 128])
        row_max = sb("row_max", [128, PAIRS, HF])
        row_sum = sb("row_sum", [128, PAIRS, HF])
        row_inv = sb("row_inv", [128, PAIRS, HF])

        xT = sb("xT", [97, 2, IMAGES * SLOT])
        oT = sb("oT", [97, 2, IMAGES * SLOT])

        ident = sb("ident", [128, 128])
        mask_pair = sb("mask_pair", [128, 2])
        mask_head = sb("mask_head", [C, 6])
        run = sb("run", [128, PAIRS * (G0 + E0)])
        basis = sb("basis", [NPOS, REL])
        c96 = sb("c96", [C, N96])
        c128 = sb("c128", [128, N128])
        b2_row = sb("b2_row", [128, D])
        route_bias = sb("route_bias", [128, E0])
        wproj0 = sb("wproj0", [97, 2, D])
        gate0w = sb("gate0w", [97, 2, E0])
        bd0 = sb("bd0", [E0, D])
        wq1 = sb("wq1", [C, 2, HB * HD])
        wk1 = sb("wk1", [C, 2, HB * HD])
        wv1 = sb("wv1", [C, 2, D])
        wout1 = sb("wout1", [97, 2, D])
        wposT = sb("wposT", [NPOS, HB * HD])
        w1a = sb("w1a", [C, 2, HID1])
        w2a = sb("w2a", [128, 3, D])
        wqk2 = sb("wqk2", [C, 2, 2 * D])
        wv2 = sb("wv2", [97, 2, D])
        wout2 = sb("wout2", [97, 2, D])
        gate1w = sb("gate1w", [C, 2, E1])
        b2m = sb("b2m", [E1, D])
        wT = sb("wT", [E0, T])

        def phase():
            return ExitStack()

        def in_phase(scope, name, shape, dt=F32):
            return scope.enter_context(nc.sbuf_tensor(name, shape, dt))

        with phase() as scope:
            arena = in_phase(scope, "arena", [128, 25624])

        def part(lo, n):
            return arena[:, lo:lo + n]

        KB, VB, PT, QU, QV, RS, PP = 0, 7448, 10520, 12056, 16152, 20248, 22552
        qu = part(QU, 4096).rearrange("p (m t) -> p m t", m=4)
        qv = part(QV, 4096).rearrange("p (m t) -> p m t", m=4)
        kbd1 = part(KB, 4608).rearrange("p (m i e j) -> p m i e j", m=4, i=IMAGES, e=2)
        rbd = part(KB + 4608, 568).rearrange("p (m e r) -> p m e r", m=4, e=2)
        relb = part(KB + 5176, HP * HB * REL).rearrange("p (q n) -> p q n", q=HP)
        rels = part(RS, PAIRS * HB * TOK).rearrange("p (q h j) -> p q h j", q=PAIRS, h=HB)
        vbd1 = part(VB, IMAGES * D).rearrange("p (n e d) -> p n e d", e=2, d=HBV)
        probs1 = part(PP, AHEAD * HB * SLOT).rearrange("p (r h j) -> p r h j", r=AHEAD, h=HB)
        pt1 = part(PT, 2 * 512).rearrange("p (r n) -> p r n", r=2)
        g1 = qu[:, 0:3, :]
        q2 = qv[0:C, 0:2, :]
        kbd2 = part(KB, 6912)[0:C, :].rearrange("p (c i e j) -> p c i e j", c=2, i=IMAGES, e=6)
        k2 = part(RS, 2 * T)[0:C, :].rearrange("p (c t) -> p c t", c=2)
        vbd2 = part(VB, IMAGES * D).rearrange("p (n e d) -> p n e d", e=2, d=HFD)
        probs2 = part(PP, AHEAD * HF * SLOT).rearrange("p (r h j) -> p r h j", r=AHEAD, h=HF)
        pt2 = part(PT, 2 * 768).rearrange("p (r n) -> p r n", r=2)
        xp = part(0, 6144).rearrange("p (q k t) -> p q k t", q=PAIRS, k=PATCH_CHUNKS)
        tokw = part(6144, 1152).rearrange("p (k n) -> p k n", k=PATCH_CHUNKS)
        kv = part(7296, 3072).rearrange("p (q n) -> p q n", q=PAIRS)
        gq = part(10368, 1152)[0:C, :].rearrange("p (c t) -> p c t", c=2)
        gkr = part(11520, 3072)[0:C, :].rearrange("p (i c e) -> p i c e", i=IMAGES, c=2)
        gkv = part(14592, 3072)[0:C, :].rearrange("p (i c e) -> p i c e", i=IMAGES, c=2)
        wqkv0 = part(17664, 1152)[0:C, :].rearrange("p (c n) -> p c n", c=2)

        def routing_buffers(at):
            t = {}
            for name, n in (("e", E0), ("score", E0), ("s", E0), ("gs", G0), ("sel", E0), ("w", E0),
                            ("le", E0), ("eq", E0), ("before", E0), ("top", 8), ("pen", G0),
                            ("mx", 1), ("sum", 1), ("inv", 1), ("les", 1)):
                n *= PAIRS
                t[name] = part(at, n)
                at += n
            return t

        rt0, rt1 = routing_buffers(8832), routing_buffers(RS)

        def parts(scope, name, shape):
            return [in_phase(scope, f"{name}_{x}", shape, F32R) for x in ("high", "low")]

        with phase() as scope:
            x0 = parts(scope, "x0", [C, 2, IMAGES * SLOT])
            up0s = [parts(scope, f"up0_{b}", [C, 2, 2 * HID0]) for b in range(NB0)]
            down0s = [parts(scope, f"down0_{b}", [128, D]) for b in range(NB0)]
            a0 = [parts(scope, f"a0_{hf}", [128, HT]) for hf in range(2)]
        with phase() as scope:
            x1 = parts(scope, "x1", [C, 2, IMAGES * SLOT])
            up1s = [parts(scope, f"up1_{b}", [C, 2, HID1M]) for b in range(NB1)]
            down1s = [parts(scope, f"down1_{b}", [128, M1 * D]) for b in range(NB1)]
            hs = [parts(scope, f"hs_{r}", [128, HT]) for r in range(4)]
        in_phase(ctx, "phases", [128, 25624])

        moe = sb("moe", [128, 8844])

        def moe_part(lo, n):
            return moe[:, lo:lo + n]

        up0 = [moe_part(706 * b, 512)[0:C, :].rearrange("p (c n) -> p c n", c=2) for b in range(NB0)]
        down0 = [moe_part(706 * b + 512, D) for b in range(NB0)]
        bias0 = [moe_part(706 * b + 512 + D, 2) for b in range(NB0)]
        wb0 = [moe_part(706 * NB0 + T * b, T) for b in range(NB0)]
        at = (706 + T) * NB0
        s0, p0, f0 = ([moe_part(at + (3 * hf + i) * HT, HT) for hf in range(2)] for i in range(3))
        up1 = [moe_part(2694 * b, 1536)[0:C, :].rearrange("p (c n) -> p c n", c=2) for b in range(NB1)]
        down1 = [moe_part(2694 * b + 1536, M1 * D) for b in range(NB1)]
        bias1 = [moe_part(2694 * b + 1536 + M1 * D, M1) for b in range(NB1)]
        wb1 = [moe_part(2694 * NB1 + T * b, T) for b in range(NB1)]
        at = (2694 + T) * NB1
        hg, hp = ([moe_part(at + (4 * i + r) * HT, HT) for r in range(4)] for i in range(2))

        turns = 2 * M1 // 4

        def col96(name, c):
            return c96[:, COL96[name][0] + c:COL96[name][0] + c + 1]

        def col128(name, m):
            return c128[:, COL128[name][0] + m:COL128[name][0] + m + 1]

        def real(t, c, hf):
            rows = min(t.shape[0], 128) if t.shape[0] != 97 else C
            return t[0:rows, c, hf * HI * SLOT:(hf + 1) * HI * SLOT]\
                .rearrange("p (i t) -> p i t", t=SLOT)[:, :, 0:TOK]

        def pieces1(buf):
            up = [([t[:, c, :] for t in up1s[buf]], up1[buf][:, c, :]) for c in range(2)]
            return up + [([t[:, :] for t in down1s[buf]], down1[buf])]

        def by_image(x):
            return x.rearrange("p (i t) -> p i t", t=TOK)

        def half(hf):
            return slice(hf * HT, (hf + 1) * HT)

        def pad_half(hf):
            return slice(hf * HI * SLOT, (hf + 1) * HI * SLOT)

        def pairs(hf):
            return range(HP * hf, HP * hf + HP)

        def pair_cols(p):
            return slice(2 * SLOT * p, 2 * SLOT * (p + 1))

        def fill(pe, key):
            b, n = uses[key]
            if n:
                pe.wait_ge(bank_free[b], n)
            return bank[b]

        def full(ins, key):
            ins.then_inc(bank_full[uses[key][0]], 1)

        def read(eng, key):
            b, n = uses[key]
            eng.wait_ge(bank_full[b], n + 1)
            return bank[b]

        def free(ins, key):
            ins.then_inc(bank_free[uses[key][0]], 1)

        def await_read_out(eng, key):
            b, n = uses[key]
            eng.wait_ge(bank_free[b], n + 1)

        block = ctx.enter_context(nc.Block())

        @block.sync
        def _(sp):
            for i, (p, n) in enumerate(PATCH_LOADS):
                sp.dma_start(xp[:, p:p + n], a["patches"][p:p + n].rearrange("q p k t -> p q k t"))\
                  .then_inc(sem(f"patches{i}_loaded"), 16)
            for dst, name in ((ident[:, :], "ident"), (c96[:, :], "c96"), (mask_head[:, :], "mask_head"),
                              (wqkv0, "wqkv0"), (wproj0[:, :, :], "wproj0")):
                sp.dma_start(dst, a[name]).then_inc(sem("set0_loaded"), 16)
            for dst, name in ((gate0w[:, :, :], "gate0w"), (run[:, :], "run"), (route_bias[:, :], "route_bias"),
                              (bd0[:, :], "bd0")):
                sp.dma_start(dst, a[name]).then_inc(sem("set1_loaded"), 16)
            for x in range(NB0):
                sp.dma_start(up0[x], a["up0"][x]).then_inc(sem(f"expert0_loaded{x}"), 16)
                sp.dma_start(down0[x], a["down0"][x]).then_inc(sem(f"expert0_loaded{x}"), 16)
                sp.dma_start(bias0[x], a["bias0"][x]).then_inc(sem(f"bias0_loaded{x}"), 16)
            for dst, name in ((mask_pair[:, :], "mask_pair"), (basis[:, :], "basis"), (c128[:, :], "c128"),
                              (b2_row[:, :], "b2_row"), (wq1[:, :, :], "wq1"), (wk1[:, :, :], "wk1"),
                              (wv1[:, :, :], "wv1"), (wout1[:, :, :], "wout1"), (wposT[:, :], "wposT"),
                              (w1a[:, :, :], "w1a"), (w2a[:, :, :], "w2a")):
                sp.dma_start(dst, a[name]).then_inc(sem("set2_loaded"), 16)
            for dst, name in ((wqk2[:, :, :], "wqk2"), (wv2[:, :, :], "wv2"), (wout2[:, :, :], "wout2"),
                              (gate1w[:, :, :], "gate1w"), (b2m[:, :], "b2m"),
                              (first_row[:, :], "first_row")):
                sp.dma_start(dst, a[name]).then_inc(sem("set3_loaded"), 16)

            for hf in range(2):
                await_read_out(sp, ("wT0", hf))
            sp.dma_start(w0_d, wT[:, :]).then_inc(sem("w0_stored"), 16)
            sp.wait_ge(sem("w0_stored"), 16)
            for x in range(1, NB0):
                sp.dma_start(wb0[x], w0_d[x - 1].partition_broadcast(128)).then_inc(sem(f"w0_loaded{x}"), 16)

            def reload0(it, b):
                sp.wait_ge(sem("expert0_low"), it * NB0 + (b + 1))
                sp.dma_start(up0[b], a["up0"][it * NB0 + (NB0 + b)]).then_inc(sem(f"expert0_loaded{b}"), 16)
                sp.dma_start(down0[b], a["down0"][it * NB0 + (NB0 + b)]).then_inc(sem(f"expert0_loaded{b}"), 16)
                sp.wait_ge(sem("expert0_done"), it * NB0 + (b + 1))
                sp.dma_start(bias0[b], a["bias0"][it * NB0 + (NB0 + b)]).then_inc(sem(f"bias0_loaded{b}"), 16)
                sp.dma_start(wb0[b], w0_d[it * NB0 + (NB0 + b - 1)].partition_broadcast(128))\
                  .then_inc(sem(f"w0_loaded{b}"), 16)

            with sp.Fori(0, E0 // NB0 - 1) as it:
                for b in range(NB0):
                    reload0(it, b)
            reload0(E0 // NB0 - 1, 0)

            sp.wait_ge(sem("expert0_done"), E0 + 1)
            for b in range(NB1):
                sp.dma_start(up1[b], a["up1"][b]).then_inc(sem(f"expert1_loaded{b}"), 16)
                sp.dma_start(down1[b], a["down1"][b]).then_inc(sem(f"expert1_loaded{b}"), 16)
                sp.dma_start(bias1[b], a["bias1"][b]).then_inc(sem(f"bias1_loaded{b}"), 16)

            for hf in range(2):
                for p in pairs(hf):
                    for s in range(2):
                        await_read_out(sp, ("rel", p, s))
                sp.dma_start(rel_d[HP * hf:HP * hf + HP].rearrange("q p n -> p q n"), relb)\
                  .then_inc(sem("rel_stored"), 16)
                sp.wait_ge(sem("rel_stored"), 16 * (hf + 1))
                for par in range(2):
                    row = HB * REL
                    for p in pairs(hf):
                        at = (p * 128 + par * SLOT) * row + TOK - 1
                        skewed = bass.AP(tensor=rel_d.tensor, offset=at,
                                         ap=[[row - 1, TOK], [REL, HB], [1, TOK]])
                        sp.dma_start(rels[par * SLOT:par * SLOT + TOK, p], skewed)\
                          .then_inc(sem(f"rel_loaded{hf}"), 16)

            for hf in range(2):
                await_read_out(sp, ("wT1", hf))
            sp.dma_start(w1_d, wT[0:E1, :]).then_inc(sem("w1_stored"), 16)
            sp.wait_ge(sem("w1_stored"), 16)

            def load_row1(x, b, hf):
                sp.dma_start(wb1[b][:, half(hf)], w1_d[x, half(hf)].partition_broadcast(128))\
                  .then_inc(sem(f"w1_loaded{b}{hf}"), 16)

            for b in range(NB1):
                for hf in range(2):
                    if b or hf:
                        load_row1(b, b, hf)
            with sp.Fori(0, E1 // NB1 - 1) as it:
                for b in range(NB1):
                    sp.wait_ge(sem("expert1_low"), it * (3 * NB1) + 3 * (b + 1))
                    sp.dma_start(up1[b], a["up1"][it * NB1 + NB1 + b]).then_inc(sem(f"expert1_loaded{b}"), 16)
                    sp.dma_start(down1[b], a["down1"][it * NB1 + NB1 + b])\
                      .then_inc(sem(f"expert1_loaded{b}"), 16)
                    sp.wait_ge(sem("expert1_done"), it * NB1 + b + 1)
                    sp.dma_start(bias1[b], a["bias1"][it * NB1 + NB1 + b]).then_inc(sem(f"bias1_loaded{b}"), 16)
                    for hf in range(2):
                        load_row1(it * NB1 + NB1 + b, b, hf)
            result = out.rearrange("(q par) t d -> par t q d", par=2)
            for q in range(4):
                sp.wait_ge(sem("result_ready"), 2 * q + 2)
                for par in range(2):
                    sp.dma_start(result[par, :, 2 * q:2 * q + 2], h[par * SLOT:par * SLOT + TOK, 2 * q:2 * q + 2, :])\
                      .then_inc(sem("result_stored"), 16)
            sp.wait_ge(sem("result_stored"), 16 * 2 * 4)

        @block.gpsimd
        def _(pool):
            step = [0]

            def link(ins):
                step[0] += 1
                ins.then_inc(sem("pool_step"), 1)
                pool.wait_ge(sem("pool_step"), step[0])

            link(nc.gpsimd.memset(minus_half[:, :, :], -0.5))
            link(nc.gpsimd.memset(warm[:, :], 0.0))
            link(nc.gpsimd.memset(xT[C:C + 1, :, :], 1.0))
            link(nc.gpsimd.memset(oT[C:C + 1, :, :], 1.0))
            nc.gpsimd.memset(oT[0:C, :, :], 0.0).then_inc(sem("pool_init"), 1)
            pool.wait_ge(sem("pool_init"), 1)
            nc.gpsimd.memset(part(RS, PAIRS * HB * TOK + AHEAD * HF * SLOT), 0.0).then_inc(sem("pads_zeroed"), 1)
            pool.wait_ge(sem("pads_zeroed"), 1)

            def rstd(n, hf, kind):
                sl = slice(HP * hf, HP * hf + HP)
                mean, var = mv[:, sl, 0], mv[:, sl, 1]
                pool.wait_ge(sem("stats_done"), 2 * n + hf + 1)
                if kind == "rms":
                    link(nc.gpsimd.tensor_tensor(pw_in[:, 0, sl], mean, mean, ALU.mult))
                    link(nc.gpsimd.tensor_tensor(pw_in[:, 0, sl], pw_in[:, 0, sl], var, ALU.add))
                    link(nc.gpsimd.tensor_scalar(pw_in[:, 0, sl], pw_in[:, 0, sl], EPS, None, ALU.add))
                else:
                    link(nc.gpsimd.tensor_scalar(pw_in[:, 0, sl], var, EPS, None, ALU.add))
                k = 1
                if kind == "ln+norm":
                    link(nc.gpsimd.tensor_scalar(pw_in[:, 1, sl], var, 1.0 + EPS, EPS * EPS, ALU.mult, ALU.add))
                    k = 2
                nc.gpsimd.tensor_tensor(pw_out[:, 0:k, sl], pw_in[:, 0:k, sl], minus_half[:, 0:k, sl], ALU.pow)\
                    .then_inc(sem("rstd_done"), 1)

            def low(dst, src):
                return nc.gpsimd.tensor_tensor(dst[1], src, dst[0].bitcast(F32), ALU.subtract)

            def low_inputs(n, x):
                for hf in range(2):
                    pool.wait_ge(sem(f"x_high{n}"), hf + 1)
                    low([t[:, :, pad_half(hf)] for t in x], xT[0:C, :, pad_half(hf)])\
                        .then_inc(sem(f"x_low{n}"), 1)

            def low0(x, buf):
                pool.wait_ge(sem("expert0_high"), x + 1)
                low([t[:, :, :] for t in up0s[buf]], up0[buf])
                low([t[:, :] for t in down0s[buf]], down0[buf]).then_inc(sem("expert0_low"), 1)

            def low1(x, buf, piece):
                pool.wait_ge(sem("expert1_high"), 3 * x + (piece + 1))
                dst, src = pieces1(buf)[piece]
                low(dst, src).then_inc(sem("expert1_low"), 1)

            for hf in range(2):
                rstd(0, hf, "ln")
            low0(0, 0)
            for hf in range(2):
                for c in range(2):
                    await_read_out(pool, ("o0", hf, c))
            nc.gpsimd.memset(part(QU, 4096), 0.0).then_inc(sem("pads_zeroed"), 1)
            pool.wait_ge(sem("pads_zeroed"), 2)
            for hf in range(2):
                rstd(1, hf, "ln")
            low_inputs(1, x0)
            nc.gpsimd.memset(part(QV, 4096), 0.0).then_inc(sem("pads_zeroed"), 1)
            pool.wait_ge(sem("pads_zeroed"), 3)
            with pool.Fori(0, E0 // NB0) as it:
                for j in range(NB0):
                    low0(it * NB0 + (j + 1), (j + 1) % NB0)
            def skips(hf):
                for p in pairs(hf):
                    last = nc.gpsimd.tensor_scalar(u[:, p, :], h[:, p, :], mv[:, p, 0:1], pw_out[:, 0, p:p + 1],
                                                   ALU.subtract, ALU.mult)
                last.then_inc(sem("skip_ready"), 1)

            for hf in range(2):
                rstd(2, hf, "ln+norm")
            for hf in range(2):
                pool.wait_ge(sem("rstd_done"), 2 * 2 + hf + 1)
                skips(hf)
            pool.wait_ge(sem("set2_loaded"), 16 * 11)
            for hf in range(2):
                rstd(3, hf, "rms")
                sl = slice(HP * hf, HP * hf + HP)
                link(nc.gpsimd.tensor_tensor(h[:, sl, :], h[:, sl, :], u[:, sl, :], ALU.add))
                nc.gpsimd.tensor_tensor(h[:, sl, :], h[:, sl, :],
                                        b2_row[:, :].unsqueeze(1).broadcast_to([128, HP, D]), ALU.add)\
                    .then_inc(sem("skip1_added"), 1)
            for hf in range(2):
                rstd(4, hf, "ln+norm")
            for hf in range(2):
                pool.wait_ge(sem("rstd_done"), 2 * 4 + hf + 1)
                skips(hf)
            for hf in range(2):
                await_read_out(pool, ("k2", hf, 0))
                imgs = slice(HI * hf, HI * hf + HI)
                nc.gpsimd.tensor_tensor(
                    kbd2[:, 0, imgs], by_image(k2[:, 0, half(hf)]).unsqueeze(2).broadcast_to([C, HI, 6, TOK]),
                    mask_head[:, :].unsqueeze(1).unsqueeze(3).broadcast_to([C, HI, 6, TOK]), ALU.mult)\
                    .then_inc(sem("keys2_masked_pool"), 1)
            for piece in range(2):
                low1(0, 0, piece)
            for hf in range(2):
                rstd(5, hf, "ln")
            low_inputs(5, x1)
            low1(0, 0, 2)
            nc.gpsimd.tensor_tensor(h[:, :, :], h[:, :, :], u[:, :, :], ALU.add).then_inc(sem("skip2_added"), 1)
            with pool.Fori(0, E1 // NB1 - 1) as it:
                for j in range(NB1):
                    for piece in range(3):
                        low1(it * NB1 + (j + 1), (j + 1) % NB1, piece)
            for piece in range(3):
                low1(E1 - 1, NB1 - 1, piece)

        @block.tensor
        def _(pe):
            mm = nc.tensor.matmul

            def transposes(n, hf):
                pe.wait_ge(sem("xn_done"), 2 * n + hf + 1)
                for c in range(2):
                    b = fill(pe, (f"n{n}", hf, c))
                    for q, p in enumerate(pairs(hf)):
                        last = nc.tensor.transpose(b[0:C, q * 128:(q + 1) * 128], xn[:, p, c * C:(c + 1) * C],
                                                   ident[:, :])
                    full(last, (f"n{n}", hf, c))

            def await_xT(n, hf):
                for c in range(2):
                    await_read_out(pe, (f"n{n}", hf, c))

            def feature_major(key, w, c0, width, src, hf):
                b = fill(pe, key)
                o = by_image(b[0:width, 0:HT])
                for kc in range(2):
                    last = mm(o, w[0:C, kc, c0:c0 + width], real(src, kc, hf), start=kc == 0, stop=kc == 1)
                full(last, key)

            def token_major(key, src, w, p, biased):
                b = fill(pe, key)
                n = w.shape[2]
                for kc in range(2):
                    rows = C + (1 if kc and biased else 0)
                    last = mm(b[:, 0:n], src[0:rows, kc, pair_cols(p)], w[0:rows, kc, :],
                              start=kc == 0, stop=kc == 1)
                full(last, key)

            def embed(p):
                for i, (first, _) in enumerate(PATCH_LOADS):
                    if p == first:
                        pe.wait_ge(sem(f"patches{i}_loaded"), 16)
                b = fill(pe, ("tok", p))
                for k in range(PATCH_CHUNKS):
                    last = mm(b[:, 0:D], xp[:, p, k, :], tokw[:, k, :], start=k == 0, stop=k == PATCH_CHUNKS - 1)
                full(last, ("tok", p))

            def queries_keys_values0(hf):
                await_xT(0, hf)
                for c in range(2):
                    feature_major(("q0", hf, c), wqkv0, c * C, C, xT, hf)
                for p in pairs(hf):
                    token_major(("kv0", p), xT, wqkv0[:, :, D:3 * D], p, False)

            def keys_by_values0(hf):
                for p in pairs(hf):
                    await_read_out(pe, ("kv0", p))
                for pp in range(2):
                    for par in range(2):
                        key = ("kTv", hf, pp, par)
                        b = fill(pe, key)
                        rows = slice(par * SLOT, par * SLOT + TOK)
                        for q in range(2):
                            for c in range(2):
                                p = HP * hf + 2 * pp + q
                                at = (2 * q + c) * C
                                last = mm(b[0:C, at:at + C], kv[rows, p, c * C:(c + 1) * C],
                                          kv[rows, p, D + c * C:D + (c + 1) * C], start=True, stop=True)
                        full(last, key)

            def attend0(hf):
                pe.wait_ge(sem("kv_masked"), 4 * (hf + 1))
                for c in range(2):
                    await_read_out(pe, ("q0", hf, c))
                    b = fill(pe, ("o0", hf, c))
                    for i in range(HI):
                        at = hf * HT + i * TOK
                        last = mm(b[0:C, i * TOK:(i + 1) * TOK], gkv[:, HI * hf + i, c, :], gq[:, c, at:at + TOK],
                                  start=True, stop=True)
                    full(last, ("o0", hf, c))

            def project(attended, wo, w, hf):
                for c in range(2):
                    await_read_out(pe, (attended, hf, c))
                for p in pairs(hf):
                    token_major((wo, p), oT, w, p, True)

            pe.wait_ge(sem("tok_w_loaded"), 16)
            for p in range(HP + 2):
                embed(p)
            pe.wait_ge(sem("set0_loaded"), 16 * 5)
            pe.wait_ge(sem("pool_init"), 1)
            transposes(0, 0)
            for p in range(HP + 2, PAIRS):
                embed(p)
            queries_keys_values0(0)
            transposes(0, 1)
            keys_by_values0(0)
            queries_keys_values0(1)
            attend0(0)
            keys_by_values0(1)
            project("o0", "proj0", wproj0, 0)
            attend0(1)
            project("o0", "proj0", wproj0, 1)

            pe.wait_ge(sem("set1_loaded"), 16 * 4)
            for hf in range(2):
                transposes(1, hf)
                await_xT(1, hf)
                key = ("gate0", hf)
                b = fill(pe, key)
                for q, p in enumerate(pairs(hf)):
                    for kc in range(2):
                        rows = C + kc
                        last = mm(b[:, q * E0:(q + 1) * E0], xT[0:rows, kc, pair_cols(p)], gate0w[0:rows, kc, :],
                                  start=kc == 0, stop=kc == 1)
                full(last, key)

            def split_mm(o, w, x, start, stop):
                mm(o, w[0], x[0], start=start, stop=False, skip_group_check=True)
                mm(o, w[0], x[1], start=False, stop=False, skip_group_check=True)
                return mm(o, w[1], x[0], start=False, stop=stop, skip_group_check=True)

            y = {(hf, c): bank[2 * hf + c][0:C, 0:HT] for hf in range(2) for c in range(2)}

            def hidden0(x, buf, hf):
                for name in "ug":
                    b, n = uses[name, hf]
                    pe.wait_ge(bank_free[b], x + n)
                for name, at in (("u", 0), ("g", HID0)):
                    b, n = uses[name, hf]
                    o = by_image(bank[b][:, 0:HT])
                    for kc in range(2):
                        last = split_mm(o, [t[:, kc, at:at + HID0] for t in up0s[buf]],
                                        [real(t, kc, hf) for t in x0], start=kc == 0, stop=kc == 1)
                    last.then_inc(bank_full[b], 1)

            def sums0(x, buf, hf):
                pe.wait_ge(sem(f"act0_ready{hf}"), x * 3 + 2)
                for c in range(2):
                    last = split_mm(y[hf, c], [t[:, c * C:(c + 1) * C] for t in down0s[buf]],
                                    [t[:, :] for t in a0[hf]], start=False, stop=False)
                return last

            pe.wait_ge(sem("x_low1"), 2)
            pe.wait_ge(sem("expert0_low"), 1)
            hidden0(0, 0, 0)
            hidden0(0, 0, 1)
            pe.wait_ge(sem("routed"), 1)
            for hf in range(2):
                b = fill(pe, ("wT0", hf))
                for q in range(HP):
                    at = (HP * hf + q) * E0
                    last = nc.tensor.transpose(b[0:E0, q * 128:(q + 1) * 128], rt0["w"][:, at:at + E0], ident[:, :])
                full(last, ("wT0", hf))
            for hf in range(2):
                await_read_out(pe, ("wT0", hf))
            for hf in range(2):
                for c in range(2):
                    fill(pe, ("y0", hf, c))
                    full(mm(y[hf, c], bd0[:, c * C:(c + 1) * C], wT[0:E0, half(hf)], start=True, stop=False,
                            skip_group_check=True), ("y0", hf, c))
            sums0(0, 0, 0)
            with pe.Fori(0, E0 // NB0) as it:
                for j in range(NB0):
                    x, buf = it * NB0 + (j + 1), (j + 1) % NB0
                    pe.wait_ge(sem("expert0_low"), x + 1)
                    hidden0(x, buf, 0)
                    sums0(it * NB0 + j, j, 1).then_inc(sem("expert0_done"), 1)
                    hidden0(x, buf, 1)
                    sums0(x, buf, 0).then_inc(sem("sums0_done"), 1)
            sums0(E0, E0 % NB0, 1).then_inc(sem("expert0_done"), 1)

            def sums_token_major(tag):
                for p in range(PAIRS):
                    if p % HP == 0:
                        for c in range(2):
                            await_read_out(pe, (tag, p // HP, c))
                    b = fill(pe, (tag + "t", p))
                    for c in range(2):
                        last = nc.tensor.transpose(b[:, c * C:(c + 1) * C], oT[0:C, c, pair_cols(p)],
                                                   ident[0:C, 0:C])
                    full(last, (tag + "t", p))

            sums_token_major("y0")

            pe.wait_ge(sem("set2_loaded"), 16 * 11)
            for m in range(4):
                b = fill(pe, ("rel_w", m))
                full(mm(b[:, 0:REL], wposT[:, m * 128:(m + 1) * 128], basis[:, :], start=True, stop=True),
                     ("rel_w", m))
            for hf in range(2):
                transposes(2, hf)
            for hf in range(2):
                await_xT(2, hf)
                for m in range(4):
                    feature_major(("q1", hf, m), wq1, m * 128, 128, xT, hf)
                for m in range(4):
                    feature_major(("k1", hf, m), wk1, m * 128, 128, xT, hf)
                for m in range(4):
                    await_read_out(pe, ("rel_w", m))
                    await_read_out(pe, ("q1", hf, m))
                for p in pairs(hf):
                    for s in range(2):
                        b = fill(pe, ("rel", p, s))
                        for m in (2 * s, 2 * s + 1):
                            at = (m % 2) * 2 * REL
                            last = mm(b[:, at:at + 2 * REL], qv[:, m, pair_cols(p)],
                                      rbd[:, m].rearrange("p e r -> p (e r)"), start=True, stop=True)
                        full(last, ("rel", p, s))
                for q in range(2):
                    key = ("v1", hf, q)
                    b = fill(pe, key)
                    for i in range(4):
                        img = HI * hf + 4 * q + i
                        for par in range(2):
                            for kc in range(2):
                                last = mm(b[par * SLOT:(par + 1) * SLOT, i * C:(i + 1) * C],
                                          xT[0:C, kc, img * SLOT:(img + 1) * SLOT],
                                          wv1[:, kc, par * C:(par + 1) * C], start=kc == 0, stop=kc == 1,
                                          skip_group_check=True)
                    full(last, key)

            def scores1(p):
                if p % HP == 0:
                    for m in range(4):
                        await_read_out(pe, ("k1", p // HP, m))
                b = fill(pe, ("s1", p))
                for m in range(4):
                    for par in range(2):
                        img = 2 * p + par
                        last = mm(b[par * SLOT:(par + 1) * SLOT, m * 2 * TOK:(m + 1) * 2 * TOK],
                                  qu[:, m, img * SLOT:(img + 1) * SLOT],
                                  kbd1[:, m, img].rearrange("p e j -> p (e j)"), start=True, stop=True,
                                  skip_group_check=True)
                full(last, ("s1", p))

            for p in range(AHEAD):
                scores1(p)
            def attended_columns(tag, av, hf):
                for p in pairs(hf):
                    await_read_out(pe, (av, p))
                for c in range(2):
                    b = fill(pe, (tag, hf, c))
                    for q, p in enumerate(pairs(hf)):
                        last = nc.tensor.transpose(b[0:C, q * 128:(q + 1) * 128], xn[:, p, c * C:(c + 1) * C],
                                                   ident[:, :])
                    full(last, (tag, hf, c))

            def attend1(p):
                await_read_out(pe, ("p1t", p))
                if p % 2 == 0:
                    await_read_out(pe, ("v1", p // HP, (p % HP) // 2))
                b = fill(pe, ("av1", p))
                for m in range(4):
                    for par in range(2):
                        img = 2 * p + par
                        last = mm(b[par * SLOT:(par + 1) * SLOT, m * 2 * HBV:(m + 1) * 2 * HBV],
                                  pt1[:, p % 2, m * 128 + par * SLOT:m * 128 + (par + 1) * SLOT],
                                  vbd1[:, img * 4 + m].rearrange("p e d -> p (e d)"), start=True, stop=True,
                                  skip_group_check=True)
                full(last, ("av1", p))

            for p in range(PAIRS):
                pe.wait_ge(sem("exp1_done"), p + 1)
                b = fill(pe, ("p1t", p))
                for m in range(4):
                    last = nc.tensor.transpose(b[:, m * 128:(m + 1) * 128],
                                               probs1[:, p % AHEAD, 2 * m:2 * m + 2].rearrange("p h j -> p (h j)"),
                                               ident[:, :])
                full(last, ("p1t", p))
                if p + AHEAD < PAIRS:
                    scores1(p + AHEAD)
                if p:
                    attend1(p - 1)
                if p == HP + 1:
                    attended_columns("o1t", "av1", 0)
                if p == HP + 2:
                    project("o1t", "wo1", wout1, 0)
            attend1(PAIRS - 1)
            attended_columns("o1t", "av1", 1)
            project("o1t", "wo1", wout1, 1)

            def ffn_hidden(hf):
                await_xT(3, hf)
                for m in range(3):
                    feature_major(("f1", hf, m), w1a, m * 128, 128, xT, hf)

            def ffn_out(hf):
                for m in range(3):
                    await_read_out(pe, ("f1", hf, m))
                for p in pairs(hf):
                    b = fill(pe, ("f2", p))
                    for m in range(3):
                        last = mm(b[:, 0:D], g1[:, m, pair_cols(p)], w2a[:, m, :], start=m == 0, stop=m == 2)
                    full(last, ("f2", p))

            transposes(3, 0)
            ffn_hidden(0)
            transposes(3, 1)
            ffn_out(0)
            ffn_hidden(1)
            transposes(4, 0)
            ffn_out(1)
            pe.wait_ge(sem("set3_loaded"), 16 * 6)
            for hf in range(2):
                await_xT(4, hf)
                for c in range(2):
                    feature_major(("q2", hf, c), wqk2, c * C, C, xT, hf)
                for c in range(2):
                    feature_major(("k2", hf, c), wqk2, D + c * C, C, xT, hf)
                if hf == 0:
                    transposes(4, 1)
                for q in range(2):
                    key = ("v2", hf, q)
                    b = fill(pe, key)
                    for i in range(4):
                        img = HI * hf + 4 * q + i
                        for par in range(2):
                            for kc in range(2):
                                rows = C + kc
                                last = mm(b[par * SLOT:(par + 1) * SLOT, i * C:(i + 1) * C],
                                          xT[0:rows, kc, img * SLOT:(img + 1) * SLOT],
                                          wv2[0:rows, kc, par * C:(par + 1) * C], start=kc == 0, stop=kc == 1,
                                          skip_group_check=True)
                    full(last, key)

            def scores2(p):
                if p % HP == 0:
                    for c in range(2):
                        await_read_out(pe, ("q2", p // HP, c))
                    pe.wait_ge(sem("keys2_masked_pool"), p // HP + 1)
                    pe.wait_ge(sem("keys2_masked_dve"), p // HP + 1)
                b = fill(pe, ("s2", p))
                for c in range(2):
                    for par in range(2):
                        img = 2 * p + par
                        last = mm(b[par * SLOT:(par + 1) * SLOT, c * 6 * TOK:(c + 1) * 6 * TOK],
                                  q2[:, c, img * SLOT:(img + 1) * SLOT],
                                  kbd2[:, c, img].rearrange("p e j -> p (e j)"), start=True, stop=True,
                                  skip_group_check=True)
                full(last, ("s2", p))

            for p in range(AHEAD):
                scores2(p)
            def attend2(p):
                for s in range(2):
                    await_read_out(pe, ("p2t", p, s))
                if p % 2 == 0:
                    await_read_out(pe, ("v2", p // HP, (p % HP) // 2))
                b = fill(pe, ("av2", p))
                for m in range(6):
                    for par in range(2):
                        img = 2 * p + par
                        last = mm(b[par * SLOT:(par + 1) * SLOT, m * 2 * HFD:(m + 1) * 2 * HFD],
                                  pt2[:, p % 2, m * 128 + par * SLOT:m * 128 + (par + 1) * SLOT],
                                  vbd2[:, img * 6 + m].rearrange("p e d -> p (e d)"), start=True, stop=True,
                                  skip_group_check=True)
                full(last, ("av2", p))

            for p in range(PAIRS):
                pe.wait_ge(sem("exp2_done"), p + 1)
                for s in range(2):
                    b = fill(pe, ("p2t", p, s))
                    for m in range(3):
                        h0 = 2 * (3 * s + m)
                        last = nc.tensor.transpose(b[:, m * 128:(m + 1) * 128],
                                                   probs2[:, p % AHEAD, h0:h0 + 2].rearrange("p h j -> p (h j)"),
                                                   ident[:, :])
                    full(last, ("p2t", p, s))
                if p + AHEAD < PAIRS:
                    scores2(p + AHEAD)
                if p:
                    attend2(p - 1)
                if p == HP + 1:
                    attended_columns("o2t", "av2", 0)
                if p == HP + 2:
                    project("o2t", "wo2", wout2, 0)
            attend2(PAIRS - 1)
            attended_columns("o2t", "av2", 1)
            project("o2t", "wo2", wout2, 1)

            for hf in range(2):
                transposes(5, hf)
                await_xT(5, hf)
                key = ("gate1", hf)
                b = fill(pe, key)
                for q, p in enumerate(pairs(hf)):
                    for kc in range(2):
                        last = mm(b[:, q * E1:(q + 1) * E1], xT[0:C, kc, pair_cols(p)], gate1w[:, kc, :],
                                  start=kc == 0, stop=kc == 1)
                full(last, key)

            def hidden1(it, buf, n):
                b, base = uses["hid", n % 4]
                m, hf = n % M1, n // M1
                pe.wait_ge(bank_free[b], it * (NB1 * turns) + (base + buf * turns + n // 4))
                o = by_image(bank[b][:, 0:HT])
                for kc in range(2):
                    last = split_mm(o, [t[:, kc, m * 128:(m + 1) * 128] for t in up1s[buf]],
                                    [real(t, kc, hf) for t in x1], start=kc == 0, stop=kc == 1)
                last.then_inc(bank_full[b], 1)

            def sums1(it, buf, n):
                m, hf = n % M1, n // M1
                pe.wait_ge(sem("hid1_ready"), it * (3 * NB1 * 2 * M1) + 3 * (buf * 2 * M1 + n + 1))
                for c in range(2):
                    at = m * D + c * C
                    last = split_mm(y[hf, c], [t[:, at:at + C] for t in down1s[buf]],
                                    [t[:, :] for t in hs[n % 4]], start=False, stop=False)
                if n == M1 - 1:
                    last.then_inc(sem("sums1_done"), 1)
                if n == 2 * M1 - 1:
                    last.then_inc(sem("expert1_done"), 1)

            def expert1(it, buf, next_it):
                for n in range(2 * M1):
                    ahead = n + 3
                    if ahead < 2 * M1:
                        hidden1(it, buf, ahead)
                    elif next_it is not None:
                        nxt = (buf + 1) % NB1
                        if ahead == 2 * M1:
                            pe.wait_ge(sem("expert1_low"), it * (3 * NB1) + 3 * (buf + 2))
                        hidden1(next_it, nxt, ahead - 2 * M1)
                    sums1(it, buf, n)

            pe.wait_ge(sem("x_low5"), 1)
            pe.wait_ge(sem("expert1_low"), 2)
            for n in range(3):
                hidden1(0, 0, n)
            pe.wait_ge(sem("x_low5"), 2)
            pe.wait_ge(sem("routed"), 2)
            for hf in range(2):
                b = fill(pe, ("wT1", hf))
                for q in range(HP):
                    at = (HP * hf + q) * E1
                    last = nc.tensor.transpose(b[0:E1, q * 128:(q + 1) * 128], rt1["w"][:, at:at + E1], ident[:, :])
                full(last, ("wT1", hf))
            for hf in range(2):
                await_read_out(pe, ("wT1", hf))
            b = fill(pe, "first_row1")
            full(mm(b[:, 0:HT], first_row[:, :], wT[0:E1, half(0)], start=True, stop=True), "first_row1")
            for hf in range(2):
                for c in range(2):
                    fill(pe, ("y1", hf, c))
                    full(mm(y[hf, c], b2m[:, c * C:(c + 1) * C], wT[0:E1, half(hf)], start=True, stop=False,
                            skip_group_check=True), ("y1", hf, c))
            pe.wait_ge(sem("expert1_low"), 3)
            with pe.Fori(0, E1 // NB1 - 1) as it:
                expert1(it, 0, it)
                expert1(it, 1, it + 1)
            expert1(E1 // NB1 - 1, 0, E1 // NB1 - 1)
            expert1(E1 // NB1 - 1, 1, None)
            sums_token_major("y1")

        @block.scalar
        def _(act):
            activation = nc.scalar.activation
            act.dma_start(tokw, a["tok_w"]).then_inc(sem("tok_w_loaded"), 16)

            def columns(n, hf, scale=None, bias=None):
                key = (f"n{n}", hf, 0)
                b = read(act, key)
                free(activation(xT[0:C, 0, pad_half(hf)], b[0:C, :], ACT.Identity,
                                scale=col96(scale, 0) if scale else 1.0,
                                bias=col96(bias, 0) if bias else 0.0), key)

            def embedded(p):
                b = read(act, ("tok", p))
                free(activation(h[:, p, :], b[:, 0:D], ACT.Copy), ("tok", p))

            def queries_keys_values0(hf):
                for c in range(2):
                    b = read(act, ("q0", hf, c))
                    free(activation(gq[:, c, half(hf)], b[0:C, 0:HT], ACT.Gelu), ("q0", hf, c))
                for p in pairs(hf):
                    if p % 2:
                        b = read(act, ("kv0", p))
                        free(activation(kv[:, p, :], b[:, 0:2 * D], ACT.Copy), ("kv0", p))

            def keys_by_values0(hf):
                for pp in range(2):
                    for par in range(2):
                        key = ("kTv", hf, pp, par)
                        b = read(act, key)
                        img = HI * hf + 4 * pp + par
                        free(activation(gkr[:, img:img + 3:2], b[0:C, 0:4 * C].rearrange(
                            "p (q c e) -> p q c e", q=2, c=2), ACT.Gelu, scale=float(HFD) ** -0.5), key)

            for p in range(HP + 2):
                embedded(p)
            act.wait_ge(sem("set0_loaded"), 16 * 5)
            act.wait_ge(sem("pool_init"), 1)
            columns(0, 0)
            for p in range(HP + 2, PAIRS):
                embedded(p)
            queries_keys_values0(0)
            columns(0, 1)
            keys_by_values0(0)
            queries_keys_values0(1)
            keys_by_values0(1)

            def high_inputs(n, hf, x):
                for c in range(2):
                    await_read_out(act, (f"n{n}", hf, c))
                activation(x[0][:, :, pad_half(hf)], xT[0:C, :, pad_half(hf)], ACT.Copy)\
                    .then_inc(sem(f"x_high{n}"), 1)

            def high0(x, buf, loads):
                act.wait_ge(sem(f"expert0_loaded{buf}"), loads)
                activation(up0s[buf][0][:, :, :], up0[buf], ACT.Copy)
                activation(down0s[buf][0][:, :], down0[buf], ACT.Copy).then_inc(sem("expert0_high"), 1)

            def silu(x, buf, hf):
                b, n = uses["u", hf]
                act.wait_ge(bank_full[b], x + (n + 1))
                activation(s0[hf], bank[b][:, 0:HT], ACT.Silu, bias=bias0[buf][:, 0:1])\
                    .then_inc(bank_free[b], 1)

            high0(0, 0, 32)
            act.wait_ge(sem("pool_init"), 1)
            for hf in range(2):
                columns(1, hf)
            for hf in range(2):
                high_inputs(1, hf, x0)
                await_read_out(act, ("gate0", hf))
                at = slice(hf * HP * E0, (hf + 1) * HP * E0)
                activation(rt0["e"][:, at], rt0["s"][:, at], ACT.Exp).then_inc(sem("route_exp"), 1)
            for hf in range(2):
                b = read(act, ("wT0", hf))
                free(activation(by_image(wT[0:E0, half(hf)]), b[0:E0, :].rearrange(
                    "p (i t) -> p i t", t=SLOT)[:, :, 0:TOK], ACT.Copy), ("wT0", hf))
            high0(1, 1, 32)

            def expert0(it, j, prepare):
                act.wait_ge(sem(f"bias0_loaded{j}"), it * 16 + 16)
                silu(it * NB0 + j, j, 0)
                if prepare:
                    high0(it * NB0 + (j + 2), (j + 2) % NB0, it * 32 + 32 * (2 if j + 2 >= NB0 else 1))
                silu(it * NB0 + j, j, 1)

            with act.Fori(0, E0 // NB0 - 1) as it:
                activation(warm[:, :], warm[:, :], ACT.Silu)
                for j in range(NB0):
                    expert0(it, j, True)
            for j in range(NB0):
                expert0(E0 // NB0 - 1, j, j + 2 <= NB0)
            expert0(E0 // NB0, 0, False)
            for hf in range(2):
                act.wait_ge(sem("expert0_done" if hf else "sums0_done"), E0 + hf)
                for c in range(2):
                    b = read(act, ("y0", hf, c))
                    free(activation(real(oT, c, hf), by_image(b[0:C, 0:HT]), ACT.Identity,
                                    bias=col96("sbd", c)), ("y0", hf, c))

            act.wait_ge(sem("set2_loaded"), 16 * 11)
            for hf in range(2):
                columns(2, hf, "rms1_w")
            act.wait_ge(sem("pads_zeroed"), 3)
            for hf in range(2):
                for m in range(4):
                    b = read(act, ("q1", hf, m))
                    activation(real(qu, m, hf), by_image(b[:, 0:HT]), ACT.Identity, bias=col128("u", m))
                    free(activation(real(qv, m, hf), by_image(b[:, 0:HT]), ACT.Identity, bias=col128("v", m)),
                         ("q1", hf, m))
                if hf:
                    act.wait_ge(sem("rel_stored"), 16)
                for q, p in enumerate(pairs(hf)):
                    for s in range(2):
                        b = read(act, ("rel", p, s))
                        free(activation(relb[:, q, s * 4 * REL:(s + 1) * 4 * REL], b[:, 0:4 * REL], ACT.Copy),
                             ("rel", p, s))

            def softmax_exp1(p):
                act.wait_ge(sem("shifted1"), p + 1)
                x = probs1[:, p % AHEAD, :, 0:TOK]
                activation(x, x, ACT.Exp, scale=float(HD) ** -0.5).then_inc(sem("exp1_done"), 1)

            def attended(tag, hf):
                b = read(act, (tag, hf, 0))
                free(activation(oT[0:C, 0, pad_half(hf)], b[0:C, :], ACT.Copy), (tag, hf, 0))

            softmax_exp1(0)
            for p in range(PAIRS):
                if p + 1 < PAIRS:
                    softmax_exp1(p + 1)
                b = read(act, ("p1t", p))
                free(activation(pt1[:, p % 2, :], b[:, :], ACT.Copy), ("p1t", p))
                if p == HP + 1:
                    attended("o1t", 0)
            attended("o1t", 1)

            def ffn_hidden(hf):
                for m in range(3):
                    b = read(act, ("f1", hf, m))
                    free(activation(real(g1, m, hf), by_image(b[:, 0:HT]), ACT.Gelu, bias=col128("b1", m)),
                         ("f1", hf, m))

            columns(3, 0, "rms2_w")
            ffn_hidden(0)
            columns(3, 1, "rms2_w")
            ffn_hidden(1)
            columns(4, 0, "ln1_w", "ln1_b")
            for hf in range(2):
                for c in range(2):
                    b = read(act, ("q2", hf, c))
                    free(activation(real(q2, c, hf), by_image(b[0:C, 0:HT]), ACT.Identity, bias=col96("q_b", c)),
                         ("q2", hf, c))
                for c in range(2):
                    b = read(act, ("k2", hf, c))
                    free(activation(k2[:, c, half(hf)], b[0:C, 0:HT], ACT.Identity, bias=col96("k_b", c)),
                         ("k2", hf, c))
                if hf == 0:
                    columns(4, 1, "ln1_w", "ln1_b")

            def softmax_exp2(p):
                await_read_out(act, ("s2", p))
                x = probs2[:, p % AHEAD, :, 0:TOK]
                activation(x, x, ACT.Exp, scale=float(HFD) ** -0.5).then_inc(sem("exp2_done"), 1)

            def high1(x, buf, piece):
                dst, src = pieces1(buf)[piece]
                activation(dst[0], src, ACT.Copy).then_inc(sem("expert1_high"), 1)

            softmax_exp2(0)
            for p in range(PAIRS):
                if p + 1 < PAIRS:
                    softmax_exp2(p + 1)
                for s in range(2):
                    b = read(act, ("p2t", p, s))
                    free(activation(pt2[:, p % 2, s * 384:(s + 1) * 384], b[:, 0:384], ACT.Copy), ("p2t", p, s))
                if p == HP + 1:
                    attended("o2t", 0)
                if p == HP + 2:
                    act.wait_ge(sem("expert1_loaded0"), 32)
                    for piece in range(2):
                        high1(0, 0, piece)
            attended("o2t", 1)
            high1(0, 0, 2)
            for hf in range(2):
                columns(5, hf, "ln2_w", "ln2_b")

            for hf in range(2):
                high_inputs(5, hf, x1)
                await_read_out(act, ("gate1", hf))
                at = slice(hf * HP * E1, (hf + 1) * HP * E1)
                activation(rt1["e"][:, at], rt1["s"][:, at], ACT.Exp).then_inc(sem("route_exp"), 1)
            act.wait_ge(sem("w0_stored"), 16)
            for hf in range(2):
                b = read(act, ("wT1", hf))
                free(activation(by_image(wT[0:E1, half(hf)]), b[0:E1, :].rearrange(
                    "p (i t) -> p i t", t=SLOT)[:, :, 0:TOK], ACT.Copy), ("wT1", hf))

            def expert1(it, buf, prepare_next):
                act.wait_ge(sem(f"bias1_loaded{buf}"), it * 16 + 16)
                for n in range(2 * M1):
                    b, base = uses["hid", n % 4]
                    m = n % M1
                    act.wait_ge(bank_full[b], it * (NB1 * turns) + (base + buf * turns + n // 4 + 1))
                    activation(hg[n % 4], bank[b][:, 0:HT], ACT.Gelu, bias=bias1[buf][:, m:m + 1])\
                        .then_inc(bank_free[b], 1)
                    if prepare_next and n in (3, 5, 7):
                        nxt = (buf + 1) % NB1
                        if n == 3:
                            act.wait_ge(sem(f"expert1_loaded{nxt}"), it * 32 + (32 if nxt else 64))
                        high1(it * NB1 + (buf + 1), nxt, (n - 3) // 2)

            with act.Fori(0, E1 // NB1 - 1) as it:
                for buf in range(NB1):
                    expert1(it, buf, True)
            for buf in range(NB1):
                expert1(E1 // NB1 - 1, buf, buf < NB1 - 1)
            for hf in range(2):
                act.wait_ge(sem("expert1_done" if hf else "sums1_done"), E1)
                for c in range(2):
                    b = read(act, ("y1", hf, c))
                    free(activation(real(oT, c, hf), by_image(b[0:C, 0:HT]), ACT.Copy), ("y1", hf, c))

        @block.vector
        def _(dve):
            tt, ts, stt, reduce = (nc.vector.tensor_tensor, nc.vector.tensor_scalar,
                                   nc.vector.scalar_tensor_tensor, nc.vector.tensor_reduce)
            step = [0]

            def link(ins):
                step[0] += 1
                ins.then_inc(sem("dve_step"), 1)
                dve.wait_ge(sem("dve_step"), step[0])

            bn = [0]

            def statistics(x, hf, tag=None):
                first = HP * hf
                for i in range(HP + 2):
                    if tag and i < HP:
                        p = first + i
                        b = read(dve, (tag, p))
                        free(tt(x[:, p, :], b[:, 0:D], x[:, p, :], ALU.add), (tag, p))
                    if 1 <= i <= HP:
                        p = first + i - 1
                        await_read_out(dve, (tag or "tok", p))
                        nc.vector.bn_stats(stats[:, p, :], x[:, p, :]).then_inc(sem("bn_done"), 1)
                    if i >= 2:
                        p = first + i - 2
                        bn[0] += 1
                        dve.wait_ge(sem("bn_done"), bn[0])
                        last = nc.vector.bn_aggr(mv[:, p, :], stats[:, p, :])
                last.then_inc(sem("stats_done"), 1)

            def normalize(n, hf, kind):
                dve.wait_ge(sem("rstd_done"), 2 * n + hf + 1)
                for p in pairs(hf):
                    mean = mv[:, p, 0:1]
                    first, second = pw_out[:, 0, p:p + 1], pw_out[:, 1, p:p + 1]
                    if kind == "ln":
                        last = ts(xn[:, p, :], rows[n][:, p, :], mean, first, ALU.subtract, ALU.mult)
                    elif kind == "ln+norm":
                        last = ts(xn[:, p, :], rows[n][:, p, :], mean, second, ALU.subtract, ALU.mult)
                    else:
                        last = ts(xn[:, p, :], rows[n][:, p, :], first, None, ALU.mult)
                last.then_inc(sem("xn_done"), 1)

            def columns(n, hf, scale=None, bias=None):
                key = (f"n{n}", hf, 1)
                b = read(dve, key)
                if scale and bias:
                    last = ts(xT[0:C, 1, pad_half(hf)], b[0:C, :], col96(scale, 1), col96(bias, 1), ALU.mult, ALU.add)
                elif scale:
                    last = ts(xT[0:C, 1, pad_half(hf)], b[0:C, :], col96(scale, 1), None, ALU.mult)
                else:
                    last = nc.vector.tensor_copy(xT[0:C, 1, pad_half(hf)], b[0:C, :])
                free(last, key)

            rows = {0: h, 1: h, 2: h, 3: u, 4: h, 5: u}

            def keys_values0(hf):
                for p in pairs(hf):
                    if p % 2 == 0:
                        b = read(dve, ("kv0", p))
                        free(nc.vector.tensor_copy(kv[:, p, :], b[:, 0:2 * D]), ("kv0", p))

            def own_blocks(hf):
                for pp in range(2):
                    for par in range(2):
                        await_read_out(dve, ("kTv", hf, pp, par))
                        img = HI * hf + 4 * pp + par
                        blocks = gkr[:, img:img + 3:2].rearrange("p i c (h e) -> p i c h e", e=HFD)
                        kept = gkv[:, img:img + 3:2].rearrange("p i c (h e) -> p i c h e", e=HFD)
                        for i in range(2):
                            last = tt(kept[:, i], blocks[:, i], mask_head[:, :].unsqueeze(1).unsqueeze(3)
                                      .broadcast_to([C, 2, 6, HFD]), ALU.mult)
                        last.then_inc(sem("kv_masked"), 1)

            def attended0(hf):
                for c in range(2):
                    b = read(dve, ("o0", hf, c))
                    free(nc.vector.tensor_copy(real(oT, c, hf), by_image(b[0:C, 0:HT])), ("o0", hf, c))

            statistics(h, 0)
            normalize(0, 0, "ln")
            dve.wait_ge(sem("pool_init"), 1)
            columns(0, 0)
            statistics(h, 1)
            normalize(0, 1, "ln")
            keys_values0(0)
            columns(0, 1)
            dve.wait_ge(sem("set0_loaded"), 16 * 5)
            own_blocks(0)
            keys_values0(1)
            attended0(0)
            own_blocks(1)
            statistics(h, 0, "proj0")
            attended0(1)
            normalize(1, 0, "ln")
            statistics(h, 1, "proj0")
            columns(1, 0)
            normalize(1, 1, "ln")
            columns(1, 1)

            def by_token(rt, name, n, hf=None):
                sl = slice(0, PAIRS) if hf is None else slice(HP * hf, HP * hf + HP)
                return rt[name][:, 0:PAIRS * n].rearrange("p (q e) -> p q e", q=PAIRS)[:, sl]

            def spread(x, n):
                return x.unsqueeze(2).broadcast_to([128, x.shape[1], n])

            def shifted_logits(rt, key, n, hf):
                b = read(dve, (key, hf))
                logits = b[:, 0:HP * n].rearrange("p (q e) -> p q e", q=HP)
                mx = by_token(rt, "mx", 1, hf)[:, :, 0]
                link(reduce(mx, logits, AX.X, ALU.max))
                free(tt(by_token(rt, "s", n, hf), logits, spread(mx, n), ALU.subtract), (key, hf))

            def best(rt, x, n, k, run):
                le, eq, before, sel = (by_token(rt, name, n) for name in ("le", "eq", "before", "sel"))
                for q in range(PAIRS):
                    last = nc.vector.max(rt["top"][:, q * 8:(q + 1) * 8], x[:, q, :])
                link(last)
                kth = rt["top"][:, :].rearrange("p (q k) -> p q k", q=PAIRS)[:, :, k - 1]
                tt(le, x, spread(kth, n), ALU.is_le)
                link(tt(eq, x, spread(kth, n), ALU.is_equal))
                nc.vector.tensor_tensor_scan(rt["before"][:, 0:PAIRS * n], run, rt["eq"][:, 0:PAIRS * n], 0.0,
                                             ALU.mult, ALU.add)
                link(reduce(rt["les"][:, :], le, AX.X, ALU.add))
                link(stt(before, before, float(n - k), spread(rt["les"], n), ALU.add, ALU.is_le))
                link(tt(eq, eq, before, ALU.mult))
                link(stt(sel, le, 1.0, eq, ALU.subtract, ALU.subtract))

            dve.wait_ge(sem("set1_loaded"), 16 * 4)
            for hf in range(2):
                shifted_logits(rt0, "gate0", E0, hf)
            dve.wait_ge(sem("route_exp"), 2)
            e, score, biased_score = (by_token(rt0, name, E0) for name in ("e", "score", "s"))
            link(reduce(rt0["sum"][:, :], e, AX.X, ALU.add))
            link(nc.vector.reciprocal(rt0["inv"][:, :], rt0["sum"][:, :]))
            link(tt(score, e, spread(rt0["inv"], E0), ALU.mult))
            link(tt(biased_score, score, route_bias[:, :].unsqueeze(1).broadcast_to([128, PAIRS, E0]), ALU.add))
            by_group = rt0["s"][:, :].rearrange("p (n two) -> p n two", two=2)
            link(reduce(rt0["gs"][:, :], by_group, AX.X, ALU.add))
            best(rt0, by_token(rt0, "gs", G0), G0, 4, run[:, 0:PAIRS * G0])
            link(ts(rt0["pen"][:, :], rt0["sel"][:, 0:PAIRS * G0], -BIG, -BIG, ALU.mult, ALU.add))
            link(tt(by_group, by_group, spread(rt0["pen"], 2), ALU.add))
            best(rt0, biased_score, E0, 4, run[:, PAIRS * G0:])
            stt(by_token(rt0, "w", E0), by_token(rt0, "sel", E0), -2.5, score, ALU.mult, ALU.mult)\
                .then_inc(sem("routed"), 1)

            def split(dst, src, ready, count):
                nc.vector.tensor_copy(dst[0][:, :], src).then_inc(ready, 1)
                dve.wait_ge(ready, count)
                tt(dst[1][:, :], src, dst[0][:, :].bitcast(F32), ALU.subtract).then_inc(ready, 1)

            def gate(x, buf, hf, dst):
                b, n = uses["g", hf]
                dve.wait_ge(bank_full[b], x + (n + 1))
                bu, nu = uses["u", hf]
                dve.wait_ge(bank_free[bu], x + (nu + 1))
                return stt(dst, bank[b][:, 0:HT], bias0[buf][:, 1:2], s0[hf], ALU.add, ALU.mult), bank_free[b]

            dve.wait_ge(sem("bias0_loaded0"), 16)
            for hf in range(2):
                ins, freed = gate(0, 0, hf, p0[hf])
                ins.then_inc(freed, 1)
                dve.wait_ge(freed, uses["g", hf][1] + 1)
                split(a0[hf], p0[hf], sem(f"act0_ready{hf}"), 1)
            with dve.Fori(0, E0 // NB0) as it:
                for j in range(NB0):
                    x, buf = it * NB0 + (j + 1), (j + 1) % NB0
                    dve.wait_ge(sem(f"w0_loaded{buf}"), it * 16 + 16)
                    dve.wait_ge(sem(f"bias0_loaded{buf}"), it * 16 + (16 if buf else 32))
                    for hf in range(2):
                        ins, freed = gate(x, buf, hf, f0[hf])
                        ins.then_inc(freed, 1)
                        dve.wait_ge(freed, x + (uses["g", hf][1] + 1))
                        tt(p0[hf], f0[hf], wb0[buf][:, half(hf)], ALU.mult).then_inc(sem(f"act0_ready{hf}"), 1)
                        dve.wait_ge(sem(f"act0_ready{hf}"), x * 3)
                        split(a0[hf], p0[hf], sem(f"act0_ready{hf}"), x * 3 + 1)
            for hf in range(2):
                statistics(h, hf, "y0t")

            for hf in range(2):
                normalize(2, hf, "ln+norm")
            dve.wait_ge(sem("set2_loaded"), 16 * 11)
            for hf in range(2):
                columns(2, hf, "rms1_w")
            for m in range(4):
                b = read(dve, ("rel_w", m))
                free(tt(rbd[:, m], b[:, 0:REL].unsqueeze(1).broadcast_to([128, 2, REL]),
                        mask_pair[:, :].unsqueeze(2).broadcast_to([128, 2, REL]), ALU.mult), ("rel_w", m))
            for hf in range(2):
                imgs = slice(HI * hf, HI * hf + HI)
                for m in range(4):
                    b = read(dve, ("k1", hf, m))
                    shape = [128, HI, 2, TOK]
                    free(tt(kbd1[:, m, imgs], by_image(b[:, 0:HT]).unsqueeze(2).broadcast_to(shape),
                            mask_pair[:, :].unsqueeze(1).unsqueeze(3).broadcast_to(shape), ALU.mult), ("k1", hf, m))
                for q in range(2):
                    b = read(dve, ("v1", hf, q))
                    shape = [128, 16, 2, HBV]
                    at = (HI * hf + 4 * q) * 4
                    free(tt(vbd1[:, at:at + 16], b[:, 0:4 * C].rearrange("p (n d) -> p n d", d=HBV)
                            .unsqueeze(2).broadcast_to(shape),
                            mask_pair[:, :].unsqueeze(1).unsqueeze(3).broadcast_to(shape), ALU.mult), ("v1", hf, q))

            def attended(tag, hf):
                b = read(dve, (tag, hf, 1))
                free(nc.vector.tensor_copy(oT[0:C, 1, pad_half(hf)], b[0:C, :]), (tag, hf, 1))

            def shifted1(p):
                if p % HP == 0:
                    dve.wait_ge(sem(f"rel_loaded{p // HP}"), 16 * 2 * HP)
                x = probs1[:, p % AHEAD, :, 0:TOK]
                b = read(dve, ("s1", p))
                free(tt(x, b[:, 0:HB * TOK].rearrange("p (h j) -> p h j", h=HB), rels[:, p], ALU.add), ("s1", p))
                await_read_out(dve, ("s1", p))
                mx = row_max[:, p, 0:HB]
                link(reduce(mx, x, AX.X, ALU.max))
                tt(x, x, mx.unsqueeze(2).broadcast_to([128, HB, TOK]), ALU.subtract).then_inc(sem("shifted1"), 1)

            def sums(p, probs, done, n):
                dve.wait_ge(sem(done), p + 1)
                link(reduce(row_sum[:, p, 0:n], probs[:, p % AHEAD, :, 0:TOK], AX.X, ALU.add))
                link(nc.vector.reciprocal(row_inv[:, p, 0:n], row_sum[:, p, 0:n]))

            def scaled(p, key, n):
                b = read(dve, key)
                shape = [128, n, D // n]
                ins = tt(xn[:, p, :].rearrange("p (h d) -> p h d", h=n),
                         b[:, 0:D].rearrange("p (h d) -> p h d", h=n),
                         row_inv[:, p, 0:n].unsqueeze(2).broadcast_to(shape), ALU.mult)
                free(ins, key)

            for p in range(2):
                shifted1(p)
            for p in range(PAIRS):
                if p + 2 < PAIRS:
                    shifted1(p + 2)
                sums(p, probs1, "exp1_done", HB)
                if p:
                    scaled(p - 1, ("av1", p - 1), HB)
                if p == HP + 1:
                    attended("o1t", 0)
                if p == HP + 2:
                    dve.wait_ge(sem("skip_ready"), 1)
                    statistics(u, 0, "wo1")
            scaled(PAIRS - 1, ("av1", PAIRS - 1), HB)

            attended("o1t", 1)
            normalize(3, 0, "rms")
            dve.wait_ge(sem("skip_ready"), 2)
            statistics(u, 1, "wo1")

            columns(3, 0, "rms2_w")
            normalize(3, 1, "rms")
            columns(3, 1, "rms2_w")
            dve.wait_ge(sem("set3_loaded"), 16 * 6)
            for hf in range(2):
                dve.wait_ge(sem("skip1_added"), hf + 1)
                statistics(h, hf, "f2")
                normalize(4, hf, "ln+norm")
                columns(4, hf, "ln1_w", "ln1_b")
            for hf in range(2):
                imgs = slice(HI * hf, HI * hf + HI)
                await_read_out(dve, ("k2", hf, 1))
                shape = [C, HI, 6, TOK]
                tt(kbd2[:, 1, imgs], by_image(k2[:, 1, half(hf)]).unsqueeze(2).broadcast_to(shape),
                   mask_head[:, :].unsqueeze(1).unsqueeze(3).broadcast_to(shape), ALU.mult)\
                    .then_inc(sem("keys2_masked_dve"), 1)
                for q in range(2):
                    b = read(dve, ("v2", hf, q))
                    shape = [128, 24, 2, HFD]
                    at = (HI * hf + 4 * q) * 6
                    free(tt(vbd2[:, at:at + 24], b[:, 0:4 * C].rearrange("p (n d) -> p n d", d=HFD)
                            .unsqueeze(2).broadcast_to(shape),
                            mask_pair[:, :].unsqueeze(1).unsqueeze(3).broadcast_to(shape), ALU.mult), ("v2", hf, q))

            def shifted2(p):
                x = probs2[:, p % AHEAD, :, 0:TOK]
                b = read(dve, ("s2", p))
                scores = b[:, 0:HF * TOK].rearrange("p (h j) -> p h j", h=HF)
                mx = row_max[:, p, :]
                link(reduce(mx, scores, AX.X, ALU.max))
                free(tt(x, scores, mx.unsqueeze(2).broadcast_to([128, HF, TOK]), ALU.subtract), ("s2", p))

            for p in range(2):
                shifted2(p)
            for p in range(PAIRS):
                if p + 2 < PAIRS:
                    shifted2(p + 2)
                sums(p, probs2, "exp2_done", HF)
                if p:
                    scaled(p - 1, ("av2", p - 1), HF)
                if p == HP + 1:
                    attended("o2t", 0)
                if p == HP + 2:
                    dve.wait_ge(sem("skip_ready"), 3)
                    statistics(u, 0, "wo2")
            scaled(PAIRS - 1, ("av2", PAIRS - 1), HF)
            attended("o2t", 1)
            normalize(5, 0, "ln")
            dve.wait_ge(sem("skip_ready"), 4)
            statistics(u, 1, "wo2")
            columns(5, 0, "ln2_w", "ln2_b")
            normalize(5, 1, "ln")
            columns(5, 1, "ln2_w", "ln2_b")

            for hf in range(2):
                shifted_logits(rt1, "gate1", E1, hf)
                await_read_out(dve, ("gate1", hf))
            best(rt1, by_token(rt1, "s", E1), E1, 2, run[:, 0:PAIRS * E1])
            dve.wait_ge(sem("route_exp"), 4)
            e = by_token(rt1, "e", E1)
            link(stt(e, by_token(rt1, "sel", E1), -1.0, e, ALU.mult, ALU.mult))
            link(reduce(rt1["sum"][:, :], e, AX.X, ALU.add))
            link(nc.vector.reciprocal(rt1["inv"][:, :], rt1["sum"][:, :]))
            tt(by_token(rt1, "w", E1), e, spread(rt1["inv"], E1), ALU.mult).then_inc(sem("routed"), 1)

            b = read(dve, "first_row1")
            nc.vector.tensor_copy(wb1[0][:, half(0)], b[:, 0:HT]).then_inc(sem("w1_loaded00"), 16)
            dve.wait_ge(sem("w1_loaded00"), 16)
            free(nc.vector.tensor_copy(warm_dve[:, :], wb1[0][:, 0:1]), "first_row1")

            with dve.Fori(0, E1 // NB1) as it:
                for buf in range(NB1):
                    for n in range(2 * M1):
                        if n % M1 == 0:
                            dve.wait_ge(sem(f"w1_loaded{buf}{n // M1}"), it * 16 + 16)
                        b, base = uses["hid", n % 4]
                        dve.wait_ge(bank_free[b], it * (NB1 * turns) + (base + buf * turns + n // 4 + 1))
                        done = it * (3 * NB1 * 2 * M1) + 3 * (buf * 2 * M1 + n)
                        tt(hp[n % 4], hg[n % 4], wb1[buf][:, half(n // M1)], ALU.mult)\
                            .then_inc(sem("hid1_ready"), 1)
                        dve.wait_ge(sem("hid1_ready"), done + 1)
                        split(hs[n % 4], hp[n % 4], sem("hid1_ready"), done + 2)
            dve.wait_ge(sem("skip2_added"), 1)
            for p in range(PAIRS):
                b = read(dve, ("y1t", p))
                tt(h[:, p, :], b[:, 0:D], h[:, p, :], ALU.add).then_inc(sem("result_ready"), 1)


def laid_out(i):
    f = {k: np.asarray(v) for k, v in i.items()}
    z = np.zeros
    t = np.float32

    def chunks(w, p=C):
        return np.ascontiguousarray(w.reshape(-1, p, w.shape[1]).transpose(1, 0, 2))

    def biased(w, b):
        r = z((C + 1, 2, w.shape[1]), t)
        r[:C] = chunks(w)
        r[C, 1] = b
        return r

    def columns(v, p=C):
        return v.reshape(-1, p).T

    def by_parity(w, heads):
        return w.reshape(*w.shape[:-1], heads // 2, 2, D // heads).swapaxes(-3, -2).reshape(*w.shape[:-1], D)

    p = f["x"].reshape(IMAGES, 3, 6, 16, 6, 16).transpose(0, 2, 4, 1, 3, 5).reshape(IMAGES, TOK, 768)
    padded = z((IMAGES, SLOT, 768), t)
    padded[:, :TOK] = p
    o = {}
    o["patches"] = padded.reshape(PAIRS, 128, PATCH_CHUNKS, 128).transpose(0, 3, 2, 1)
    o["tok_w"] = chunks(f["L0_tok_W"].T, 128)
    o["wqkv0"] = chunks(f["L0_attn_w_qkv"])
    o["wproj0"] = biased(f["L0_attn_w_proj"], f["L0_attn_b_proj"])
    o["gate0w"] = biased(f["L0_ffn_gate_w"], f["L0_ffn_gate_b"])
    o["route_bias"] = np.tile(f["L0_ffn_bias"], (128, 1))
    o["bd0"] = f["L0_ffn_bd"]
    wu = np.concatenate([f["L0_ffn_sWu"][None], f["L0_ffn_Wu"]]).reshape(E0 + 1, 2, C, HID0)
    wg = np.concatenate([f["L0_ffn_sWg"][None], f["L0_ffn_Wg"]]).reshape(E0 + 1, 2, C, HID0)
    o["up0"] = np.concatenate([wu, wg], 3).transpose(0, 2, 1, 3)
    wd = np.concatenate([f["L0_ffn_sWd"][None], f["L0_ffn_Wd"]])
    bu = np.concatenate([f["L0_ffn_sbu"][None], f["L0_ffn_bu"]])[:, :, None]
    bg = np.concatenate([f["L0_ffn_sbg"][None], f["L0_ffn_bg"]])[:, :, None]
    o["down0"] = wd
    o["bias0"] = np.concatenate([bu, bg], 2)
    o["wq1"], o["wk1"] = chunks(f["L1_attn_wq"]), chunks(f["L1_attn_wk"])
    o["wv1"] = chunks(by_parity(f["L1_attn_wv"], HB))
    o["wout1"] = biased(f["L1_attn_wo"], f["L1_attn_bo"])
    o["wposT"] = f["L1_attn_w_pos"].reshape(HB * HD, NPOS).T
    o["w1a"], o["w2a"] = chunks(f["L1_attn_w1"]), chunks(f["L1_attn_w2"], 128)
    o["b2_row"] = np.tile(f["L1_attn_b2"], (128, 1))
    qkv = f["L1_ffn_qkv_w"].T
    o["wqk2"] = chunks(qkv[:, :2 * D])
    qkv_b = f["L1_ffn_qkv_b"]
    o["wv2"] = biased(by_parity(qkv[:, 2 * D:], HF), by_parity(qkv_b[2 * D:], HF))
    o["wout2"] = biased(f["L1_ffn_proj_w"].T, f["L1_ffn_proj_b"])
    o["gate1w"] = chunks(f["L1_ffn_w_gate"])
    o["b2m"] = f["L1_ffn_b2"]
    o["up1"] = f["L1_ffn_W1"].reshape(E1, 2, C, HID1M).transpose(0, 2, 1, 3)
    w2 = f["L1_ffn_W2"].reshape(E1, M1, 128, D).transpose(0, 2, 1, 3).reshape(E1, 128, M1 * D)
    o["down1"] = w2
    o["bias1"] = f["L1_ffn_b1"].reshape(E1, M1, 128).transpose(0, 2, 1)
    o["c96"] = np.concatenate([columns(v) for v in (
        f["L0_ffn_sbd"], f["L1_attn_norm1_w"], f["L1_attn_norm2_w"], f["L1_ffn_norm1_w"], f["L1_ffn_norm1_b"],
        f["L1_ffn_norm2_w"], f["L1_ffn_norm2_b"], qkv_b[:D], qkv_b[D:2 * D])], 1)
    o["c128"] = np.concatenate([columns(f["L1_attn_u_param"].reshape(-1), 128),
                                columns(f["L1_attn_v_param"].reshape(-1), 128),
                                columns(f["L1_attn_b1"], 128)], 1)
    o["first_row"] = np.repeat((np.arange(E1)[:, None] == 0).astype(t), 128, 1)
    o["ident"] = np.eye(128, dtype=t)
    o["mask_pair"] = (np.arange(128)[:, None] // 64 == np.arange(2)).astype(t)
    o["mask_head"] = (np.arange(C)[:, None] // HFD == np.arange(6)).astype(t)
    inside = lambda n: np.tile((np.arange(n) > 0).astype(t), PAIRS)
    o["run"] = np.tile(np.concatenate([inside(G0), inside(E0)]), (128, 1))
    d = np.arange(-(TOK - 1), TOK).astype(t)
    rate = np.exp(np.log(t((TOK + 1) / 2.0)) / t(NPOS // 2)).astype(t)
    widths = (rate ** np.arange(1, NPOS // 2 + 1, dtype=t)).astype(t)
    near = (np.abs(d)[None, :] <= widths[:, None]).astype(t)
    o["basis"] = np.concatenate([near, np.sign(d)[None, :] * near]).astype(t)
    return {k: np.ascontiguousarray(v) for k, v in o.items()}


def kernel(**inputs):
    import concourse.bacc as bacc
    from concourse.bass_utils import run_bass_kernel_spmd

    arrays = laid_out(inputs)
    nc = bacc.Bacc("TRN2", target_bir_lowering=False, num_devices=1)
    args = {k: nc.dram_tensor(f"in_{k}", v.shape, mybir.dt.from_np(v.dtype), kind="ExternalInput").ap()
            for k, v in arrays.items()}
    out = nc.dram_tensor("out", (IMAGES, TOK, D), F32, kind="ExternalOutput").ap()
    build_tower(nc, args, out)
    r = run_bass_kernel_spmd(nc, [{f"in_{k}": v for k, v in arrays.items()}], core_ids=[0])
    return r.results[0]["out"]
```

```python
from contextlib import ExitStack

import numpy as np

import concourse.bass as bass
from concourse import mybir

F32 = mybir.dt.float32
F32R = mybir.dt.float32r
ALU = mybir.AluOpType
ACT = mybir.ActivationFunctionType
AX = mybir.AxisListType

IMAGES = 16
TOK = 36
D = 192
C = 96
CB = D - 128
SLOT = 64
PAIRS = IMAGES // 2
HP = PAIRS // 2
HI = IMAGES // 2
HT = HI * TOK
T = IMAGES * TOK
PATCH_CHUNKS = 768 // 128
PATCH_LOADS = [(0, 1), (1, 1), (2, 2), (4, 2), (6, 2)]
EPS = 1e-5
SPLIT_NORMS = (0, 1, 5)
PARTS = [(0, 0), (0, 2), (2, 0), (1, 1), (3, 1)]
AB = [(0, 128), (128, CB)]

H0 = 12
HB, HD = 8, 64
HBV = D // HB
HF, HFD = 12, 16
REL = 2 * TOK - 1
NPOS = 32
HID1 = 384

E0, G0, HID0 = 16, 8, 128
E1, HID1M = 8, 768
M1 = HID1M // 128
NB0, NB1 = 4, 2
AHEAD = 4
BIG = 1.0e30

COL96 = {n: (2 * i, 2) for i, n in enumerate(
    ["rms1_w", "rms2_w", "ln1_w", "ln1_b", "q_b", "k_b"])}
N96 = 2 * len(COL96)
COL128 = {"u": (0, 4), "v": (4, 4), "b1": (8, 3), "ln2_w": (11, 2), "ln2_b": (13, 2),
          "sbd": (15, 2)}
N128 = 17


def psum_uses():
    keys = []
    halves = range(2)
    pairs = lambda hf: range(HP * hf, HP * hf + HP)

    def norm(tag, hf):
        keys.extend((tag, hf, c) for c in range(2))

    keys.extend(("tok", p) for p in range(HP + 2))
    norm("n0", 0)
    keys.extend(("tok", p) for p in range(HP + 2, PAIRS))
    for hf in halves:
        keys.extend(("q0", hf, c) for c in range(2))
        for p in pairs(hf):
            keys.append(("kv0", p))
            if p == HP - 2:
                norm("n0", 1)
        if hf == 0:
            keys.extend(("kTv", 0, pp, par) for pp in range(2) for par in range(2))
    keys.extend(("o0", 0, c) for c in range(2))
    keys.extend(("kTv", 1, pp, par) for pp in range(2) for par in range(2))
    keys.extend(("proj0", p) for p in pairs(0))
    keys.extend(("o0", 1, c) for c in range(2))
    keys.extend(("proj0", p) for p in pairs(1))
    for hf in halves:
        norm("n1", hf)
        keys.append(("gate0", hf))
    used, uses, at = [0] * 8, {}, 0

    def place(keys, at):
        for k in keys:
            b = at % 8
            assert k not in uses
            uses[k] = (b, used[b])
            used[b] += 1
            at += 1
        return at

    place(keys, at)
    for hf in halves:
        uses["wT0", hf] = (2 * hf, used[2 * hf])
        used[2 * hf] += 1
    for hf in halves:
        uses["u", hf] = (4 + 2 * hf, used[4 + 2 * hf])
        uses["g", hf] = (5 + 2 * hf, used[5 + 2 * hf])
        for c in range(2):
            uses["y0", hf, c] = (2 * hf + c, used[2 * hf + c])
    for b in range(4):
        used[b] += 1
        used[4 + b] += E0 + 1
    place([("y0t", p) for p in range(PAIRS)], 4)
    keys = [("rel_w", m) for m in range(4)]
    for hf in halves:
        keys += [("n2", hf, c) for c in range(2)]
    for hf in halves:
        keys += [("q1", hf, m) for m in range(4)]
        keys += [("k1", hf, m) for m in range(4)]
        keys += [("rel", p, s) for p in pairs(hf) for s in range(2)]
        keys += [("v1", hf, q) for q in range(2)]
    keys += [("s1", p) for p in range(AHEAD)]
    for p in range(PAIRS + 1):
        keys += [("p1t", p)] * (p < PAIRS) + [("s1", p + AHEAD)] * (p + AHEAD < PAIRS)
        keys += [("av1", p - 1)] * (p > 0)
        if p == HP + 1:
            norm("o1t", 0)
        if p == HP + 2:
            keys += [("wo1", q) for q in pairs(0)]
    norm("o1t", 1)
    keys += [("wo1", p) for p in pairs(1)]
    norm("n3", 0)
    keys += [("f1", 0, m) for m in range(3)]
    norm("n3", 1)
    keys += [("f2", p) for p in pairs(0)]
    keys += [("f1", 1, m) for m in range(3)]
    keys += [("f2", p) for p in pairs(1)[:2]]
    norm("n4", 0)
    keys += [("f2", p) for p in pairs(1)[2:]]
    for hf in halves:
        keys += [("q2", hf, c) for c in range(2)]
        keys += [("k2", hf, c) for c in range(2)]
        keys += [("v2", hf, 0)]
        if hf == 0:
            norm("n4", 1)
        keys += [("v2", hf, 1)]
    keys += [("s2", p) for p in range(AHEAD)]
    for p in range(PAIRS + 1):
        keys += [("p2t", p, 0), ("p2t", p, 1)] * (p < PAIRS) + [("s2", p + AHEAD)] * (p + AHEAD < PAIRS)
        keys += [("av2", p - 1)] * (p > 0)
        if p == HP + 1:
            norm("o2t", 0)
        if p == HP + 2:
            keys += [("wo2", q) for q in pairs(0)]
    norm("o2t", 1)
    keys += [("wo2", p) for p in pairs(1)]
    place(keys, 0)
    for hf in halves:
        for i, key in enumerate([("n5", hf, 0), ("n5", hf, 1), ("gate1", hf)]):
            b = (3 * hf + i) % 4
            uses[key] = (b, used[b])
            used[b] += 1
    for hf in halves:
        uses["wT1", hf] = (2 * hf, used[2 * hf])
        used[2 * hf] += 1
    uses["first_row1"] = (7, used[7])
    used[7] += 1
    for b in range(4):
        uses["hid", b] = (4 + b, used[4 + b])
        uses["y1", b // 2, b % 2] = (b, used[b])
    for b in range(4):
        used[b] += 1
        used[4 + b] += E1 * 2 * M1 // 4
    place([("y1t", p) for p in range(PAIRS)], 4)
    return uses


def build_tower(nc, a, out):
    uses = psum_uses()
    ctx = ExitStack()
    with ctx:
        def sb(name, shape):
            return ctx.enter_context(nc.sbuf_tensor(name, shape, F32))

        semaphores = {}

        def sem(name):
            if name not in semaphores:
                semaphores[name] = ctx.enter_context(nc.semaphore(name))
            return semaphores[name]

        def dram(name, shape):
            return nc.dram_tensor(name, shape, F32, kind="Internal").ap()

        bank = [ctx.enter_context(nc.psum_tensor(f"bank{b}", [128, 512], F32)) for b in range(8)]
        bank_full = [sem(f"bank_full{b}") for b in range(8)]
        bank_free = [sem(f"bank_free{b}") for b in range(8)]

        rel_d = dram("rel_by_distance", [PAIRS, 128, HB * REL])
        w0_d = dram("expert_weights0", [E0, T])
        w1_d = dram("expert_weights1", [E1, T])

        h = sb("h", [128, PAIRS, D])
        xn = sb("xn", [128, PAIRS, D])
        u = sb("u", [128, PAIRS, D])
        stats = sb("stats", [128, PAIRS, 6])
        mv = sb("mv", [128, PAIRS, 2])
        pw_in = sb("pw_in", [128, 2, PAIRS])
        pw_out = sb("pw_out", [128, 2, PAIRS])
        minus_half = sb("minus_half", [128, 2, PAIRS])
        warm = sb("warm", [128, 1])
        first_row = sb("first_row", [E1, 128])
        row_max = sb("row_max", [128, PAIRS, HF])
        row_sum = sb("row_sum", [128, PAIRS, HF])
        row_inv = sb("row_inv", [128, PAIRS, HF])

        xT = sb("xT", [128, 2, IMAGES * SLOT])
        oT = sb("oT", [97, 2, IMAGES * SLOT])

        ident = sb("ident", [128, 128])
        mask_pair = sb("mask_pair", [128, 2])
        mask_head = sb("mask_head", [C, 6])
        run = sb("run", [128, PAIRS * (G0 + E0)])
        basis = sb("basis", [NPOS, REL])
        c96 = sb("c96", [C, N96])
        c128 = sb("c128", [128, N128])
        b2_row = sb("b2_row", [128, D])
        route_bias = sb("route_bias", [128, E0])
        wproj0 = sb("wproj0", [97, 2, D])
        gate0w = sb("gate0w", [128, 2, E0])
        gate0_bias = sb("gate0_bias", [128, E0])
        bd0 = sb("bd0", [E0, 256])
        wq1 = sb("wq1", [C, 2, HB * HD])
        wk1 = sb("wk1", [C, 2, HB * HD])
        wv1 = sb("wv1", [C, 2, D])
        wout1 = sb("wout1", [97, 2, D])
        wposT = sb("wposT", [NPOS, HB * HD])
        w1a = sb("w1a", [C, 2, HID1])
        w2a = sb("w2a", [128, 3, D])
        wqk2 = sb("wqk2", [C, 2, 2 * D])
        wv2 = sb("wv2", [97, 2, D])
        wout2 = sb("wout2", [97, 2, D])
        gate1w = sb("gate1w", [128, 2, E1])
        b2m = sb("b2m", [E1, 256])
        fold = sb("fold", [128, CB])
        wT = sb("wT", [E0, T])

        def phase():
            return ExitStack()

        def in_phase(scope, name, shape, dt=F32):
            return scope.enter_context(nc.sbuf_tensor(name, shape, dt))

        with phase() as scope:
            arena = in_phase(scope, "arena", [128, 25624])

        def part(lo, n):
            return arena[:, lo:lo + n]

        KB, VB, PT, QU, QV, RS, PP = 0, 7448, 10520, 12056, 16152, 20248, 22552
        qu = part(QU, 4096).rearrange("p (m t) -> p m t", m=4)
        qv = part(QV, 4096).rearrange("p (m t) -> p m t", m=4)
        kbd1 = part(KB, 4608).rearrange("p (m i e j) -> p m i e j", m=4, i=IMAGES, e=2)
        rbd = part(KB + 4608, 568).rearrange("p (m e r) -> p m e r", m=4, e=2)
        relb = part(KB + 5176, HP * HB * REL).rearrange("p (q n) -> p q n", q=HP)
        rels = part(RS, PAIRS * HB * TOK).rearrange("p (q h j) -> p q h j", q=PAIRS, h=HB)
        vbd1 = part(VB, IMAGES * D).rearrange("p (n e d) -> p n e d", e=2, d=HBV)
        probs1 = part(PP, AHEAD * HB * SLOT).rearrange("p (r h j) -> p r h j", r=AHEAD, h=HB)
        pt1 = part(PT, 2 * 512).rearrange("p (r n) -> p r n", r=2)
        g1 = qu[:, 0:3, :]
        q2 = qv[0:C, 0:2, :]
        kbd2 = part(KB, 6912)[0:C, :].rearrange("p (c i e j) -> p c i e j", c=2, i=IMAGES, e=6)
        k2 = part(RS, 2 * T)[0:C, :].rearrange("p (c t) -> p c t", c=2)
        vbd2 = part(VB, IMAGES * D).rearrange("p (n e d) -> p n e d", e=2, d=HFD)
        probs2 = part(PP, AHEAD * HF * SLOT).rearrange("p (r h j) -> p r h j", r=AHEAD, h=HF)
        pt2 = part(PT, 2 * 768).rearrange("p (r n) -> p r n", r=2)
        xp = part(0, 6144).rearrange("p (q k t) -> p q k t", q=PAIRS, k=PATCH_CHUNKS)
        tokw = part(6144, 1152).rearrange("p (k n) -> p k n", k=PATCH_CHUNKS)
        kv = part(7296, 3072).rearrange("p (q n) -> p q n", q=PAIRS)
        gq = part(10368, 1152)[0:C, :].rearrange("p (c t) -> p c t", c=2)
        gkr = part(11520, 3072)[0:C, :].rearrange("p (i c e) -> p i c e", i=IMAGES, c=2)
        gkv = part(14592, 3072)[0:C, :].rearrange("p (i c e) -> p i c e", i=IMAGES, c=2)
        wqkv0 = part(17664, 1152).rearrange("p (c n) -> p c n", c=2)

        def parts(scope, name, shape):
            return [in_phase(scope, f"{name}_{x}", shape, F32R) for x in ("high", "low")]

        with phase() as scope:
            in_phase(scope, "before_qkv0", [128, RS])
            xq = in_phase(scope, "xq_parts", [128, 3, IMAGES * SLOT], F32R)
            wq = in_phase(scope, "wqkv0_parts", [128, 4, 3 * D], F32R)
        with phase() as scope:
            x0 = in_phase(scope, "x0_parts", [128, 3, IMAGES * SLOT], F32R)
            up0s = [in_phase(scope, f"up0_{b}_parts", [128, 4, 2 * HID0], F32R) for b in range(NB0)]
            down0s = [in_phase(scope, f"down0_{b}_parts", [128, 1, 2 * D], F32R) for b in range(NB0)]
            a0 = [[parts(scope, f"a0_{r}{hf}", [128, HT]) for hf in range(2)] for r in range(2)]
        with phase() as scope:
            x1 = in_phase(scope, "x1_parts", [128, 3, IMAGES * SLOT], F32R)
            up1s = [in_phase(scope, f"up1_{b}_parts", [128, 4, HID1M], F32R) for b in range(NB1)]
            down1s = [in_phase(scope, f"down1_{b}_parts", [128, M1, 2 * D], F32R) for b in range(NB1)]
            hs = [parts(scope, f"hs_{r}", [128, HT]) for r in range(4)]
        in_phase(ctx, "phases", [128, 25624])

        moe = sb("moe", [128, 8844])

        def moe_part(lo, n):
            return moe[:, lo:lo + n]

        up0 = [moe_part(706 * b, 512).rearrange("p (c n) -> p c n", c=2) for b in range(NB0)]
        down0 = [moe_part(706 * b + 512, D) for b in range(NB0)]
        bias0 = [moe_part(706 * b + 512 + D, 2) for b in range(NB0)]
        wb0 = [moe_part(706 * NB0 + T * b, T) for b in range(NB0)]
        at = (706 + T) * NB0
        s0, p0, f0 = ([moe_part(at + (3 * hf + i) * HT, HT) for hf in range(2)] for i in range(3))
        up1 = [moe_part(2694 * b, 1536).rearrange("p (c n) -> p c n", c=2) for b in range(NB1)]
        down1 = [moe_part(2694 * b + 1536, M1 * D) for b in range(NB1)]
        bias1 = [moe_part(2694 * b + 1536 + M1 * D, M1) for b in range(NB1)]
        wb1 = [moe_part(2694 * NB1 + T * b, T) for b in range(NB1)]
        at = (2694 + T) * NB1
        hg, hp = ([moe_part(at + (4 * i + r) * HT, HT) for r in range(4)] for i in range(2))

        def routing_buffers(region, at):
            t = {}
            for name, n in (("e", E0), ("score", E0), ("s", E0), ("gs", G0), ("sel", E0), ("w", E0),
                            ("le", E0), ("eq", E0), ("before", E0), ("top", 8), ("pen", G0),
                            ("mx", 1), ("sum", 1), ("inv", 1), ("les", 1)):
                n *= PAIRS
                t[name] = region[:, at:at + n]
                at += n
            return t

        rt0, rt1 = routing_buffers(moe, (706 + T) * NB0 + 6 * HT), routing_buffers(arena, RS)

        turns = 2 * M1 // 4

        def col96(name, c):
            return c96[:, COL96[name][0] + c:COL96[name][0] + c + 1]

        def col128(name, m):
            return c128[:, COL128[name][0] + m:COL128[name][0] + m + 1]

        def real(t, c, hf, rows=None):
            rows = rows or (C if t.shape[0] == 97 else t.shape[0])
            return t[0:rows, c, hf * HI * SLOT:(hf + 1) * HI * SLOT]\
                .rearrange("p (i t) -> p i t", t=SLOT)[:, :, 0:TOK]

        def by_chunk(x):
            return x.rearrange("p (m n) -> p m n", n=D)

        def by_image(x):
            return x.rearrange("p (i t) -> p i t", t=TOK)

        def half(hf):
            return slice(hf * HT, (hf + 1) * HT)

        def pad_half(hf):
            return slice(hf * HI * SLOT, (hf + 1) * HI * SLOT)

        def pairs(hf):
            return range(HP * hf, HP * hf + HP)

        def pair_cols(p):
            return slice(2 * SLOT * p, 2 * SLOT * (p + 1))

        def fill(pe, key):
            b, n = uses[key]
            if n:
                pe.wait_ge(bank_free[b], n)
            return bank[b]

        def full(ins, key):
            ins.then_inc(bank_full[uses[key][0]], 1)

        def read(eng, key):
            b, n = uses[key]
            eng.wait_ge(bank_full[b], n + 1)
            return bank[b]

        def free(ins, key):
            ins.then_inc(bank_free[uses[key][0]], 1)

        def await_read_out(eng, key):
            b, n = uses[key]
            eng.wait_ge(bank_free[b], n + 1)

        block = ctx.enter_context(nc.Block())

        @block.sync
        def _(sp):
            def load_up(dst, src, loaded):
                sp.dma_start(dst[:, 0, :], src[0:128, :]).then_inc(sem(loaded), 16)
                sp.dma_start(dst[0:CB, 1, :], src[128:D, :]).then_inc(sem(loaded), 16)

            for i, (p, n) in enumerate(PATCH_LOADS):
                sp.dma_start(xp[:, p:p + n], a["patches"][p:p + n].rearrange("q p k t -> p q k t"))\
                  .then_inc(sem(f"patches{i}_loaded"), 16)
            for dst, name in ((ident[:, :], "ident"), (c96[:, :], "c96"), (mask_head[:, :], "mask_head"),
                              (wqkv0, "wqkv0"), (wproj0[:, :, :], "wproj0")):
                sp.dma_start(dst, a[name]).then_inc(sem("set0_loaded"), 16)
            for dst, name in ((gate0w[:, :, :], "gate0w"), (gate0_bias[:, :], "gate0_bias"), (run[:, :], "run"), (route_bias[:, :], "route_bias"),
                              (bd0[:, :], "bd0")):
                sp.dma_start(dst, a[name]).then_inc(sem("set1_loaded"), 16)
            for x in range(NB0):
                load_up(up0[x], a["up0"][x], f"expert0_loaded{x}")
                sp.dma_start(down0[x], a["down0"][x]).then_inc(sem(f"expert0_loaded{x}"), 16)
                sp.dma_start(bias0[x], a["bias0"][x]).then_inc(sem(f"bias0_loaded{x}"), 16)
            for dst, name in ((mask_pair[:, :], "mask_pair"), (basis[:, :], "basis"), (c128[:, :], "c128"),
                              (fold[:, :], "fold"), (b2_row[:, :], "b2_row"), (wq1[:, :, :], "wq1"), (wk1[:, :, :], "wk1"),
                              (wv1[:, :, :], "wv1"), (wout1[:, :, :], "wout1"), (wposT[:, :], "wposT"),
                              (w1a[:, :, :], "w1a"), (w2a[:, :, :], "w2a")):
                sp.dma_start(dst, a[name]).then_inc(sem("set2_loaded"), 16)
            for dst, name in ((wqk2[:, :, :], "wqk2"), (wv2[:, :, :], "wv2"), (wout2[:, :, :], "wout2"),
                              (gate1w[:, :, :], "gate1w"), (b2m[:, :], "b2m"),
                              (first_row[:, :], "first_row")):
                sp.dma_start(dst, a[name]).then_inc(sem("set3_loaded"), 16)

            for hf in range(2):
                await_read_out(sp, ("wT0", hf))
            sp.dma_start(w0_d, wT[:, :]).then_inc(sem("w0_stored"), 16)
            sp.wait_ge(sem("w0_stored"), 16)
            for x in range(1, NB0):
                sp.dma_start(wb0[x], w0_d[x - 1].partition_broadcast(128)).then_inc(sem(f"w0_loaded{x}"), 16)

            def reload0(it, b):
                sp.wait_ge(sem("expert0_low"), it * (3 * NB0) + 3 * (b + 1))
                load_up(up0[b], a["up0"][it * NB0 + (NB0 + b)], f"expert0_loaded{b}")
                sp.dma_start(down0[b], a["down0"][it * NB0 + (NB0 + b)]).then_inc(sem(f"expert0_loaded{b}"), 16)
                sp.wait_ge(sem("expert0_done"), it * NB0 + (b + 1))
                sp.dma_start(bias0[b], a["bias0"][it * NB0 + (NB0 + b)]).then_inc(sem(f"bias0_loaded{b}"), 16)
                sp.dma_start(wb0[b], w0_d[it * NB0 + (NB0 + b - 1)].partition_broadcast(128))\
                  .then_inc(sem(f"w0_loaded{b}"), 16)

            with sp.Fori(0, E0 // NB0 - 1) as it:
                for b in range(NB0):
                    reload0(it, b)
            reload0(E0 // NB0 - 1, 0)

            sp.wait_ge(sem("expert0_done"), E0 + 1)
            for b in range(NB1):
                load_up(up1[b], a["up1"][b], f"expert1_loaded{b}")
                sp.dma_start(down1[b], a["down1"][b]).then_inc(sem(f"expert1_loaded{b}"), 16)
                sp.dma_start(bias1[b], a["bias1"][b]).then_inc(sem(f"bias1_loaded{b}"), 16)

            for hf in range(2):
                for p in pairs(hf):
                    for s in range(2):
                        await_read_out(sp, ("rel", p, s))
                sp.dma_start(rel_d[HP * hf:HP * hf + HP].rearrange("q p n -> p q n"), relb)\
                  .then_inc(sem("rel_stored"), 16)
                sp.wait_ge(sem("rel_stored"), 16 * (hf + 1))
                for par in range(2):
                    row = HB * REL
                    for p in pairs(hf):
                        at = (p * 128 + par * SLOT) * row + TOK - 1
                        skewed = bass.AP(tensor=rel_d.tensor, offset=at,
                                         ap=[[row - 1, TOK], [REL, HB], [1, TOK]])
                        sp.dma_start(rels[par * SLOT:par * SLOT + TOK, p], skewed)\
                          .then_inc(sem(f"rel_loaded{hf}"), 16)

            for hf in range(2):
                await_read_out(sp, ("wT1", hf))
            sp.dma_start(w1_d, wT[0:E1, :]).then_inc(sem("w1_stored"), 16)
            sp.wait_ge(sem("w1_stored"), 16)

            def load_row1(x, b, hf):
                sp.dma_start(wb1[b][:, half(hf)], w1_d[x, half(hf)].partition_broadcast(128))\
                  .then_inc(sem(f"w1_loaded{b}{hf}"), 16)

            for b in range(NB1):
                for hf in range(2):
                    if b or hf:
                        load_row1(b, b, hf)
            with sp.Fori(0, E1 // NB1 - 1) as it:
                for b in range(NB1):
                    sp.wait_ge(sem("expert1_low"), it * (3 * NB1) + 3 * (b + 1))
                    load_up(up1[b], a["up1"][it * NB1 + NB1 + b], f"expert1_loaded{b}")
                    sp.dma_start(down1[b], a["down1"][it * NB1 + NB1 + b])\
                      .then_inc(sem(f"expert1_loaded{b}"), 16)
                    sp.wait_ge(sem("expert1_done"), it * NB1 + b + 1)
                    sp.dma_start(bias1[b], a["bias1"][it * NB1 + NB1 + b]).then_inc(sem(f"bias1_loaded{b}"), 16)
                    for hf in range(2):
                        load_row1(it * NB1 + NB1 + b, b, hf)
            result = out.rearrange("(q par) t d -> par t q d", par=2)
            for q in range(4):
                sp.wait_ge(sem("result_ready"), 2 * q + 2)
                for par in range(2):
                    sp.dma_start(result[par, :, 2 * q:2 * q + 2], h[par * SLOT:par * SLOT + TOK, 2 * q:2 * q + 2, :])\
                      .then_inc(sem("result_stored"), 16)
            sp.wait_ge(sem("result_stored"), 16 * 2 * 4)

        @block.gpsimd
        def _(pool):
            step = [0]

            def link(ins):
                step[0] += 1
                ins.then_inc(sem("pool_step"), 1)
                pool.wait_ge(sem("pool_step"), step[0])

            link(nc.gpsimd.memset(minus_half[:, :, :], -0.5))
            link(nc.gpsimd.memset(warm[:, :], 0.0))
            link(nc.gpsimd.memset(xT[:, :, :], 0.0))
            link(nc.gpsimd.memset(oT[C:C + 1, :, :], 1.0))
            nc.gpsimd.memset(oT[0:C, :, :], 0.0).then_inc(sem("pool_init"), 1)
            pool.wait_ge(sem("pool_init"), 1)

            def rstd(n, hf, kind):
                sl = slice(HP * hf, HP * hf + HP)
                mean, var = mv[:, sl, 0], mv[:, sl, 1]
                pool.wait_ge(sem("stats_done"), 2 * n + hf + 1)
                if kind == "rms":
                    link(nc.gpsimd.tensor_tensor(pw_in[:, 0, sl], mean, mean, ALU.mult))
                    link(nc.gpsimd.tensor_tensor(pw_in[:, 0, sl], pw_in[:, 0, sl], var, ALU.add))
                    link(nc.gpsimd.tensor_scalar(pw_in[:, 0, sl], pw_in[:, 0, sl], EPS, None, ALU.add))
                else:
                    link(nc.gpsimd.tensor_scalar(pw_in[:, 0, sl], var, EPS, None, ALU.add))
                k = 1
                if kind == "ln+norm":
                    link(nc.gpsimd.tensor_scalar(pw_in[:, 1, sl], var, 1.0 + EPS, EPS * EPS, ALU.mult, ALU.add))
                    k = 2
                nc.gpsimd.tensor_tensor(pw_out[:, 0:k, sl], pw_in[:, 0:k, sl], minus_half[:, 0:k, sl], ALU.pow)\
                    .then_inc(sem("rstd_done"), 1)

            def low(dst, src):
                return nc.gpsimd.tensor_tensor(dst[1], src, dst[0].bitcast(F32), ALU.subtract)

            def low_inputs(n, hf, x):
                cols = pad_half(hf)
                pool.wait_ge(sem("rstd_done"), 2 * n + hf + 1)
                pool.wait_ge(sem(f"x_high{n}"), hf + 1)
                link(low([x[:, 0, cols], x[:, 2, cols]], xT[:, 0, cols]))
                low([x[0:CB, 1, cols], x[CB:, 1, cols]], xT[0:CB, 1, cols]).then_inc(sem(f"x_low{n}"), 1)
                pool.wait_ge(sem(f"x_low{n}"), hf + 1)

            def low_up(w, src, chunk):
                rows = 128 if chunk == 0 else CB
                return low([w[0:rows, chunk, :], w[0:rows, chunk + 2, :]], src[0:rows, chunk, :])

            def low_down(w, src):
                low([w[:, :, 0:128], w[:, :, 256:384]], src[:, :, 0:128])
                return low([w[:, :, 128:192], w[:, :, 192:256]], src[:, :, 128:192])

            def low0(x, buf):
                pool.wait_ge(sem("expert0_high"), x + 1)
                for chunk in range(2):
                    low_up(up0s[buf], up0[buf], chunk).then_inc(sem("expert0_low"), 1)
                    pool.wait_ge(sem("expert0_low"), x * 3 + (chunk + 1))
                low_down(down0s[buf], by_chunk(down0[buf])).then_inc(sem("expert0_low"), 1)
                pool.wait_ge(sem("expert0_low"), x * 3 + 3)

            def low1(x, buf, piece):
                pool.wait_ge(sem("expert1_high"), x * 3 + (piece + 1))
                if piece < 2:
                    last = low_up(up1s[buf], up1[buf], piece)
                else:
                    last = low_down(down1s[buf], by_chunk(down1[buf]))
                last.then_inc(sem("expert1_low"), 1)
                pool.wait_ge(sem("expert1_low"), x * 3 + (piece + 1))

            rstd(0, 0, "ln")
            pool.wait_ge(sem("rstd_done"), 1)
            pool.wait_ge(sem("qkv0_high"), 1)
            for chunk in range(2):
                link(low_up(wq, wqkv0, chunk))
            low_inputs(0, 0, xq)
            rstd(0, 1, "ln")
            low_inputs(0, 1, xq)
            low0(0, 0)
            for hf in range(2):
                rstd(1, hf, "ln")
            for hf in range(2):
                low_inputs(1, hf, x0)
            nc.gpsimd.memset(part(QU, 4096), 0.0).then_inc(sem("pads_zeroed"), 1)
            pool.wait_ge(sem("pads_zeroed"), 1)
            with pool.Fori(0, E0 // NB0) as it:
                for j in range(NB0):
                    low0(it * NB0 + (j + 1), (j + 1) % NB0)
            def skips(hf):
                for p in pairs(hf):
                    last = nc.gpsimd.tensor_scalar(u[:, p, :], h[:, p, :], mv[:, p, 0:1], pw_out[:, 0, p:p + 1],
                                                   ALU.subtract, ALU.mult)
                last.then_inc(sem("skip_ready"), 1)

            nc.gpsimd.memset(part(QV, 4096), 0.0).then_inc(sem("pads_zeroed"), 1)
            pool.wait_ge(sem("pads_zeroed"), 2)
            nc.gpsimd.memset(part(RS, PAIRS * HB * TOK + AHEAD * HF * SLOT), 0.0).then_inc(sem("pads_zeroed"), 1)
            pool.wait_ge(sem("pads_zeroed"), 3)
            for hf in range(2):
                rstd(2, hf, "ln+norm")
            for p in range(PAIRS):
                await_read_out(pool, ("y0t", p))
            pool.wait_ge(sem("rstd_done"), 2 * 2 + 2)
            link(nc.gpsimd.memset(xT[C:C + 1, :, :], 1.0))
            for hf in range(2):
                pool.wait_ge(sem("rstd_done"), 2 * 2 + hf + 1)
                skips(hf)
            pool.wait_ge(sem("set2_loaded"), 16 * 12)
            for hf in range(2):
                rstd(3, hf, "rms")
                sl = slice(HP * hf, HP * hf + HP)
                link(nc.gpsimd.tensor_tensor(h[:, sl, :], h[:, sl, :], u[:, sl, :], ALU.add))
                nc.gpsimd.tensor_tensor(h[:, sl, :], h[:, sl, :],
                                        b2_row[:, :].unsqueeze(1).broadcast_to([128, HP, D]), ALU.add)\
                    .then_inc(sem("skip1_added"), 1)
            for hf in range(2):
                rstd(4, hf, "ln+norm")
            for hf in range(2):
                pool.wait_ge(sem("rstd_done"), 2 * 4 + hf + 1)
                skips(hf)
            for hf in range(2):
                await_read_out(pool, ("k2", hf, 0))
                imgs = slice(HI * hf, HI * hf + HI)
                nc.gpsimd.tensor_tensor(
                    kbd2[:, 0, imgs], by_image(k2[:, 0, half(hf)]).unsqueeze(2).broadcast_to([C, HI, 6, TOK]),
                    mask_head[:, :].unsqueeze(1).unsqueeze(3).broadcast_to([C, HI, 6, TOK]), ALU.mult)\
                    .then_inc(sem("keys2_masked_pool"), 1)
            for piece in range(2):
                low1(0, 0, piece)
            for hf in range(2):
                rstd(5, hf, "ln")
            for hf in range(2):
                low_inputs(5, hf, x1)
            low1(0, 0, 2)
            nc.gpsimd.tensor_tensor(h[:, :, :], h[:, :, :], u[:, :, :], ALU.add).then_inc(sem("skip2_added"), 1)
            with pool.Fori(0, E1 // NB1 - 1) as it:
                for j in range(NB1):
                    for piece in range(3):
                        low1(it * NB1 + (j + 1), (j + 1) % NB1, piece)
            for piece in range(3):
                low1(E1 - 1, NB1 - 1, piece)

        @block.tensor
        def _(pe):
            mm = nc.tensor.matmul

            def transposes(n, hf):
                pe.wait_ge(sem("xn_done"), 2 * n + hf + 1)
                for c in range(2):
                    b = fill(pe, (f"n{n}", hf, c))
                    for q, p in enumerate(pairs(hf)):
                        first, rows = AB[c] if n in SPLIT_NORMS else (c * C, C)
                        last = nc.tensor.transpose(b[0:rows, q * 128:(q + 1) * 128],
                                                   xn[:, p, first:first + rows], ident[:, :])
                    full(last, (f"n{n}", hf, c))

            def keep_warm(key, n=4):
                b = fill(pe, key)
                for _ in range(n):
                    mm(b[:, 0:128], ident[:, :], ident[:, :], start=True, stop=True)

            def await_xT(n, hf):
                for c in range(2):
                    await_read_out(pe, (f"n{n}", hf, c))

            def feature_major(key, w, c0, width, src, hf):
                b = fill(pe, key)
                o = by_image(b[0:width, 0:HT])
                for kc in range(2):
                    last = mm(o, w[0:C, kc, c0:c0 + width], real(src, kc, hf, C), start=kc == 0, stop=kc == 1)
                full(last, key)

            def token_major(key, src, w, p, biased):
                b = fill(pe, key)
                n = w.shape[2]
                for kc in range(2):
                    rows = C + (1 if kc and biased else 0)
                    last = mm(b[:, 0:n], src[0:rows, kc, pair_cols(p)], w[0:rows, kc, :],
                              start=kc == 0, stop=kc == 1)
                full(last, key)

            def hidden_mm(o, w, x, hf):
                for k, (i, j) in enumerate(PARTS):
                    rows = CB if i == 3 else 128
                    last = mm(o, w[0:rows, i, :], real(x, j, hf, rows), start=k == 0, stop=k == len(PARTS) - 1)
                return last

            def embed(p):
                for i, (first, _) in enumerate(PATCH_LOADS):
                    if p == first:
                        pe.wait_ge(sem(f"patches{i}_loaded"), 16)
                b = fill(pe, ("tok", p))
                for k in range(PATCH_CHUNKS):
                    last = mm(b[:, 0:D], xp[:, p, k, :], tokw[:, k, :], start=k == 0, stop=k == PATCH_CHUNKS - 1)
                full(last, ("tok", p))

            def queries0(hf):
                keep_warm(("q0", hf, 0), 2)
                pe.wait_ge(sem("x_low0"), hf + 1)
                for c in range(2):
                    b = fill(pe, ("q0", hf, c))
                    full(hidden_mm(by_image(b[0:C, 0:HT]), wq[:, :, c * C:(c + 1) * C], xq, hf), ("q0", hf, c))

            def keys_values0(p):
                b = fill(pe, ("kv0", p))
                for k, (i, j) in enumerate(PARTS):
                    rows = CB if i == 3 else 128
                    last = mm(b[:, 0:2 * D], xq[0:rows, j, pair_cols(p)], wq[0:rows, i, D:3 * D],
                              start=k == 0, stop=k == len(PARTS) - 1)
                full(last, ("kv0", p))

            def keys_by_values0(hf):
                keep_warm(("kTv", hf, 0, 0))
                for p in pairs(hf):
                    await_read_out(pe, ("kv0", p))
                for pp in range(2):
                    for par in range(2):
                        key = ("kTv", hf, pp, par)
                        b = fill(pe, key)
                        rows = slice(par * SLOT, par * SLOT + TOK)
                        for q in range(2):
                            for c in range(2):
                                p = HP * hf + 2 * pp + q
                                at = (2 * q + c) * C
                                last = mm(b[0:C, at:at + C], kv[rows, p, c * C:(c + 1) * C],
                                          kv[rows, p, D + c * C:D + (c + 1) * C], start=True, stop=True)
                        full(last, key)

            def attend0(hf):
                keep_warm(("o0", hf, 0), 3)
                pe.wait_ge(sem("kv_masked"), 4 * (hf + 1))
                for c in range(2):
                    await_read_out(pe, ("q0", hf, c))
                    b = fill(pe, ("o0", hf, c))
                    for i in range(HI):
                        at = hf * HT + i * TOK
                        last = mm(b[0:C, i * TOK:(i + 1) * TOK], gkv[:, HI * hf + i, c, :], gq[:, c, at:at + TOK],
                                  start=True, stop=True)
                    full(last, ("o0", hf, c))

            def project(attended, wo, w, hf):
                for c in range(2):
                    await_read_out(pe, (attended, hf, c))
                for p in pairs(hf):
                    token_major((wo, p), oT, w, p, True)

            pe.wait_ge(sem("tok_w_loaded"), 16)
            for p in range(HP + 2):
                embed(p)
            pe.wait_ge(sem("set0_loaded"), 16 * 5)
            pe.wait_ge(sem("pool_init"), 1)
            transposes(0, 0)
            for p in range(HP + 2, PAIRS):
                embed(p)
            queries0(0)
            for p in pairs(0):
                keys_values0(p)
                if p == HP - 2:
                    transposes(0, 1)
            keys_by_values0(0)
            queries0(1)
            for p in pairs(1):
                keys_values0(p)
            attend0(0)
            keys_by_values0(1)
            keep_warm(("proj0", 0), 2)
            project("o0", "proj0", wproj0, 0)
            attend0(1)
            keep_warm(("proj0", HP))
            project("o0", "proj0", wproj0, 1)

            pe.wait_ge(sem("set1_loaded"), 16 * 5)
            for hf in range(2):
                keep_warm(("n1", hf, 0))
                transposes(1, hf)
                keep_warm(("gate0", hf))
                await_xT(1, hf)
                key = ("gate0", hf)
                b = fill(pe, key)
                for q, p in enumerate(pairs(hf)):
                    for kc in range(2):
                        rows = CB if kc else 128
                        last = mm(b[:, q * E0:(q + 1) * E0], xT[0:rows, kc, pair_cols(p)], gate0w[0:rows, kc, :],
                                  start=kc == 0, stop=kc == 1)
                full(last, key)

            def sums_mm(hf, w, x):
                ya, yb = y[hf, 0], y[hf, 1]
                high, low = x
                for o, part_, operand in ((ya, w[:, 0:128], high), (ya, w[:, 2 * D - 128:2 * D], high),
                                          (ya, w[:, 0:128], low), (yb, w[:, 128:256], high),
                                          (yb[0:CB, :], w[:, 128:128 + CB], low)):
                    last = mm(o, part_, operand[:, :], start=False, stop=False, skip_group_check=True)
                return last

            y = {(hf, c): bank[2 * hf + c][:, 0:HT] for hf in range(2) for c in range(2)}

            def hidden0(x, buf, hf):
                for name in "ug":
                    b, n = uses[name, hf]
                    pe.wait_ge(bank_free[b], x + n)
                for name, at in (("u", 0), ("g", HID0)):
                    b, n = uses[name, hf]
                    o = by_image(bank[b][:, 0:HT])
                    hidden_mm(o, up0s[buf][:, :, at:at + HID0], x0, hf).then_inc(bank_full[b], 1)

            def sums0(x, buf, hf):
                pe.wait_ge(sem(f"act0_ready{hf}"), x * 3 + 2)
                return sums_mm(hf, down0s[buf][:, 0, :], a0[buf % 2][hf])

            pe.wait_ge(sem("expert0_low"), 3)
            for hf in range(2):
                pe.wait_ge(sem("x_low1"), hf + 1)
                hidden0(0, 0, hf)
            keep_warm(("wT0", 0), 12)
            pe.wait_ge(sem("routed"), 1)
            for hf in range(2):
                b = fill(pe, ("wT0", hf))
                for q in range(HP):
                    at = (HP * hf + q) * E0
                    last = nc.tensor.transpose(b[0:E0, q * 128:(q + 1) * 128], rt0["w"][:, at:at + E0], ident[:, :])
                full(last, ("wT0", hf))
            keep_warm(("y0", 0, 1))
            for hf in range(2):
                await_read_out(pe, ("wT0", hf))
            for hf in range(2):
                for c in range(2):
                    fill(pe, ("y0", hf, c))
                    full(mm(y[hf, c], bd0[:, c * 128:(c + 1) * 128], wT[0:E0, half(hf)], start=True, stop=False,
                            skip_group_check=True), ("y0", hf, c))
            with pe.Fori(0, E0 // NB0) as it:
                for j in range(NB0):
                    x, buf = it * NB0 + (j + 1), (j + 1) % NB0
                    pe.wait_ge(sem("expert0_low"), x * 3 + 3)
                    hidden0(x, buf, 0)
                    sums0(it * NB0 + j, j, 0)
                    hidden0(x, buf, 1)
                    sums0(it * NB0 + j, j, 1).then_inc(sem("expert0_done"), 1)
            sums0(E0, E0 % NB0, 0).then_inc(sem("sums0_done"), 1)
            sums0(E0, E0 % NB0, 1).then_inc(sem("expert0_done"), 1)

            def sums_token_major(tag):
                for p in range(PAIRS):
                    if p % HP == 0:
                        for c in range(2):
                            await_read_out(pe, (tag, p // HP, c))
                    b = fill(pe, (tag + "t", p))
                    nc.tensor.transpose(b[:, 0:128], xT[:, 0, pair_cols(p)], ident[:, :])
                    full(mm(b[:, 128:D], xT[:, 1, pair_cols(p)], fold[:, :], start=True, stop=True),
                         (tag + "t", p))

            sums_token_major("y0")

            pe.wait_ge(sem("set2_loaded"), 16 * 12)
            for m in range(4):
                b = fill(pe, ("rel_w", m))
                full(mm(b[:, 0:REL], wposT[:, m * 128:(m + 1) * 128], basis[:, :], start=True, stop=True),
                     ("rel_w", m))
            for hf in range(2):
                keep_warm(("n2", hf, 0))
                transposes(2, hf)
            for hf in range(2):
                await_xT(2, hf)
                for m in range(4):
                    feature_major(("q1", hf, m), wq1, m * 128, 128, xT, hf)
                for m in range(4):
                    feature_major(("k1", hf, m), wk1, m * 128, 128, xT, hf)
                for m in range(4):
                    await_read_out(pe, ("rel_w", m))
                    await_read_out(pe, ("q1", hf, m))
                for p in pairs(hf):
                    for s in range(2):
                        b = fill(pe, ("rel", p, s))
                        for m in (2 * s, 2 * s + 1):
                            at = (m % 2) * 2 * REL
                            last = mm(b[:, at:at + 2 * REL], qv[:, m, pair_cols(p)],
                                      rbd[:, m].rearrange("p e r -> p (e r)"), start=True, stop=True)
                        full(last, ("rel", p, s))
                for q in range(2):
                    key = ("v1", hf, q)
                    b = fill(pe, key)
                    for i in range(4):
                        img = HI * hf + 4 * q + i
                        for par in range(2):
                            for kc in range(2):
                                last = mm(b[par * SLOT:(par + 1) * SLOT, i * C:(i + 1) * C],
                                          xT[0:C, kc, img * SLOT:(img + 1) * SLOT],
                                          wv1[:, kc, par * C:(par + 1) * C], start=kc == 0, stop=kc == 1,
                                          skip_group_check=True)
                    full(last, key)

            def scores1(p):
                if p % HP == 0:
                    for m in range(4):
                        await_read_out(pe, ("k1", p // HP, m))
                b = fill(pe, ("s1", p))
                for m in range(4):
                    for par in range(2):
                        img = 2 * p + par
                        last = mm(b[par * SLOT:(par + 1) * SLOT, m * 2 * TOK:(m + 1) * 2 * TOK],
                                  qu[:, m, img * SLOT:(img + 1) * SLOT],
                                  kbd1[:, m, img].rearrange("p e j -> p (e j)"), start=True, stop=True,
                                  skip_group_check=True)
                full(last, ("s1", p))

            for p in range(AHEAD):
                scores1(p)
            def attended_columns(tag, av, hf):
                for p in pairs(hf):
                    await_read_out(pe, (av, p))
                for c in range(2):
                    b = fill(pe, (tag, hf, c))
                    for q, p in enumerate(pairs(hf)):
                        last = nc.tensor.transpose(b[0:C, q * 128:(q + 1) * 128], xn[:, p, c * C:(c + 1) * C],
                                                   ident[:, :])
                    full(last, (tag, hf, c))

            def attend1(p):
                await_read_out(pe, ("p1t", p))
                if p % 2 == 0:
                    await_read_out(pe, ("v1", p // HP, (p % HP) // 2))
                b = fill(pe, ("av1", p))
                for m in range(4):
                    for par in range(2):
                        img = 2 * p + par
                        last = mm(b[par * SLOT:(par + 1) * SLOT, m * 2 * HBV:(m + 1) * 2 * HBV],
                                  pt1[:, p % 2, m * 128 + par * SLOT:m * 128 + (par + 1) * SLOT],
                                  vbd1[:, img * 4 + m].rearrange("p e d -> p (e d)"), start=True, stop=True,
                                  skip_group_check=True)
                full(last, ("av1", p))

            for p in range(PAIRS):
                pe.wait_ge(sem("exp1_done"), p + 1)
                b = fill(pe, ("p1t", p))
                for m in range(4):
                    last = nc.tensor.transpose(b[:, m * 128:(m + 1) * 128],
                                               probs1[:, p % AHEAD, 2 * m:2 * m + 2].rearrange("p h j -> p (h j)"),
                                               ident[:, :])
                full(last, ("p1t", p))
                if p + AHEAD < PAIRS:
                    scores1(p + AHEAD)
                if p:
                    attend1(p - 1)
                if p == HP + 1:
                    attended_columns("o1t", "av1", 0)
                if p == HP + 2:
                    project("o1t", "wo1", wout1, 0)
            attend1(PAIRS - 1)
            attended_columns("o1t", "av1", 1)
            project("o1t", "wo1", wout1, 1)

            def ffn_hidden(hf):
                await_xT(3, hf)
                for m in range(3):
                    feature_major(("f1", hf, m), w1a, m * 128, 128, xT, hf)

            def ffn_out(hf, places):
                for m in range(3):
                    await_read_out(pe, ("f1", hf, m))
                for p in pairs(hf)[places]:
                    b = fill(pe, ("f2", p))
                    for m in range(3):
                        last = mm(b[:, 0:D], g1[:, m, pair_cols(p)], w2a[:, m, :], start=m == 0, stop=m == 2)
                    full(last, ("f2", p))

            transposes(3, 0)
            ffn_hidden(0)
            transposes(3, 1)
            ffn_out(0, slice(0, HP))
            ffn_hidden(1)
            ffn_out(1, slice(0, 2))
            transposes(4, 0)
            ffn_out(1, slice(2, HP))
            pe.wait_ge(sem("set3_loaded"), 16 * 6)
            for hf in range(2):
                await_xT(4, hf)
                for c in range(2):
                    feature_major(("q2", hf, c), wqk2, c * C, C, xT, hf)
                for c in range(2):
                    feature_major(("k2", hf, c), wqk2, D + c * C, C, xT, hf)
                for q in range(2):
                    if (hf, q) == (0, 1):
                        transposes(4, 1)
                    key = ("v2", hf, q)
                    b = fill(pe, key)
                    for i in range(4):
                        img = HI * hf + 4 * q + i
                        for par in range(2):
                            for kc in range(2):
                                rows = C + kc
                                last = mm(b[par * SLOT:(par + 1) * SLOT, i * C:(i + 1) * C],
                                          xT[0:rows, kc, img * SLOT:(img + 1) * SLOT],
                                          wv2[0:rows, kc, par * C:(par + 1) * C], start=kc == 0, stop=kc == 1,
                                          skip_group_check=True)
                    full(last, key)

            def scores2(p):
                if p % HP == 0:
                    for c in range(2):
                        await_read_out(pe, ("q2", p // HP, c))
                    pe.wait_ge(sem("keys2_masked_pool"), p // HP + 1)
                    pe.wait_ge(sem("keys2_masked_dve"), p // HP + 1)
                b = fill(pe, ("s2", p))
                for c in range(2):
                    for par in range(2):
                        img = 2 * p + par
                        last = mm(b[par * SLOT:(par + 1) * SLOT, c * 6 * TOK:(c + 1) * 6 * TOK],
                                  q2[:, c, img * SLOT:(img + 1) * SLOT],
                                  kbd2[:, c, img].rearrange("p e j -> p (e j)"), start=True, stop=True,
                                  skip_group_check=True)
                full(last, ("s2", p))

            keep_warm(("s2", 0), 6)
            for p in range(AHEAD):
                scores2(p)
            def attend2(p):
                for s in range(2):
                    await_read_out(pe, ("p2t", p, s))
                if p % 2 == 0:
                    await_read_out(pe, ("v2", p // HP, (p % HP) // 2))
                b = fill(pe, ("av2", p))
                for m in range(6):
                    for par in range(2):
                        img = 2 * p + par
                        last = mm(b[par * SLOT:(par + 1) * SLOT, m * 2 * HFD:(m + 1) * 2 * HFD],
                                  pt2[:, p % 2, m * 128 + par * SLOT:m * 128 + (par + 1) * SLOT],
                                  vbd2[:, img * 6 + m].rearrange("p e d -> p (e d)"), start=True, stop=True,
                                  skip_group_check=True)
                full(last, ("av2", p))

            for p in range(PAIRS):
                keep_warm(("p2t", p, 0), 1)
                pe.wait_ge(sem("exp2_done"), p + 1)
                for s in range(2):
                    b = fill(pe, ("p2t", p, s))
                    for m in range(3):
                        h0 = 2 * (3 * s + m)
                        last = nc.tensor.transpose(b[:, m * 128:(m + 1) * 128],
                                                   probs2[:, p % AHEAD, h0:h0 + 2].rearrange("p h j -> p (h j)"),
                                                   ident[:, :])
                    full(last, ("p2t", p, s))
                if p + AHEAD < PAIRS:
                    scores2(p + AHEAD)
                if p:
                    attend2(p - 1)
                if p == HP + 1:
                    attended_columns("o2t", "av2", 0)
                if p == HP + 2:
                    project("o2t", "wo2", wout2, 0)
            attend2(PAIRS - 1)
            attended_columns("o2t", "av2", 1)
            project("o2t", "wo2", wout2, 1)

            def hidden1(it, buf, n):
                b, base = uses["hid", n % 4]
                m, hf = n % M1, n // M1
                pe.wait_ge(bank_free[b], it * (NB1 * turns) + (base + buf * turns + n // 4))
                o = by_image(bank[b][:, 0:HT])
                hidden_mm(o, up1s[buf][:, :, m * 128:(m + 1) * 128], x1, hf).then_inc(bank_full[b], 1)

            for hf in range(2):
                keep_warm(("n5", hf, 0))
                transposes(5, hf)
                keep_warm(("gate1", hf))
                await_xT(5, hf)
                key = ("gate1", hf)
                b = fill(pe, key)
                for q, p in enumerate(pairs(hf)):
                    for kc in range(2):
                        rows = CB if kc else 128
                        last = mm(b[:, q * E1:(q + 1) * E1], xT[0:rows, kc, pair_cols(p)], gate1w[0:rows, kc, :],
                                  start=kc == 0, stop=kc == 1)
                full(last, key)

            def sums1(it, buf, n):
                m, hf = n % M1, n // M1
                pe.wait_ge(sem("hid1_ready"), it * (3 * NB1 * 2 * M1) + 3 * (buf * 2 * M1 + n + 1))
                last = sums_mm(hf, down1s[buf][:, m, :], hs[n % 4])
                if n == M1 - 1:
                    last.then_inc(sem("sums1_done"), 1)
                if n == 2 * M1 - 1:
                    last.then_inc(sem("expert1_done"), 1)

            def expert1(it, buf, next_it):
                for n in range(2 * M1):
                    ahead = n + 3
                    if ahead < 2 * M1:
                        hidden1(it, buf, ahead)
                    elif next_it is not None:
                        nxt = (buf + 1) % NB1
                        if ahead == 2 * M1:
                            pe.wait_ge(sem("expert1_low"), it * (3 * NB1) + 3 * (buf + 2))
                        hidden1(next_it, nxt, ahead - 2 * M1)
                    sums1(it, buf, n)

            pe.wait_ge(sem("x_low5"), 1)
            pe.wait_ge(sem("expert1_low"), 2)
            for n in range(3):
                hidden1(0, 0, n)
            pe.wait_ge(sem("x_low5"), 2)
            keep_warm(("wT1", 0), 8)
            pe.wait_ge(sem("routed"), 2)
            for hf in range(2):
                b = fill(pe, ("wT1", hf))
                for q in range(HP):
                    at = (HP * hf + q) * E1
                    last = nc.tensor.transpose(b[0:E1, q * 128:(q + 1) * 128], rt1["w"][:, at:at + E1], ident[:, :])
                full(last, ("wT1", hf))
            keep_warm(("y1", 0, 1), 3)
            for hf in range(2):
                await_read_out(pe, ("wT1", hf))
            b = fill(pe, "first_row1")
            full(mm(b[:, 0:HT], first_row[:, :], wT[0:E1, half(0)], start=True, stop=True), "first_row1")
            for hf in range(2):
                for c in range(2):
                    fill(pe, ("y1", hf, c))
                    full(mm(y[hf, c], b2m[:, c * 128:(c + 1) * 128], wT[0:E1, half(hf)], start=True, stop=False,
                            skip_group_check=True), ("y1", hf, c))
            pe.wait_ge(sem("expert1_low"), 3)
            with pe.Fori(0, E1 // NB1 - 1) as it:
                expert1(it, 0, it)
                expert1(it, 1, it + 1)
            expert1(E1 // NB1 - 1, 0, E1 // NB1 - 1)
            expert1(E1 // NB1 - 1, 1, None)
            sums_token_major("y1")

        @block.scalar
        def _(act):
            activation = nc.scalar.activation
            act.dma_start(tokw, a["tok_w"]).then_inc(sem("tok_w_loaded"), 16)

            def columns(n, hf, scale=None, bias=None, chunk=0):
                key = (f"n{n}", hf, chunk)
                b = read(act, key)
                if n in SPLIT_NORMS:
                    free(activation(xT[:, 0, pad_half(hf)], b[:, :], ACT.Identity,
                                    scale=col128(scale, 0) if scale else 1.0,
                                    bias=col128(bias, 0) if bias else 0.0), key)
                    return
                free(activation(xT[0:C, chunk, pad_half(hf)], b[0:C, :], ACT.Identity,
                                scale=col96(scale, chunk) if scale else 1.0,
                                bias=col96(bias, chunk) if bias else 0.0), key)

            def embedded(p):
                b = read(act, ("tok", p))
                free(activation(h[:, p, :], b[:, 0:D], ACT.Copy), ("tok", p))

            def queries0(hf):
                for c in range(2):
                    b = read(act, ("q0", hf, c))
                    free(activation(gq[:, c, half(hf)], b[0:C, 0:HT], ACT.Gelu), ("q0", hf, c))

            def keys_values0(p):
                b = read(act, ("kv0", p))
                free(activation(kv[:, p, :], b[:, 0:2 * D], ACT.Copy), ("kv0", p))

            def keys_by_values0(hf):
                for pp in range(2):
                    for par in range(2):
                        key = ("kTv", hf, pp, par)
                        b = read(act, key)
                        img = HI * hf + 4 * pp + par
                        free(activation(gkr[:, img:img + 3:2], b[0:C, 0:4 * C].rearrange(
                            "p (q c e) -> p q c e", q=2, c=2), ACT.Gelu, scale=float(HFD) ** -0.5), key)

            def high_inputs(n, hf, x):
                for c in range(2):
                    await_read_out(act, (f"n{n}", hf, c))
                activation(x[:, 0, pad_half(hf)], xT[:, 0, pad_half(hf)], ACT.Copy)
                activation(x[0:CB, 1, pad_half(hf)], xT[0:CB, 1, pad_half(hf)], ACT.Copy)\
                    .then_inc(sem(f"x_high{n}"), 1)

            def high_up(w, src, chunk):
                if chunk == 0:
                    return activation(w[:, 0, :], src[:, 0, :], ACT.Copy)
                for at in (0, CB):
                    last = activation(w[at:at + CB, 1, :], src[0:CB, 1, :], ACT.Copy)
                return last

            for p in range(HP):
                embedded(p)
            act.wait_ge(sem("set0_loaded"), 16 * 5)
            act.wait_ge(sem("pool_init"), 1)
            high_up(wq, wqkv0, 0)
            high_up(wq, wqkv0, 1).then_inc(sem("qkv0_high"), 1)
            for p in range(HP, HP + 2):
                embedded(p)
            columns(0, 0)
            high_inputs(0, 0, xq)
            for p in range(HP + 2, PAIRS):
                embedded(p)
            queries0(0)
            keys_values0(1)
            columns(0, 1)
            high_inputs(0, 1, xq)
            keys_values0(3)
            keys_by_values0(0)
            queries0(1)
            for p in (5, 7):
                keys_values0(p)
            keys_by_values0(1)

            def high0(x, buf, loads):
                act.wait_ge(sem(f"expert0_loaded{buf}"), loads)
                for chunk in range(2):
                    high_up(up0s[buf], up0[buf], chunk)
                activation(down0s[buf][:, :, 0:D], by_chunk(down0[buf]), ACT.Copy).then_inc(sem("expert0_high"), 1)

            def silu(x, buf, hf):
                b, n = uses["u", hf]
                act.wait_ge(bank_full[b], x + (n + 1))
                activation(s0[hf], bank[b][:, 0:HT], ACT.Silu, bias=bias0[buf][:, 0:1])\
                    .then_inc(bank_free[b], 1)

            high0(0, 0, 48)
            act.wait_ge(sem("pool_init"), 1)
            for hf in range(2):
                columns(1, hf)
                high_inputs(1, hf, x0)
            for hf in range(2):
                await_read_out(act, ("gate0", hf))
                at = slice(hf * HP * E0, (hf + 1) * HP * E0)
                activation(rt0["e"][:, at], rt0["s"][:, at], ACT.Exp).then_inc(sem("route_exp"), 1)
            high0(1, 1, 48)
            act.wait_ge(sem("bias0_loaded0"), 16)
            for hf in range(2):
                silu(0, 0, hf)
            for hf in range(2):
                b = read(act, ("wT0", hf))
                free(activation(by_image(wT[0:E0, half(hf)]), b[0:E0, :].rearrange(
                    "p (i t) -> p i t", t=SLOT)[:, :, 0:TOK], ACT.Copy), ("wT0", hf))

            def expert0(it, j, prepare):
                x, buf, ahead = it * NB0 + (j + 1), (j + 1) % NB0, j + 3
                act.wait_ge(sem(f"bias0_loaded{buf}"), it * 16 + (16 if buf else 32))
                silu(x, buf, 0)
                if prepare:
                    high0(it * NB0 + ahead, ahead % NB0, it * 48 + 48 * (2 if ahead >= NB0 else 1))
                silu(x, buf, 1)

            high0(2, 2, 48)
            with act.Fori(0, E0 // NB0 - 1) as it:
                activation(warm[:, :], warm[:, :], ACT.Silu)
                for j in range(NB0):
                    expert0(it, j, True)
            for j in range(NB0):
                expert0(E0 // NB0 - 1, j, j + 3 <= NB0)
            act.wait_ge(sem("set2_loaded"), 16 * 12)
            for hf in range(2):
                act.wait_ge(sem("expert0_done" if hf else "sums0_done"), E0 + 1 if hf else 1)
                for c in range(2):
                    b = read(act, ("y0", hf, c))
                    free(activation(real(xT, c, hf), by_image(b[:, 0:HT]), ACT.Identity,
                                    bias=col128("sbd", c)), ("y0", hf, c))

            columns(2, 0, "rms1_w")
            columns(2, 0, "rms1_w", chunk=1)
            columns(2, 1, "rms1_w")
            act.wait_ge(sem("pads_zeroed"), 3)
            for hf in range(2):
                for m in range(4):
                    b = read(act, ("q1", hf, m))
                    activation(real(qu, m, hf), by_image(b[:, 0:HT]), ACT.Identity, bias=col128("u", m))
                    free(activation(real(qv, m, hf), by_image(b[:, 0:HT]), ACT.Identity, bias=col128("v", m)),
                         ("q1", hf, m))
                if hf:
                    act.wait_ge(sem("rel_stored"), 16)
                for q, p in enumerate(pairs(hf)):
                    for s in range(2):
                        b = read(act, ("rel", p, s))
                        free(activation(relb[:, q, s * 4 * REL:(s + 1) * 4 * REL], b[:, 0:4 * REL], ACT.Copy),
                             ("rel", p, s))

            def softmax_exp1(p):
                act.wait_ge(sem("shifted1"), p + 1)
                x = probs1[:, p % AHEAD, :, 0:TOK]
                activation(x, x, ACT.Exp, scale=float(HD) ** -0.5).then_inc(sem("exp1_done"), 1)

            def attended(tag, hf):
                b = read(act, (tag, hf, 0))
                free(activation(oT[0:C, 0, pad_half(hf)], b[0:C, :], ACT.Copy), (tag, hf, 0))

            softmax_exp1(0)
            for p in range(PAIRS):
                if p + 1 < PAIRS:
                    softmax_exp1(p + 1)
                b = read(act, ("p1t", p))
                free(activation(pt1[:, p % 2, :], b[:, :], ACT.Copy), ("p1t", p))
                if p == HP + 1:
                    attended("o1t", 0)
            attended("o1t", 1)

            def ffn_hidden(hf):
                for m in range(3):
                    b = read(act, ("f1", hf, m))
                    free(activation(real(g1, m, hf), by_image(b[:, 0:HT]), ACT.Gelu, bias=col128("b1", m)),
                         ("f1", hf, m))

            columns(3, 0, "rms2_w")
            columns(3, 0, "rms2_w", chunk=1)
            ffn_hidden(0)
            columns(3, 1, "rms2_w")
            ffn_hidden(1)
            columns(4, 0, "ln1_w", "ln1_b")
            for hf in range(2):
                for c in range(2):
                    b = read(act, ("q2", hf, c))
                    free(activation(real(q2, c, hf), by_image(b[0:C, 0:HT]), ACT.Identity, bias=col96("q_b", c)),
                         ("q2", hf, c))
                for c in range(2):
                    b = read(act, ("k2", hf, c))
                    free(activation(k2[:, c, half(hf)], b[0:C, 0:HT], ACT.Identity, bias=col96("k_b", c)),
                         ("k2", hf, c))
                if hf == 0:
                    columns(4, 1, "ln1_w", "ln1_b")

            def softmax_exp2(p):
                await_read_out(act, ("s2", p))
                x = probs2[:, p % AHEAD, :, 0:TOK]
                activation(x, x, ACT.Exp, scale=float(HFD) ** -0.5).then_inc(sem("exp2_done"), 1)

            def high1(x, buf, piece):
                if piece < 2:
                    last = high_up(up1s[buf], up1[buf], piece)
                else:
                    last = activation(down1s[buf][:, :, 0:D], by_chunk(down1[buf]), ACT.Copy)
                last.then_inc(sem("expert1_high"), 1)

            softmax_exp2(0)
            for p in range(PAIRS):
                if p + 1 < PAIRS:
                    softmax_exp2(p + 1)
                for s in range(2):
                    b = read(act, ("p2t", p, s))
                    free(activation(pt2[:, p % 2, s * 384:(s + 1) * 384], b[:, 0:384], ACT.Copy), ("p2t", p, s))
                if p == HP + 1:
                    attended("o2t", 0)
                if p == HP + 2:
                    act.wait_ge(sem("expert1_loaded0"), 48)
                    for piece in range(2):
                        high1(0, 0, piece)
            attended("o2t", 1)
            high1(0, 0, 2)
            for hf in range(2):
                columns(5, hf, "ln2_w", "ln2_b")
                high_inputs(5, hf, x1)
            for hf in range(2):
                await_read_out(act, ("gate1", hf))
                at = slice(hf * HP * E1, (hf + 1) * HP * E1)
                activation(rt1["e"][:, at], rt1["s"][:, at], ACT.Exp).then_inc(sem("route_exp"), 1)
            act.wait_ge(sem("w0_stored"), 16)
            for hf in range(2):
                b = read(act, ("wT1", hf))
                free(activation(by_image(wT[0:E1, half(hf)]), b[0:E1, :].rearrange(
                    "p (i t) -> p i t", t=SLOT)[:, :, 0:TOK], ACT.Copy), ("wT1", hf))

            def expert1(it, buf, prepare_next):
                act.wait_ge(sem(f"bias1_loaded{buf}"), it * 16 + 16)
                for n in range(2 * M1):
                    b, base = uses["hid", n % 4]
                    m = n % M1
                    act.wait_ge(bank_full[b], it * (NB1 * turns) + (base + buf * turns + n // 4 + 1))
                    activation(hg[n % 4], bank[b][:, 0:HT], ACT.Gelu, bias=bias1[buf][:, m:m + 1])\
                        .then_inc(bank_free[b], 1)
                    if prepare_next and n in (3, 5, 7):
                        nxt = (buf + 1) % NB1
                        if n == 3:
                            act.wait_ge(sem(f"expert1_loaded{nxt}"), it * 48 + (48 if nxt else 96))
                        high1(it * NB1 + (buf + 1), nxt, (n - 3) // 2)

            with act.Fori(0, E1 // NB1 - 1) as it:
                for buf in range(NB1):
                    expert1(it, buf, True)
            for buf in range(NB1):
                expert1(E1 // NB1 - 1, buf, buf < NB1 - 1)
            for hf in range(2):
                act.wait_ge(sem("expert1_done" if hf else "sums1_done"), E1)
                for c in range(2):
                    b = read(act, ("y1", hf, c))
                    free(activation(real(xT, c, hf), by_image(b[:, 0:HT]), ACT.Copy), ("y1", hf, c))

        @block.vector
        def _(dve):
            tt, ts, stt, reduce = (nc.vector.tensor_tensor, nc.vector.tensor_scalar,
                                   nc.vector.scalar_tensor_tensor, nc.vector.tensor_reduce)
            step = [0]

            def link(ins):
                step[0] += 1
                ins.then_inc(sem("dve_step"), 1)
                dve.wait_ge(sem("dve_step"), step[0])

            bn = [0]

            def statistics(x, hf, tag=None):
                first = HP * hf
                for i in range(HP + 2):
                    if tag and i < HP:
                        p = first + i
                        b = read(dve, (tag, p))
                        free(tt(x[:, p, :], b[:, 0:D], x[:, p, :], ALU.add), (tag, p))
                    if 1 <= i <= HP:
                        p = first + i - 1
                        await_read_out(dve, (tag or "tok", p))
                        nc.vector.bn_stats(stats[:, p, :], x[:, p, :]).then_inc(sem("bn_done"), 1)
                    if i >= 2:
                        p = first + i - 2
                        bn[0] += 1
                        dve.wait_ge(sem("bn_done"), bn[0])
                        last = nc.vector.bn_aggr(mv[:, p, :], stats[:, p, :])
                last.then_inc(sem("stats_done"), 1)

            def normalize(n, hf, kind):
                dve.wait_ge(sem("rstd_done"), 2 * n + hf + 1)
                for p in pairs(hf):
                    mean = mv[:, p, 0:1]
                    first, second = pw_out[:, 0, p:p + 1], pw_out[:, 1, p:p + 1]
                    if kind == "ln":
                        last = ts(xn[:, p, :], rows[n][:, p, :], mean, first, ALU.subtract, ALU.mult)
                    elif kind == "ln+norm":
                        last = ts(xn[:, p, :], rows[n][:, p, :], mean, second, ALU.subtract, ALU.mult)
                    else:
                        last = ts(xn[:, p, :], rows[n][:, p, :], first, None, ALU.mult)
                last.then_inc(sem("xn_done"), 1)

            def columns(n, hf, scale=None, bias=None):
                key = (f"n{n}", hf, 1)
                b = read(dve, key)
                if n in (0, 1):
                    free(nc.vector.tensor_copy(xT[0:CB, 1, pad_half(hf)], b[0:CB, :]), key)
                    return
                if n == 5:
                    free(ts(xT[0:CB, 1, pad_half(hf)], b[0:CB, :], col128(scale, 1)[0:CB, :],
                            col128(bias, 1)[0:CB, :], ALU.mult, ALU.add), key)
                    return
                if scale and bias:
                    last = ts(xT[0:C, 1, pad_half(hf)], b[0:C, :], col96(scale, 1), col96(bias, 1), ALU.mult, ALU.add)
                elif scale:
                    last = ts(xT[0:C, 1, pad_half(hf)], b[0:C, :], col96(scale, 1), None, ALU.mult)
                else:
                    last = nc.vector.tensor_copy(xT[0:C, 1, pad_half(hf)], b[0:C, :])
                free(last, key)

            rows = {0: h, 1: h, 2: h, 3: u, 4: h, 5: u}

            def keys_values0(hf):
                for p in pairs(hf):
                    if p % 2 == 0:
                        b = read(dve, ("kv0", p))
                        free(nc.vector.tensor_copy(kv[:, p, :], b[:, 0:2 * D]), ("kv0", p))

            def own_blocks(hf):
                for pp in range(2):
                    for par in range(2):
                        await_read_out(dve, ("kTv", hf, pp, par))
                        img = HI * hf + 4 * pp + par
                        blocks = gkr[:, img:img + 3:2].rearrange("p i c (h e) -> p i c h e", e=HFD)
                        kept = gkv[:, img:img + 3:2].rearrange("p i c (h e) -> p i c h e", e=HFD)
                        for i in range(2):
                            last = tt(kept[:, i], blocks[:, i], mask_head[:, :].unsqueeze(1).unsqueeze(3)
                                      .broadcast_to([C, 2, 6, HFD]), ALU.mult)
                        last.then_inc(sem("kv_masked"), 1)

            def attended0(hf):
                for c in range(2):
                    b = read(dve, ("o0", hf, c))
                    free(nc.vector.tensor_copy(real(oT, c, hf), by_image(b[0:C, 0:HT])), ("o0", hf, c))

            statistics(h, 0)
            normalize(0, 0, "ln")
            dve.wait_ge(sem("pool_init"), 1)
            columns(0, 0)
            statistics(h, 1)
            normalize(0, 1, "ln")
            keys_values0(0)
            columns(0, 1)
            dve.wait_ge(sem("set0_loaded"), 16 * 5)
            own_blocks(0)
            keys_values0(1)
            attended0(0)
            own_blocks(1)
            statistics(h, 0, "proj0")
            attended0(1)
            normalize(1, 0, "ln")
            statistics(h, 1, "proj0")
            columns(1, 0)
            normalize(1, 1, "ln")
            columns(1, 1)

            def by_token(rt, name, n, hf=None):
                sl = slice(0, PAIRS) if hf is None else slice(HP * hf, HP * hf + HP)
                return rt[name][:, 0:PAIRS * n].rearrange("p (q e) -> p q e", q=PAIRS)[:, sl]

            def spread(x, n):
                return x.unsqueeze(2).broadcast_to([128, x.shape[1], n])

            def shifted_logits(rt, key, n, hf, bias=None):
                b = read(dve, (key, hf))
                logits = b[:, 0:HP * n].rearrange("p (q e) -> p q e", q=HP)
                s, mx = by_token(rt, "s", n, hf), by_token(rt, "mx", 1, hf)[:, :, 0]
                if bias:
                    link(tt(s, logits, bias[:, :].unsqueeze(1).broadcast_to([128, HP, n]), ALU.add))
                    logits = s
                link(reduce(mx, logits, AX.X, ALU.max))
                free(tt(s, logits, spread(mx, n), ALU.subtract), (key, hf))

            def best(rt, x, n, k, run):
                le, eq, before, sel = (by_token(rt, name, n) for name in ("le", "eq", "before", "sel"))
                for q in range(PAIRS):
                    last = nc.vector.max(rt["top"][:, q * 8:(q + 1) * 8], x[:, q, :])
                link(last)
                kth = rt["top"][:, :].rearrange("p (q k) -> p q k", q=PAIRS)[:, :, k - 1]
                tt(le, x, spread(kth, n), ALU.is_le)
                link(tt(eq, x, spread(kth, n), ALU.is_equal))
                nc.vector.tensor_tensor_scan(rt["before"][:, 0:PAIRS * n], run, rt["eq"][:, 0:PAIRS * n], 0.0,
                                             ALU.mult, ALU.add)
                link(reduce(rt["les"][:, :], le, AX.X, ALU.add))
                link(stt(before, before, float(n - k), spread(rt["les"], n), ALU.add, ALU.is_le))
                link(tt(eq, eq, before, ALU.mult))
                link(stt(sel, le, 1.0, eq, ALU.subtract, ALU.subtract))

            dve.wait_ge(sem("set1_loaded"), 16 * 5)
            for hf in range(2):
                shifted_logits(rt0, "gate0", E0, hf, gate0_bias)
            dve.wait_ge(sem("route_exp"), 2)
            e, score, biased_score = (by_token(rt0, name, E0) for name in ("e", "score", "s"))
            link(reduce(rt0["sum"][:, :], e, AX.X, ALU.add))
            link(nc.vector.reciprocal(rt0["inv"][:, :], rt0["sum"][:, :]))
            link(tt(score, e, spread(rt0["inv"], E0), ALU.mult))
            link(tt(biased_score, score, route_bias[:, :].unsqueeze(1).broadcast_to([128, PAIRS, E0]), ALU.add))
            by_group = rt0["s"][:, :].rearrange("p (n two) -> p n two", two=2)
            link(reduce(rt0["gs"][:, :], by_group, AX.X, ALU.add))
            best(rt0, by_token(rt0, "gs", G0), G0, 4, run[:, 0:PAIRS * G0])
            link(ts(rt0["pen"][:, :], rt0["sel"][:, 0:PAIRS * G0], -BIG, -BIG, ALU.mult, ALU.add))
            link(tt(by_group, by_group, spread(rt0["pen"], 2), ALU.add))
            best(rt0, biased_score, E0, 4, run[:, PAIRS * G0:])
            stt(by_token(rt0, "w", E0), by_token(rt0, "sel", E0), -2.5, score, ALU.mult, ALU.mult)\
                .then_inc(sem("routed"), 1)

            def split(dst, src, ready, count):
                nc.vector.tensor_copy(dst[0][:, :], src).then_inc(ready, 1)
                dve.wait_ge(ready, count)
                tt(dst[1][:, :], src, dst[0][:, :].bitcast(F32), ALU.subtract).then_inc(ready, 1)

            def gate(x, buf, hf, dst):
                b, n = uses["g", hf]
                dve.wait_ge(bank_full[b], x + (n + 1))
                bu, nu = uses["u", hf]
                dve.wait_ge(bank_free[bu], x + (nu + 1))
                return stt(dst, bank[b][:, 0:HT], bias0[buf][:, 1:2], s0[hf], ALU.add, ALU.mult), bank_free[b]

            dve.wait_ge(sem("bias0_loaded0"), 16)
            for hf in range(2):
                ins, freed = gate(0, 0, hf, p0[hf])
                ins.then_inc(freed, 1)
                dve.wait_ge(freed, uses["g", hf][1] + 1)
                split(a0[0][hf], p0[hf], sem(f"act0_ready{hf}"), 1)
            with dve.Fori(0, E0 // NB0) as it:
                for j in range(NB0):
                    x, buf = it * NB0 + (j + 1), (j + 1) % NB0
                    dve.wait_ge(sem(f"w0_loaded{buf}"), it * 16 + 16)
                    dve.wait_ge(sem(f"bias0_loaded{buf}"), it * 16 + (16 if buf else 32))
                    for hf in range(2):
                        ins, freed = gate(x, buf, hf, f0[hf])
                        ins.then_inc(freed, 1)
                        dve.wait_ge(freed, x + (uses["g", hf][1] + 1))
                        tt(p0[hf], f0[hf], wb0[buf][:, half(hf)], ALU.mult).then_inc(sem(f"act0_ready{hf}"), 1)
                        dve.wait_ge(sem(f"act0_ready{hf}"), x * 3)
                        split(a0[buf % 2][hf], p0[hf], sem(f"act0_ready{hf}"), x * 3 + 1)
            for hf in range(2):
                statistics(h, hf, "y0t")

            for hf in range(2):
                normalize(2, hf, "ln+norm")
            dve.wait_ge(sem("set2_loaded"), 16 * 12)
            columns(2, 1, "rms1_w")
            for m in range(4):
                b = read(dve, ("rel_w", m))
                free(tt(rbd[:, m], b[:, 0:REL].unsqueeze(1).broadcast_to([128, 2, REL]),
                        mask_pair[:, :].unsqueeze(2).broadcast_to([128, 2, REL]), ALU.mult), ("rel_w", m))
            for hf in range(2):
                imgs = slice(HI * hf, HI * hf + HI)
                for m in range(4):
                    b = read(dve, ("k1", hf, m))
                    shape = [128, HI, 2, TOK]
                    free(tt(kbd1[:, m, imgs], by_image(b[:, 0:HT]).unsqueeze(2).broadcast_to(shape),
                            mask_pair[:, :].unsqueeze(1).unsqueeze(3).broadcast_to(shape), ALU.mult), ("k1", hf, m))
                for q in range(2):
                    b = read(dve, ("v1", hf, q))
                    shape = [128, 16, 2, HBV]
                    at = (HI * hf + 4 * q) * 4
                    free(tt(vbd1[:, at:at + 16], b[:, 0:4 * C].rearrange("p (n d) -> p n d", d=HBV)
                            .unsqueeze(2).broadcast_to(shape),
                            mask_pair[:, :].unsqueeze(1).unsqueeze(3).broadcast_to(shape), ALU.mult), ("v1", hf, q))

            def attended(tag, hf):
                b = read(dve, (tag, hf, 1))
                free(nc.vector.tensor_copy(oT[0:C, 1, pad_half(hf)], b[0:C, :]), (tag, hf, 1))

            def shifted1(p):
                if p % HP == 0:
                    dve.wait_ge(sem(f"rel_loaded{p // HP}"), 16 * 2 * HP)
                x = probs1[:, p % AHEAD, :, 0:TOK]
                b = read(dve, ("s1", p))
                free(tt(x, b[:, 0:HB * TOK].rearrange("p (h j) -> p h j", h=HB), rels[:, p], ALU.add), ("s1", p))
                await_read_out(dve, ("s1", p))
                mx = row_max[:, p, 0:HB]
                link(reduce(mx, x, AX.X, ALU.max))
                tt(x, x, mx.unsqueeze(2).broadcast_to([128, HB, TOK]), ALU.subtract).then_inc(sem("shifted1"), 1)

            def sums(p, probs, done, n):
                dve.wait_ge(sem(done), p + 1)
                link(reduce(row_sum[:, p, 0:n], probs[:, p % AHEAD, :, 0:TOK], AX.X, ALU.add))
                link(nc.vector.reciprocal(row_inv[:, p, 0:n], row_sum[:, p, 0:n]))

            def scaled(p, key, n):
                b = read(dve, key)
                shape = [128, n, D // n]
                ins = tt(xn[:, p, :].rearrange("p (h d) -> p h d", h=n),
                         b[:, 0:D].rearrange("p (h d) -> p h d", h=n),
                         row_inv[:, p, 0:n].unsqueeze(2).broadcast_to(shape), ALU.mult)
                free(ins, key)

            for p in range(2):
                shifted1(p)
            for p in range(PAIRS):
                if p + 2 < PAIRS:
                    shifted1(p + 2)
                sums(p, probs1, "exp1_done", HB)
                if p:
                    scaled(p - 1, ("av1", p - 1), HB)
                if p == HP + 1:
                    attended("o1t", 0)
                if p == HP + 2:
                    dve.wait_ge(sem("skip_ready"), 1)
                    statistics(u, 0, "wo1")
            scaled(PAIRS - 1, ("av1", PAIRS - 1), HB)

            attended("o1t", 1)
            normalize(3, 0, "rms")
            dve.wait_ge(sem("skip_ready"), 2)
            statistics(u, 1, "wo1")

            normalize(3, 1, "rms")
            columns(3, 1, "rms2_w")
            dve.wait_ge(sem("set3_loaded"), 16 * 6)
            for hf in range(2):
                dve.wait_ge(sem("skip1_added"), hf + 1)
                statistics(h, hf, "f2")
                normalize(4, hf, "ln+norm")
                columns(4, hf, "ln1_w", "ln1_b")
            for hf in range(2):
                imgs = slice(HI * hf, HI * hf + HI)
                await_read_out(dve, ("k2", hf, 1))
                shape = [C, HI, 6, TOK]
                tt(kbd2[:, 1, imgs], by_image(k2[:, 1, half(hf)]).unsqueeze(2).broadcast_to(shape),
                   mask_head[:, :].unsqueeze(1).unsqueeze(3).broadcast_to(shape), ALU.mult)\
                    .then_inc(sem("keys2_masked_dve"), 1)
                for q in range(2):
                    b = read(dve, ("v2", hf, q))
                    shape = [128, 24, 2, HFD]
                    at = (HI * hf + 4 * q) * 6
                    free(tt(vbd2[:, at:at + 24], b[:, 0:4 * C].rearrange("p (n d) -> p n d", d=HFD)
                            .unsqueeze(2).broadcast_to(shape),
                            mask_pair[:, :].unsqueeze(1).unsqueeze(3).broadcast_to(shape), ALU.mult), ("v2", hf, q))

            def shifted2(p):
                x = probs2[:, p % AHEAD, :, 0:TOK]
                b = read(dve, ("s2", p))
                scores = b[:, 0:HF * TOK].rearrange("p (h j) -> p h j", h=HF)
                mx = row_max[:, p, :]
                link(reduce(mx, scores, AX.X, ALU.max))
                free(tt(x, scores, mx.unsqueeze(2).broadcast_to([128, HF, TOK]), ALU.subtract), ("s2", p))

            for p in range(2):
                shifted2(p)
            for p in range(PAIRS):
                if p + 2 < PAIRS:
                    shifted2(p + 2)
                sums(p, probs2, "exp2_done", HF)
                if p:
                    scaled(p - 1, ("av2", p - 1), HF)
                if p == HP + 1:
                    attended("o2t", 0)
                if p == HP + 2:
                    dve.wait_ge(sem("skip_ready"), 3)
                    statistics(u, 0, "wo2")
            scaled(PAIRS - 1, ("av2", PAIRS - 1), HF)
            attended("o2t", 1)
            normalize(5, 0, "ln")
            dve.wait_ge(sem("skip_ready"), 4)
            statistics(u, 1, "wo2")
            columns(5, 0, "ln2_w", "ln2_b")
            normalize(5, 1, "ln")
            columns(5, 1, "ln2_w", "ln2_b")

            for hf in range(2):
                shifted_logits(rt1, "gate1", E1, hf)
                await_read_out(dve, ("gate1", hf))
            best(rt1, by_token(rt1, "s", E1), E1, 2, run[:, 0:PAIRS * E1])
            dve.wait_ge(sem("route_exp"), 4)
            e = by_token(rt1, "e", E1)
            link(stt(e, by_token(rt1, "sel", E1), -1.0, e, ALU.mult, ALU.mult))
            link(reduce(rt1["sum"][:, :], e, AX.X, ALU.add))
            link(nc.vector.reciprocal(rt1["inv"][:, :], rt1["sum"][:, :]))
            tt(by_token(rt1, "w", E1), e, spread(rt1["inv"], E1), ALU.mult).then_inc(sem("routed"), 1)

            b = read(dve, "first_row1")
            free(nc.vector.tensor_copy(wb1[0][:, half(0)], b[:, 0:HT]), "first_row1")
            await_read_out(dve, "first_row1")
            dve.sem_inc(sem("w1_loaded00"), 16)

            with dve.Fori(0, E1 // NB1) as it:
                for buf in range(NB1):
                    for n in range(2 * M1):
                        if n % M1 == 0:
                            dve.wait_ge(sem(f"w1_loaded{buf}{n // M1}"), it * 16 + 16)
                        b, base = uses["hid", n % 4]
                        dve.wait_ge(bank_free[b], it * (NB1 * turns) + (base + buf * turns + n // 4 + 1))
                        done = it * (3 * NB1 * 2 * M1) + 3 * (buf * 2 * M1 + n)
                        tt(hp[n % 4], hg[n % 4], wb1[buf][:, half(n // M1)], ALU.mult)\
                            .then_inc(sem("hid1_ready"), 1)
                        dve.wait_ge(sem("hid1_ready"), done + 1)
                        split(hs[n % 4], hp[n % 4], sem("hid1_ready"), done + 2)
            dve.wait_ge(sem("skip2_added"), 1)
            for p in range(PAIRS):
                b = read(dve, ("y1t", p))
                tt(h[:, p, :], b[:, 0:D], h[:, p, :], ALU.add).then_inc(sem("result_ready"), 1)


def laid_out(i):
    f = {k: np.asarray(v) for k, v in i.items()}
    z = np.zeros
    t = np.float32

    def chunks(w, p=C):
        return np.ascontiguousarray(w.reshape(-1, p, w.shape[1]).transpose(1, 0, 2))

    def biased(w, b):
        r = z((C + 1, 2, w.shape[1]), t)
        r[:C] = chunks(w)
        r[C, 1] = b
        return r

    def columns(v, p=C):
        return v.reshape(-1, p).T

    def chunks_ab(w):
        r = z((128, 2, w.shape[1]), t)
        r[:, 0], r[:CB, 1] = w[:128], w[128:]
        return r

    def over_zeros(w):
        return np.concatenate([w, z((w.shape[0], 256 - D), t)], 1)

    def columns_ab(v):
        return chunks_ab(v[:, None])[:, :, 0]

    def by_parity(w, heads):
        return w.reshape(*w.shape[:-1], heads // 2, 2, D // heads).swapaxes(-3, -2).reshape(*w.shape[:-1], D)

    p = f["x"].reshape(IMAGES, 3, 6, 16, 6, 16).transpose(0, 2, 4, 1, 3, 5).reshape(IMAGES, TOK, 768)
    padded = z((IMAGES, SLOT, 768), t)
    padded[:, :TOK] = p
    o = {}
    o["patches"] = padded.reshape(PAIRS, 128, PATCH_CHUNKS, 128).transpose(0, 3, 2, 1)
    o["tok_w"] = chunks(f["L0_tok_W"].T, 128)
    o["wqkv0"] = chunks_ab(f["L0_attn_w_qkv"])
    o["wproj0"] = biased(f["L0_attn_w_proj"], f["L0_attn_b_proj"])
    o["gate0w"] = chunks_ab(f["L0_ffn_gate_w"])
    o["gate0_bias"] = np.tile(f["L0_ffn_gate_b"], (128, 1))
    o["route_bias"] = np.tile(f["L0_ffn_bias"], (128, 1))
    o["bd0"] = over_zeros(f["L0_ffn_bd"])
    wu = np.concatenate([f["L0_ffn_sWu"][None], f["L0_ffn_Wu"]])
    wg = np.concatenate([f["L0_ffn_sWg"][None], f["L0_ffn_Wg"]])
    o["up0"] = np.concatenate([wu, wg], 2)
    wd = np.concatenate([f["L0_ffn_sWd"][None], f["L0_ffn_Wd"]])
    bu = np.concatenate([f["L0_ffn_sbu"][None], f["L0_ffn_bu"]])[:, :, None]
    bg = np.concatenate([f["L0_ffn_sbg"][None], f["L0_ffn_bg"]])[:, :, None]
    o["down0"] = wd
    o["bias0"] = np.concatenate([bu, bg], 2)
    o["wq1"], o["wk1"] = chunks(f["L1_attn_wq"]), chunks(f["L1_attn_wk"])
    o["wv1"] = chunks(by_parity(f["L1_attn_wv"], HB))
    o["wout1"] = biased(f["L1_attn_wo"], f["L1_attn_bo"])
    o["wposT"] = f["L1_attn_w_pos"].reshape(HB * HD, NPOS).T
    o["w1a"], o["w2a"] = chunks(f["L1_attn_w1"]), chunks(f["L1_attn_w2"], 128)
    o["b2_row"] = np.tile(f["L1_attn_b2"], (128, 1))
    qkv = f["L1_ffn_qkv_w"].T
    o["wqk2"] = chunks(qkv[:, :2 * D])
    qkv_b = f["L1_ffn_qkv_b"]
    o["wv2"] = biased(by_parity(qkv[:, 2 * D:], HF), by_parity(qkv_b[2 * D:], HF))
    o["wout2"] = biased(f["L1_ffn_proj_w"].T, f["L1_ffn_proj_b"])
    o["gate1w"] = chunks_ab(f["L1_ffn_w_gate"])
    o["b2m"] = over_zeros(f["L1_ffn_b2"])
    o["up1"] = f["L1_ffn_W1"]
    w2 = f["L1_ffn_W2"].reshape(E1, M1, 128, D).transpose(0, 2, 1, 3).reshape(E1, 128, M1 * D)
    o["down1"] = w2
    o["bias1"] = f["L1_ffn_b1"].reshape(E1, M1, 128).transpose(0, 2, 1)
    o["c96"] = np.concatenate([columns(v) for v in (
        f["L1_attn_norm1_w"], f["L1_attn_norm2_w"], f["L1_ffn_norm1_w"], f["L1_ffn_norm1_b"],
        qkv_b[:D], qkv_b[D:2 * D])], 1)
    o["c128"] = np.concatenate([columns(f["L1_attn_u_param"].reshape(-1), 128),
                                columns(f["L1_attn_v_param"].reshape(-1), 128),
                                columns(f["L1_attn_b1"], 128),
                                columns_ab(f["L1_ffn_norm2_w"]), columns_ab(f["L1_ffn_norm2_b"]),
                                columns_ab(f["L0_ffn_sbd"])], 1)
    o["fold"] = np.tile(np.eye(CB, dtype=t), (2, 1))
    o["first_row"] = np.repeat((np.arange(E1)[:, None] == 0).astype(t), 128, 1)
    o["ident"] = np.eye(128, dtype=t)
    o["mask_pair"] = (np.arange(128)[:, None] // 64 == np.arange(2)).astype(t)
    o["mask_head"] = (np.arange(C)[:, None] // HFD == np.arange(6)).astype(t)
    inside = lambda n: np.tile((np.arange(n) > 0).astype(t), PAIRS)
    o["run"] = np.tile(np.concatenate([inside(G0), inside(E0)]), (128, 1))
    d = np.arange(-(TOK - 1), TOK).astype(t)
    rate = np.exp(np.log(t((TOK + 1) / 2.0)) / t(NPOS // 2)).astype(t)
    widths = (rate ** np.arange(1, NPOS // 2 + 1, dtype=t)).astype(t)
    near = (np.abs(d)[None, :] <= widths[:, None]).astype(t)
    o["basis"] = np.concatenate([near, np.sign(d)[None, :] * near]).astype(t)
    return {k: np.ascontiguousarray(v) for k, v in o.items()}


def kernel(**inputs):
    import concourse.bacc as bacc
    from concourse.bass_utils import run_bass_kernel_spmd

    arrays = laid_out(inputs)
    nc = bacc.Bacc("TRN2", target_bir_lowering=False, num_devices=1)
    args = {k: nc.dram_tensor(f"in_{k}", v.shape, mybir.dt.from_np(v.dtype), kind="ExternalInput").ap()
            for k, v in arrays.items()}
    out = nc.dram_tensor("out", (IMAGES, TOK, D), F32, kind="ExternalOutput").ap()
    build_tower(nc, args, out)
    r = run_bass_kernel_spmd(nc, [{f"in_{k}": v for k, v in arrays.items()}], core_ids=[0])
    return r.results[0]["out"]
```
